# Optimizing a Trainium2 kernel written in Bass

```python
import numpy as np
import jax
import jax.numpy as jnp

def _softmax(x, axis=-1):
    return jax.nn.softmax(x, axis=axis)

def _gelu(x):
    return jax.nn.gelu(x, approximate=True)

def _silu(x):
    return jax.nn.silu(x)

def _sigmoid(x):
    return jax.nn.sigmoid(x)

def _layernorm(x, axis=-1, eps=1e-05):
    m = jnp.mean(x, axis=axis, keepdims=True)
    v = jnp.var(x, axis=axis, keepdims=True)
    return (x - m) / jnp.sqrt(v + eps)

def _scatter_add(tgt, idx, src, axis=0):
    return tgt.at[idx].add(src)

def _segment_sum(src, seg, n):
    return jax.ops.segment_sum(src, seg, n)
kernel_name = 'mk_vit_tower_postln_d2_tok_img1024_r4_90ddb8'

def setup_inputs(seed: int=0):
    np.random.seed(seed)
    _w = jnp.asarray

    def _rec_inputs():
        import jax
        import jax.numpy as jnp
        _rk = jax.random.key(seed)
        x = -4.65018e-05 + 0.999886 * jax.random.normal(jax.random.fold_in(_rk, 1), (64, 3, 128, 128), jnp.float32)
        return x
    x = _rec_inputs()

    def _L0_tok_setup():
        import jax, jax.numpy as jnp
        import numpy as np
        IMG_H = 128
        IMG_W = 128
        C = 3
        PH = 16
        PW = 16
        HID = 256
        NH = IMG_H // PH
        NW = IMG_W // PW
        PD = C * PH * PW
        BATCH = 64

        def sinusoidal_pos_embed(embed_dim, grid_size_x, grid_size_y):
            gh = jnp.arange(grid_size_y)
            gw = jnp.arange(grid_size_x)
            grid = jnp.stack(jnp.meshgrid(gh, gw, indexing='ij'), axis=0)
            h_pos = grid[0].reshape(-1).astype(jnp.float32)
            w_pos = grid[1].reshape(-1).astype(jnp.float32)
            quarter = embed_dim // 4
            factor = 10000.0 ** (jnp.arange(quarter, dtype=jnp.float32) / quarter)
            h = h_pos[:, None] / factor
            w = w_pos[:, None] / factor
            return jnp.concatenate([jnp.sin(h), jnp.cos(h), jnp.sin(w), jnp.cos(w)], axis=-1)
        key = jax.random.key(seed)
        k1, k2 = jax.random.split(key, 2)
        x = jax.random.normal(k1, (BATCH, C, IMG_H, IMG_W), dtype=jnp.float32)
        Wp = jax.random.normal(k2, (HID, PD), dtype=jnp.float32) * (1.0 / np.sqrt(PD))
        b = jnp.zeros((HID,), dtype=jnp.float32)
        return {'x': x, 'Wp': Wp, 'b': b}
    _L0_tok_all = _L0_tok_setup()
    _L0_tok_in = {k: v for k, v in _L0_tok_all.items() if k in ('Wp', 'b')}
    del _L0_tok_all

    def _L0_attn_setup():
        import jax, jax.numpy as jnp
        import numpy as np
        NUM_HEADS = 16
        ROPE_THETA = 1000.0

        def _rope(x, cos, sin):
            xp = x.reshape(x.shape[:-1] + (x.shape[-1] // 2, 2))
            xe, xo = (xp[..., 0], xp[..., 1])
            c = cos[None, None, :, :]
            s = sin[None, None, :, :]
            re = xe * c - xo * s
            ro = xe * s + xo * c
            return jnp.stack((re, ro), axis=-1).reshape(x.shape)
        key = jax.random.key(seed)
        ks = jax.random.split(key, 5)
        B, T, D = (2, 512, 256)
        std = 2.0 / (D + D)
        return {'x': jax.random.normal(ks[0], (B, T, D), dtype=jnp.float32), 'wq': jax.random.normal(ks[1], (D, D), dtype=jnp.float32) * std, 'wk': jax.random.normal(ks[2], (D, D), dtype=jnp.float32) * std, 'wv': jax.random.normal(ks[3], (D, D), dtype=jnp.float32) * std, 'wo': jax.random.normal(ks[4], (D, D), dtype=jnp.float32) * std}
    _L0_attn_all = _L0_attn_setup()
    _L0_attn_in = {k: v for k, v in _L0_attn_all.items() if k in ('wq', 'wk', 'wv', 'wo')}
    del _L0_attn_all

    def _L0_ffn_setup():
        import jax, jax.numpy as jnp
        import numpy as np
        QP = 127.0
        MIN_RANGE = 1e-06

        def _ste_round(x):
            return x + jax.lax.stop_gradient(jnp.round(x) - x)

        def _quant_per_tensor(x):
            scale = jnp.maximum(jnp.max(jnp.abs(x)), MIN_RANGE) / QP
            return (_ste_round(x / scale), scale)

        def _qlinear(x2d, w, b):
            xq, sx = _quant_per_tensor(x2d)
            wq, sw = _quant_per_tensor(w)
            out = jnp.matmul(xq, wq.T) + b[None, :]
            return out * (sw * sx)
        key = jax.random.key(seed)
        k = jax.random.split(key, 5)
        B, N, D, H = (8, 256, 256, 1024)
        return {'x': jax.random.normal(k[0], (B, N, D), dtype=jnp.float32), 'w1': jax.random.normal(k[1], (H, D), dtype=jnp.float32) * 0.02, 'b1': jax.random.normal(k[2], (H,), dtype=jnp.float32) * 0.02, 'w2': jax.random.normal(k[3], (D, H), dtype=jnp.float32) * 0.02, 'b2': jax.random.normal(k[4], (D,), dtype=jnp.float32) * 0.02}
    _L0_ffn_all = _L0_ffn_setup()
    _L0_ffn_in = {k: v for k, v in _L0_ffn_all.items() if k in ('w1', 'b1', 'w2', 'b2')}
    del _L0_ffn_all

    def _L1_attn_setup():
        import jax, jax.numpy as jnp
        import numpy as np
        B, T, E = (4, 512, 256)
        H, HS = (16, 64)
        key = jax.random.key(seed)
        ks = jax.random.split(key, 6)
        return {'x': jax.random.normal(ks[0], (B, T, E), dtype=jnp.float32), 'Wq': jax.random.normal(ks[1], (H, E, HS), dtype=jnp.float32) * 0.02, 'Wk': jax.random.normal(ks[2], (H, E, HS), dtype=jnp.float32) * 0.02, 'Wv': jax.random.normal(ks[3], (H, E, HS), dtype=jnp.float32) * 0.02, 'proj_w': jax.random.normal(ks[4], (E, H * HS), dtype=jnp.float32) * 0.02, 'proj_b': jax.random.normal(ks[5], (E,), dtype=jnp.float32) * 0.02}
    _L1_attn_all = _L1_attn_setup()
    _L1_attn_in = {k: v for k, v in _L1_attn_all.items() if k in ('Wq', 'Wk', 'Wv', 'proj_w', 'proj_b')}
    del _L1_attn_all

    def _L1_ffn_setup():
        import jax, jax.numpy as jnp
        import numpy as np
        TOP_K = 2
        EPS = 1e-09
        key = jax.random.key(seed)
        ks = jax.random.split(key, 6)
        B, T, D, H, E = (4, 512, 256, 512, 8)
        x = jax.random.normal(ks[0], (B, T, D), dtype=jnp.float32)
        Wg = jax.random.normal(ks[1], (E, D), dtype=jnp.float32) * 0.02
        W1 = jax.random.normal(ks[2], (E, 2 * H, D), dtype=jnp.float32) * 0.02
        b1 = jax.random.normal(ks[3], (E, 2 * H), dtype=jnp.float32) * 0.02
        Wo = jax.random.normal(ks[4], (D, H), dtype=jnp.float32) * 0.02
        bo = jax.random.normal(ks[5], (D,), dtype=jnp.float32) * 0.02
        return {'x': x, 'Wg': Wg, 'W1': W1, 'b1': b1, 'Wo': Wo, 'bo': bo}
    _L1_ffn_all = _L1_ffn_setup()
    _L1_ffn_in = {k: v for k, v in _L1_ffn_all.items() if k in ('Wg', 'W1', 'b1', 'Wo', 'bo')}
    del _L1_ffn_all
    return {'x': x, 'L0_tok_Wp': _L0_tok_in['Wp'], 'L0_tok_b': _L0_tok_in['b'], 'L0_attn_wq': _L0_attn_in['wq'], 'L0_attn_wk': _L0_attn_in['wk'], 'L0_attn_wv': _L0_attn_in['wv'], 'L0_attn_wo': _L0_attn_in['wo'], 'L0_ffn_w1': _L0_ffn_in['w1'], 'L0_ffn_b1': _L0_ffn_in['b1'], 'L0_ffn_w2': _L0_ffn_in['w2'], 'L0_ffn_b2': _L0_ffn_in['b2'], 'L1_attn_Wq': _L1_attn_in['Wq'], 'L1_attn_Wk': _L1_attn_in['Wk'], 'L1_attn_Wv': _L1_attn_in['Wv'], 'L1_attn_proj_w': _L1_attn_in['proj_w'], 'L1_attn_proj_b': _L1_attn_in['proj_b'], 'L1_ffn_Wg': _L1_ffn_in['Wg'], 'L1_ffn_W1': _L1_ffn_in['W1'], 'L1_ffn_b1': _L1_ffn_in['b1'], 'L1_ffn_Wo': _L1_ffn_in['Wo'], 'L1_ffn_bo': _L1_ffn_in['bo']}

def reference(x, L0_tok_Wp, L0_tok_b, L0_attn_wq, L0_attn_wk, L0_attn_wv, L0_attn_wo, L0_ffn_w1, L0_ffn_b1, L0_ffn_w2, L0_ffn_b2, L1_attn_Wq, L1_attn_Wk, L1_attn_Wv, L1_attn_proj_w, L1_attn_proj_b, L1_ffn_Wg, L1_ffn_W1, L1_ffn_b1, L1_ffn_Wo, L1_ffn_bo):
    import jax
    import jax.numpy as jnp

    def _L0_tok_ref(x, Wp, b):
        import jax, jax.numpy as jnp
        import numpy as np
        IMG_H = 128
        IMG_W = 128
        C = 3
        PH = 16
        PW = 16
        HID = 256
        NH = IMG_H // PH
        NW = IMG_W // PW
        PD = C * PH * PW
        BATCH = 64

        def sinusoidal_pos_embed(embed_dim, grid_size_x, grid_size_y):
            gh = jnp.arange(grid_size_y)
            gw = jnp.arange(grid_size_x)
            grid = jnp.stack(jnp.meshgrid(gh, gw, indexing='ij'), axis=0)
            h_pos = grid[0].reshape(-1).astype(jnp.float32)
            w_pos = grid[1].reshape(-1).astype(jnp.float32)
            quarter = embed_dim // 4
            factor = 10000.0 ** (jnp.arange(quarter, dtype=jnp.float32) / quarter)
            h = h_pos[:, None] / factor
            w = w_pos[:, None] / factor
            return jnp.concatenate([jnp.sin(h), jnp.cos(h), jnp.sin(w), jnp.cos(w)], axis=-1)
        B = x.shape[0]
        p = x.reshape(B, C, NH, PH, NW, PW)
        p = p.transpose(0, 2, 4, 3, 5, 1)
        p = p.reshape(B, NH * NW, PH * PW * C)
        out = jnp.einsum('bnd,hd->bnh', p, Wp) + b
        pos = sinusoidal_pos_embed(HID, NW, NH)
        return out + pos

    def _L0_attn_ref(x, wq, wk, wv, wo):
        import jax, jax.numpy as jnp
        import numpy as np
        NUM_HEADS = 16
        ROPE_THETA = 1000.0

        def _rope(x, cos, sin):
            xp = x.reshape(x.shape[:-1] + (x.shape[-1] // 2, 2))
            xe, xo = (xp[..., 0], xp[..., 1])
            c = cos[None, None, :, :]
            s = sin[None, None, :, :]
            re = xe * c - xo * s
            ro = xe * s + xo * c
            return jnp.stack((re, ro), axis=-1).reshape(x.shape)
        B, T, D = x.shape
        H = NUM_HEADS
        dk = D // H

        def proj(w):
            y = jnp.einsum('btd,ed->bte', x, w)
            return y.reshape(B, T, H, dk).transpose(0, 2, 1, 3)
        q = proj(wq)
        k = proj(wk)
        v = proj(wv)
        pos = jnp.arange(T, dtype=jnp.float32)[:, None]
        kidx = jnp.arange(dk // 2, dtype=jnp.float32)
        inv_freq = ROPE_THETA ** (-2.0 * kidx / dk)
        ang = pos * inv_freq[None, :]
        cos, sin = (jnp.cos(ang), jnp.sin(ang))
        q = _rope(q, cos, sin)
        k = _rope(k, cos, sin)
        scores = jnp.einsum('bhnd,bhmd->bhnm', q, k) / jnp.sqrt(jnp.asarray(dk, x.dtype))
        causal = jnp.tril(jnp.ones((T, T), dtype=bool))
        scores = jnp.where(causal[None, None], scores, -jnp.inf)
        attn = jax.nn.softmax(scores, axis=-1)
        head = jnp.einsum('bhnm,bhmd->bhnd', attn, v)
        concat = head.transpose(0, 2, 1, 3).reshape(B, T, D)
        return jnp.einsum('btd,ed->bte', concat, wo)

    def _L0_ffn_ref(x, w1, b1, w2, b2):
        import jax, jax.numpy as jnp
        import numpy as np
        QP = 127.0
        MIN_RANGE = 1e-06

        def _ste_round(x):
            return x + jax.lax.stop_gradient(jnp.round(x) - x)

        def _quant_per_tensor(x):
            scale = jnp.maximum(jnp.max(jnp.abs(x)), MIN_RANGE) / QP
            return (_ste_round(x / scale), scale)

        def _qlinear(x2d, w, b):
            xq, sx = _quant_per_tensor(x2d)
            wq, sw = _quant_per_tensor(w)
            out = jnp.matmul(xq, wq.T) + b[None, :]
            return out * (sw * sx)
        B, N, D = x.shape
        h = _qlinear(x.reshape(-1, D), w1, b1)
        h = jax.nn.gelu(h, approximate=False)
        o = _qlinear(h, w2, b2)
        return o.reshape(B, N, -1)

    def _L1_attn_ref(x, Wq, Wk, Wv, proj_w, proj_b):
        import jax, jax.numpy as jnp
        import numpy as np
        B, T, E = (4, 512, 256)
        H, HS = (16, 64)
        b, t, e = x.shape
        h, _, hs = Wq.shape
        q = jnp.einsum('bxy,iyk->bxik', x, Wq).reshape(h, b, t, hs)
        k = jnp.einsum('bxy,iyk->bxik', x, Wk).reshape(h, b, t, hs)
        v = jnp.einsum('bxy,iyk->bxik', x, Wv).reshape(h, b, t, hs)
        wei = jnp.einsum('hbqd,hbkd->hbqk', q, k) * hs ** (-0.5)
        causal = jnp.tril(jnp.ones((t, t), dtype=bool))
        wei = jnp.where(causal, wei, -jnp.inf)
        wei = jax.nn.softmax(wei, axis=-1)
        out = jnp.einsum('hbqk,hbkd->hbqd', wei, v)
        out = out.reshape(b, t, h * hs)
        out = out @ proj_w.T + proj_b
        return out

    def _L1_ffn_ref(x, Wg, W1, b1, Wo, bo):
        import jax, jax.numpy as jnp
        import numpy as np
        TOP_K = 2
        EPS = 1e-09
        E = Wg.shape[0]
        gate_logits = jnp.einsum('btd,ed->bte', x, Wg)
        gate_scores = jax.nn.softmax(gate_logits, axis=-1)
        topk_val, topk_idx = jax.lax.top_k(gate_scores, TOP_K)
        topk_val = topk_val / (topk_val.sum(axis=-1, keepdims=True) + EPS)
        comb = (jax.nn.one_hot(topk_idx, E, dtype=x.dtype) * topk_val[..., None]).sum(axis=-2)
        out = jnp.zeros_like(x)
        for e in range(E):
            h = jnp.einsum('btd,hd->bth', x, W1[e]) + b1[e]
            a, b = jnp.split(h, 2, axis=-1)
            g = a * jax.nn.sigmoid(b)
            eo = jnp.einsum('bth,dh->btd', g, Wo) + bo
            out = out + eo * comb[..., e:e + 1]
        return out
    h = _L0_tok_ref(x, L0_tok_Wp, L0_tok_b)
    h = _layernorm(h + _L0_attn_ref(h, L0_attn_wq, L0_attn_wk, L0_attn_wv, L0_attn_wo), axis=-1)
    h = _layernorm(h + _L0_ffn_ref(h, L0_ffn_w1, L0_ffn_b1, L0_ffn_w2, L0_ffn_b2), axis=-1)
    h = _layernorm(h + _L1_attn_ref(h, L1_attn_Wq, L1_attn_Wk, L1_attn_Wv, L1_attn_proj_w, L1_attn_proj_b), axis=-1)
    h = _layernorm(h + _L1_ffn_ref(h, L1_ffn_Wg, L1_ffn_W1, L1_ffn_b1, L1_ffn_Wo, L1_ffn_bo), axis=-1)
    return h

_drawn_inputs = setup_inputs


def setup_inputs(seed=0):
    import zlib

    import numpy as np

    out = dict(_drawn_inputs(seed))
    spreads = {'L0_tok_b': (0.0, 0.1)}
    factors = {'L0_attn_wq': 22.127,
     'L0_attn_wk': 22.484,
     'L0_attn_wv': 8.0,
     'L0_attn_wo': 8.0,
     'L0_ffn_b1': 64.0,
     'L0_ffn_b2': 64.0,
     'L1_attn_Wq': 8.0,
     'L1_attn_Wk': 8.0,
     'L1_ffn_b1': 8.0,
     'L1_ffn_bo': 2.711}
    for name, (base, spread) in spreads.items():
        noise = np.random.default_rng([zlib.crc32(name.encode()), seed]).standard_normal(out[name].shape)
        drawn = base * np.exp(spread * noise) if base else spread * noise
        out[name] = jnp.asarray(drawn.astype(out[name].dtype))
    for name, factor in factors.items():
        out[name] = (out[name] * factor).astype(out[name].dtype)
    return out
```

```python
from contextlib import ExitStack

import numpy as np
import concourse.bass as bass
from concourse import mybir

F32 = mybir.dt.float32
BF16 = mybir.dt.bfloat16
U32 = mybir.dt.uint32
ALU = mybir.AluOpType
ACT = mybir.ActivationFunctionType
AX = mybir.AxisListType

P = 128
IMAGES, TOK, DIM = 64, 64, 256
TOKENS = IMAGES * TOK
TILES = TOKENS // P
PATCH = 768
PC = PATCH // P
DC = DIM // P
HEADS0, DK0 = 16, 16
SLOT = 32
PAIRS = HEADS0 // 2
VW = DK0 + 1
HID = 1024
HC = HID // P
HEADS1, DK1 = 16, 64
EXPERTS, FF = 8, 512
ROUND = 12582912.0
MASKED = -1.0e30
CONSTANTS = 10
EPS = 1e-5


def on(t, n):
    return not isinstance(t, int) or 0 <= t < n


def wait(eng, sem, value):
    if not isinstance(value, int) or value > 0:
        eng.wait_ge(sem, value)


def wait_apart(eng, sem, value):
    wait(eng, sem, value)
    eng.nop(nofuse=True)


def in_pairs(eng, step, n):
    for t in range(4):
        step(t, t % 2, t // 2)
    with eng.Fori(2, n // 2 - 1) as pair:
        step(2 * pair, 0, pair)
        step(2 * pair + 1, 1, pair)
    for t in (n - 2, n - 1):
        step(t, t % 2, n // 2 - 1)


def split_matmul(nc, out, stat, mov, first=True, last=True):
    n = len(stat)
    for k in range(n):
        (sh, sl), (mh, ml) = stat[k], mov[k]
        nc.tensor.matmul(out, sh, mh, start=first and k == 0, stop=False)
        nc.tensor.matmul(out, sh, ml, start=False, stop=False)
        ins = nc.tensor.matmul(out, sl, mh, start=False, stop=last and k == n - 1)
    return ins


def build(nc, A, out, upto=9):
    ctx = ExitStack()
    with ctx:
        def sb(name, shape, dt=F32, c=None):
            return (c or ctx).enter_context(nc.sbuf_tensor(name, shape, dt))

        def ps(name, shape, dt=F32, c=None):
            return (c or ctx).enter_context(nc.psum_tensor(name, shape, dt))

        def sem(name):
            return ctx.enter_context(nc.semaphore(name))

        h = sb("h", [P, TILES, DIM])
        w1q = sb("w1q", [P, DC, HID], BF16)
        w2q = sb("w2q", [P, HC, DIM], BF16)
        ident = sb("ident", [P, P])
        ident_bf = sb("ident_bf", [P, P], BF16)
        b1 = sb("b1", [P, HC])
        b2 = sb("b2", [P, DIM])
        bn = sb("bn", [P, 6])
        mv = sb("mv", [P, 2])
        rstd = sb("rstd", [P, 1])
        neg_half = sb("neg_half", [P, 1])
        amax = sb("amax", [P, TILES])
        wscale = sb("wscale", [P, 2])
        S = dict(sb=sb, ps=ps, sem=sem, h=h, w1q=w1q, w2q=w2q, ident=ident, ident_bf=ident_bf,
                 b1=b1, b2=b2, bn=bn, mv=mv, rstd=rstd, neg_half=neg_half, amax=amax, wscale=wscale)
        embed_and_rotary_attention(nc, A, S)
        if upto >= 2:
            quantised_mlp(nc, A, S)
        if upto >= 3:
            cross_head_attention(nc, A, S)
        if upto >= 4:
            experts(nc, A, S, out)
        else:
            store_h(nc, S, out)


def store_h(nc, S, out):
    stored = S["sem"]("stored")
    with nc.Block() as block:
        @block.sync
        def _(sp):
            sp.dma_start(out.rearrange("(t p) d -> p t d", p=P), S["h"][:, :, :]).then_inc(stored, 16)
            sp.wait_ge(stored, 16)


def embed_and_rotary_attention(nc, A, S):
    h, ident, ident_bf = S["h"], S["ident"], S["ident_bf"]
    bn, mv, rstd, neg_half, amax = S["bn"], S["mv"], S["rstd"], S["neg_half"], S["amax"]
    sem = S["sem"]
    N = TILES
    PT = N // 4
    with ExitStack() as c:
        def sb(name, shape, dt=F32):
            return S["sb"](name, shape, dt, c)

        def ps(name, shape, dt=F32):
            return S["ps"](name, shape, dt, c)

        patches = sb("patches", [P, 2 * PT, PC * P])
        whole = {}
        parts = {}
        for name, n in (("wp", PC * DIM), ("wqkv", DC * 3 * DIM), ("wo", DC * DIM)):
            whole[name] = sb(name, [P, n])
            parts[name] = (sb(name + "_hi", [P, n], BF16), sb(name + "_lo", [P, n], BF16))
        w1f = sb("w1f", [P, DC * HID])
        w2f = sb("w2f", [P, HC * DIM])
        posb = sb("posb", [P, DIM])
        tokb = sb("tokb", [P, DIM])
        rope_c = sb("rope_c", [P, 2 * DIM])
        rope_s = sb("rope_s", [P, 2 * DIM])
        mask = sb("mask", [P, DIM], BF16)
        mask_f = sb("mask_f", [P, DIM])
        wmax = sb("wmax", [P, 2])
        wall = sb("wall", [P, 2])
        winv = sb("winv", [P, 2])
        fresh = sb("fresh", [P, DIM])
        x_hi = sb("x_hi", [P, PC * P], BF16)
        x_lo = sb("x_lo", [P, PC * P], BF16)
        hT_hi = sb("hT_hi", [P, DC * P], BF16)
        hT_lo = sb("hT_lo", [P, DC * P], BF16)
        rot_a = sb("rot_a", [P, 2 * DIM])
        rot_b = sb("rot_b", [P, 2 * DIM])
        slots = sb("slots", [P, 2 * HEADS0 * SLOT])
        qkT = sb("qkT", [P, 8, P])
        vpair = [sb(f"vpair{b}", [P, PAIRS, 2 * VW]) for b in range(2)]
        top = sb("top", [P, HEADS0])
        shifted = sb("shifted", [P, HEADS0 * TOK])
        probs = sb("probs", [P, HEADS0 * TOK])
        probsT = sb("probsT", [P, PAIRS, P])
        rsum = sb("rsum", [P, HEADS0])
        att = sb("att", [P, DIM])
        aT_hi = sb("aT_hi", [P, DC * P], BF16)
        aT_lo = sb("aT_lo", [P, DC * P], BF16)

        tr = ps("ps_tr", [P, DIM])
        ps_t = ps("ps_t", [P, 1024])
        ps_b = ps("ps_b", [P, 4, 512])
        ps_o = ps("ps_o", [P, HEADS0 * VW])
        ps_s = ps_b[:, :, 0:DIM]
        ps_qk = ps_b[:, 0:2, DIM:2 * DIM]
        ps_v = ps_b[:, 2:4, DIM:2 * DIM]
        emb = ps_b[:, 0, DIM:2 * DIM]

        consts_in, weights_in = sem("consts_in"), sem("weights_in")
        patches_in = [sem(f"patches_in{n}") for n in range(4)]
        w_hi, w_lo, setup_dve, setup_pool = sem("w_hi"), sem("w_lo"), sem("setup_dve"), sem("setup_pool")
        wmax_ready, wall_ready, wq_round = sem("wmax_ready"), sem("wall_ready"), sem("wq_round")
        x_split_hi, x_split = sem("x_split_hi"), sem("x_split")
        emb_done, h0_saved, h0_ready = sem("emb_done"), sem("h0_saved"), sem("h0_ready")
        hT_done, hT_hi_ready, hT_lo_ready = sem("hT_done"), sem("hT_hi_ready"), sem("hT_lo_ready")
        qk_done, v_done = sem("qk_done"), sem("v_done")
        rot_parts, rotated, v_ready = sem("rot_parts"), sem("rotated"), sem("v_ready")
        qkT_done, qkT_ready = sem("qkT_done"), sem("qkT_ready")
        scores_done, top_ready, shift_ready, probs_ready = (
            sem("scores_done"), sem("top_ready"), sem("shift_ready"), sem("probs_ready"))
        pT_done, pT_ready, pv_done = sem("pT_done"), sem("pT_ready"), sem("pv_done")
        rsum_ready, att_ready = sem("rsum_ready"), sem("att_ready")
        aT_done, aT_hi_ready, aT_lo_ready = sem("aT_done"), sem("aT_hi_ready"), sem("aT_lo_ready")
        wo_done, res_ready, bn_ready, var_ready = (
            sem("wo_done"), sem("res_ready"), sem("bn_ready"), sem("var_ready"))
        eps_ready, rstd_ready, ln_ready = sem("eps_ready"), sem("rstd_ready"), sem("ln_ready")
        amax_done = sem("amax_done")

        def chunks(pair, n, k0=0):
            hi, lo = pair
            return lambda a, b: [(hi[:, k * n + a:k * n + b], lo[:, k * n + a:k * n + b])
                                 for k in range(hi.shape[1] // n)]

        def both(hi, lo, n, a=0, b=P):
            return [(hi[:, k * n + a:k * n + b], lo[:, k * n + a:k * n + b])
                    for k in range(hi.shape[1] // n)]

        wp_k = chunks(parts["wp"], DIM)(0, DIM)
        wqkv = chunks(parts["wqkv"], 3 * DIM)
        wo_k = chunks(parts["wo"], DIM)(0, DIM)

        with nc.Block() as block:

            @block.sync
            def _(sp):
                for name in ("wp", "wqkv", "wo"):
                    sp.dma_start(whole[name][:, :], A[name]).then_inc(weights_in, 16)
                for part in range(4):
                    if part >= 2:
                        sp.wait_ge(x_split, (part - 1) * PT)
                    place = part % 2 * PT
                    sp.dma_start(patches[:, place:place + PT, :],
                                 A["patches"][:, part * PT:(part + 1) * PT, :]).then_inc(patches_in[part], 16)

            @block.scalar
            def _(act):
                for dst, name in ((ident, "ident"), (posb, "pos"), (tokb, "tok_b"), (rope_c, "rope_c"),
                                  (rope_s, "rope_s"), (mask_f, "mask0"), (S["b1"], "b1"), (S["b2"], "b2"),
                                  (w1f, "w1"), (w2f, "w2")):
                    act.dma_start(dst[:, :], A[name]).then_inc(consts_in, 16)
                act.wait_ge(weights_in, 48)
                for name in ("wp", "wqkv", "wo"):
                    nc.scalar.copy(parts[name][0][:, :], whole[name][:, :]).then_inc(w_hi, 1)
                act.wait_ge(consts_in, 16 * CONSTANTS)
                nc.scalar.copy(mask[:, :], mask_f[:, :])
                nc.scalar.copy(ident_bf[:, :], ident[:, :]).then_inc(w_hi, 1)

                def body(t):
                    if on(t - 1, N):
                        wait(act, shift_ready, t)
                        wait(act, pT_done, t - 1)
                        nc.scalar.activation(probs[:, :], shifted[:, :], ACT.Exp,
                                             scale=float(DK0) ** -0.5).then_inc(probs_ready, 1)
                    if on(t, N):
                        wait(act, hT_done, t + 1)
                        wait(act, v_done, t)
                        nc.scalar.copy(hT_hi[:, :], tr[:, :]).then_inc(hT_hi_ready, 1)
                    if on(t - 1, N):
                        wait(act, pT_done, t)
                        wait(act, pv_done, t - 1)
                        nc.scalar.copy(probsT[:, :, :].rearrange("p a b -> p (a b)"),
                                       ps_t[:, :]).then_inc(pT_ready, 1)
                    if on(t, N):
                        wait(act, v_done, t + 1)
                        wait(act, pv_done, t)
                        for b in range(2):
                            src = ps_v[:, b, :].rearrange("p (a two j d) -> p two j a d", two=2, j=4, d=DK0)
                            for par in range(2):
                                q = slice(64 * par, 64 * par + 64)
                                dst = vpair[b][q, :, par * VW:par * VW + DK0].rearrange(
                                    "p (j a) d -> p j a d", j=4)
                                ins = nc.scalar.copy(dst, src[q, par, :, :, :])
                        ins.then_inc(v_ready, 1)
                        wait(act, qkT_done, t + 1)
                        wait(act, scores_done, t)
                        nc.scalar.copy(qkT[:, :, :].rearrange("p a b -> p (a b)"),
                                       ps_t[:, :]).then_inc(qkT_ready, 1)
                    if on(t - 1, N):
                        wait(act, aT_done, t)
                        wait(act, wo_done, t - 1)
                        nc.scalar.copy(aT_hi[:, :], tr[:, :]).then_inc(aT_hi_ready, 1)

                body(0)
                body(1)
                with act.Fori(2, N) as t:
                    body(t)
                body(N)

            @block.gpsimd
            def _(pool):
                nc.gpsimd.memset(neg_half[:, :], -0.5)
                for b in range(2):
                    nc.gpsimd.memset(vpair[b][:, :, :], 0.0)
                nc.gpsimd.memset(slots[:, :], 0.0).then_inc(setup_pool, 1)
                pool.wait_ge(setup_pool, 1)
                for b in range(2):
                    for par in range(2):
                        col = par * VW + DK0
                        nc.gpsimd.memset(vpair[b][64 * par:64 * par + 64, :, col:col + 1],
                                         1.0).then_inc(setup_pool, 1)
                        pool.wait_ge(setup_pool, 2 + 2 * b + par)

                def split(t, part):
                    src = patches[:, t - (part - part % 2) * PT, :]
                    wait(pool, emb_done, t)
                    nc.gpsimd.tensor_copy(x_hi[:, :], src).then_inc(x_split_hi, 1)
                    wait_apart(pool, x_split_hi, t + 1)
                    nc.gpsimd.tensor_tensor(x_lo[:, :], src, x_hi[:, :],
                                            ALU.subtract).then_inc(x_split, 1)

                def save(t):
                    wait(pool, h0_ready, t + 1)
                    nc.gpsimd.tensor_copy(h[:, t, :], fresh[:, :]).then_inc(h0_saved, 1)

                def norm(t):
                    wait(pool, var_ready, t + 1)
                    wait_apart(pool, ln_ready, t)
                    nc.gpsimd.tensor_scalar(rstd[:, :], mv[:, 1:2], EPS, None, ALU.add).then_inc(eps_ready, 1)
                    wait(pool, eps_ready, t + 1)
                    nc.gpsimd.tensor_tensor(rstd[:, :], rstd[:, :], neg_half[:, :],
                                            ALU.pow).then_inc(rstd_ready, 1)

                pool.wait_ge(patches_in[0], 16)
                split(0, 0)
                pool.wait_ge(wmax_ready, 2)
                nc.gpsimd.partition_all_reduce(wall[:, :], wmax[:, :], P,
                                               bass.bass_isa.ReduceOp.max).then_inc(wall_ready, 1)
                save(0)
                split(1, 0)
                save(1)
                for part in range(4):
                    if part:
                        pool.wait_ge(patches_in[part], 16)
                    if part == 0:
                        split(2, 0)
                        save(2)
                        norm(0)
                    with pool.Fori(max(3, part * PT), (part + 1) * PT) as t:
                        split(t, part)
                        save(t)
                        norm(t - 2)
                norm(N - 2)
                norm(N - 1)

            @block.vector
            def _(dve):
                dve.wait_ge(weights_in, 48)
                for n, name in enumerate(("wp", "wqkv", "wo")):
                    dve.wait_ge(w_hi, n + 1)
                    nc.vector.tensor_tensor(parts[name][1][:, :], whole[name][:, :], parts[name][0][:, :],
                                            ALU.subtract).then_inc(w_lo, 1)
                dve.wait_ge(consts_in, 16 * CONSTANTS)
                nc.vector.tensor_tensor(posb[:, :], posb[:, :], tokb[:, :], ALU.add).then_inc(setup_dve, 1)
                for n, w in enumerate((w1f, w2f)):
                    nc.vector.tensor_reduce(wmax[:, n:n + 1], w[:, :], AX.X, ALU.max,
                                            apply_absolute_value=True).then_inc(wmax_ready, 1)
                dve.wait_ge(wall_ready, 1)
                nc.vector.tensor_scalar(S["wscale"][:, :], wall[:, :], 1e-6, 1.0 / 127.0,
                                        ALU.max, ALU.mult).then_inc(setup_dve, 1)
                dve.wait_ge(setup_dve, 2)
                nc.vector.reciprocal(winv[:, :], S["wscale"][:, :]).then_inc(setup_dve, 1)
                dve.wait_ge(setup_dve, 3)
                for n, (w, q) in enumerate(((w1f, S["w1q"]), (w2f, S["w2q"]))):
                    nc.vector.tensor_scalar(w[:, :], w[:, :], winv[:, n:n + 1], ROUND,
                                            ALU.mult, ALU.add).then_inc(wq_round, 1)
                    dve.wait_ge(wq_round, n + 1)
                    nc.vector.tensor_scalar(q[:, :, :].rearrange("p a b -> p (a b)"), w[:, :], ROUND, None,
                                            ALU.subtract).then_inc(setup_dve, 1)

                def embedded(t):
                    wait(dve, emb_done, t + 1)
                    wait(dve, h0_saved, t)
                    wait(dve, hT_done, t)
                    nc.vector.tensor_tensor(fresh[:, :], emb, posb[:, :], ALU.add).then_inc(h0_ready, 1)

                def normalise(t):
                    wait(dve, rstd_ready, t + 1)
                    nc.vector.tensor_scalar(h[:, t, :], h[:, t, :], mv[:, 0:1], rstd[:, 0:1],
                                            ALU.subtract, ALU.mult).then_inc(ln_ready, 1)
                    wait(dve, ln_ready, t + 1)
                    nc.vector.tensor_reduce(amax[:, bass.ds(t, 1)] if not isinstance(t, int) else amax[:, t:t + 1],
                                            h[:, t, :], AX.X, ALU.max,
                                            apply_absolute_value=True).then_inc(amax_done, 1)

                def body(t):
                    if on(t - 1, N):
                        s4 = ps_s.rearrange("p j (a b) -> p j a b", b=TOK)
                        t3 = top[:, :].rearrange("p (j a) -> p j a", j=4)
                        wait(dve, scores_done, t)
                        nc.vector.tensor_reduce(t3, s4, AX.X, ALU.max).then_inc(top_ready, 1)
                        wait(dve, top_ready, t)
                        wait(dve, probs_ready, t - 1)
                        nc.vector.tensor_tensor(shifted[:, :].rearrange("p (j a b) -> p j a b", j=4, b=TOK), s4,
                                                t3.unsqueeze(3).to_broadcast([P, 4, 4, TOK]),
                                                ALU.subtract).then_inc(shift_ready, 1)
                    if on(t, N):
                        wait(dve, hT_hi_ready, t + 1)
                        wait(dve, v_done, t)
                        nc.vector.tensor_tensor(hT_lo[:, :], tr[:, :], hT_hi[:, :],
                                                ALU.subtract).then_inc(hT_lo_ready, 1)
                        wait(dve, qk_done, t + 1)
                        nc.vector.tensor_tensor(rot_a[:, :].rearrange("p (s n) -> p s n", s=2), ps_qk,
                                                rope_c[:, :].rearrange("p (s n) -> p s n", s=2), ALU.mult)
                        pair = ps_qk.rearrange("p s (n two) -> p s n two", two=2)
                        sgn = rope_s[:, :].rearrange("p (s n two) -> p s n two", s=2, two=2)
                        dst = rot_b[:, :].rearrange("p (s n two) -> p s n two", s=2, two=2)
                        nc.vector.tensor_tensor(dst[:, :, :, 0], pair[:, :, :, 1], sgn[:, :, :, 0], ALU.mult)
                        nc.vector.tensor_tensor(dst[:, :, :, 1], pair[:, :, :, 0], sgn[:, :, :, 1],
                                                ALU.mult).then_inc(rot_parts, 1)
                        wait(dve, rot_parts, t + 1)
                        wait(dve, qkT_done, t)
                        s = slots[:, :].rearrange("p (n s) -> p n s", s=SLOT)
                        nc.vector.tensor_tensor(s[:, :, 0:DK0], rot_a[:, :].rearrange("p (n d) -> p n d", d=DK0),
                                                rot_b[:, :].rearrange("p (n d) -> p n d", d=DK0),
                                                ALU.add).then_inc(rotated, 1)
                    if on(t - 2, N):
                        normalise(t - 2)
                    if on(t - 1, N):
                        o3 = ps_o[:, :].rearrange("p (n d) -> p n d", d=VW)
                        wait(dve, pv_done, t)
                        nc.vector.reciprocal(rsum[:, :], o3[:, :, DK0]).then_inc(rsum_ready, 1)
                        wait(dve, rsum_ready, t)
                        wait(dve, aT_done, t - 1)
                        nc.vector.tensor_tensor(att[:, :].rearrange("p (a j d) -> p j a d", j=4, d=DK0),
                                                o3[:, :, 0:DK0].rearrange("p (j a) d -> p j a d", j=4),
                                                rsum[:, :].rearrange("p (j a) -> p j a", j=4).unsqueeze(3)
                                                .to_broadcast([P, 4, 4, DK0]),
                                                ALU.mult).then_inc(att_ready, 1)
                        wait(dve, aT_hi_ready, t)
                        wait(dve, wo_done, t - 1)
                        nc.vector.tensor_tensor(aT_lo[:, :], tr[:, :], aT_hi[:, :],
                                                ALU.subtract).then_inc(aT_lo_ready, 1)
                    if on(t + 1, N):
                        embedded(t + 1)
                    if on(t - 1, N):
                        wait(dve, wo_done, t)
                        wait(dve, h0_saved, t)
                        nc.vector.tensor_tensor(h[:, t - 1, :], tr[:, :], h[:, t - 1, :], ALU.add).then_inc(res_ready, 1)
                        wait_apart(dve, res_ready, t)
                        nc.vector.bn_stats(bn[:, :], h[:, t - 1, :]).then_inc(bn_ready, 1)
                        wait_apart(dve, bn_ready, t)
                        nc.vector.bn_aggr(mv[:, :], bn[:, :]).then_inc(var_ready, 1)

                dve.wait_ge(setup_dve, 5)
                dve.wait_ge(setup_pool, 1)
                embedded(0)
                body(0)
                body(1)
                with dve.Fori(2, N - 1) as t:
                    body(t)
                body(N - 1)
                body(N)
                normalise(N - 1)

            @block.tensor
            def _(pe):
                def embed(t):
                    wait(pe, x_split, t + 1)
                    wait(pe, h0_ready, t)
                    split_matmul(nc, emb, both(x_hi, x_lo, P), wp_k).then_inc(emb_done, 1)

                def transposes(dst, src, n):
                    for k in range(n):
                        ins = nc.tensor.transpose(dst[:, k * P:(k + 1) * P], src[:, k * P:(k + 1) * P], ident[:, :])
                    return ins

                def body(t):
                    if on(t - 1, N):
                        wait(pe, qkT_ready, t)
                        if on(t, N):
                            wait(pe, h0_ready, t + 1)
                        wait(pe, shift_ready, t - 1)
                        for j in range(4):
                            nc.tensor.matmul(ps_s[:, j, :], ident_bf[:, :], mask[:, :], start=True, stop=False,
                                             skip_group_check=True)
                        for blk in range(4):
                            for j in range(4):
                                q = slice(SLOT * j, SLOT * j + SLOT)
                                for b in range(2):
                                    tk = slice(64 * b, 64 * b + 64)
                                    ins = nc.tensor.matmul(ps_s[tk, j, blk * TOK:(blk + 1) * TOK], qkT[q, blk, tk],
                                                           qkT[q, 4 + blk, tk], start=False, stop=blk == 3,
                                                           skip_group_check=True)
                        ins.then_inc(scores_done, 1)
                    if on(t, N):
                        wait(pe, h0_ready, t + 1)
                        wait(pe, res_ready, t - 1)
                        transposes(tr, fresh, DC).then_inc(hT_done, 1)
                    if on(t - 1, N):
                        wait(pe, probs_ready, t)
                        transposes(ps_t, probs, PAIRS).then_inc(pT_done, 1)
                    if on(t, N):
                        wait(pe, hT_hi_ready, t + 1)
                        wait(pe, hT_lo_ready, t + 1)
                        wait(pe, rot_parts, t)
                        for n in range(2):
                            ins = split_matmul(nc, ps_qk[:, n, :], both(hT_hi, hT_lo, P), wqkv(n * DIM, (n + 1) * DIM))
                        ins.then_inc(qk_done, 1)
                        wait(pe, v_ready, t)
                        for b in range(2):
                            for half in range(2):
                                ins = split_matmul(nc, ps_v[64 * half:64 * half + 64, b, :],
                                                   both(hT_hi, hT_lo, P, 64 * b, 64 * b + 64),
                                                   wqkv(2 * DIM, 3 * DIM))
                        ins.then_inc(v_done, 1)
                    if on(t - 1, N):
                        wait(pe, pT_ready, t)
                        wait(pe, v_ready, t)
                        wait(pe, att_ready, t - 1)
                        for b in range(2):
                            tk = slice(64 * b, 64 * b + 64)
                            for pr in range(PAIRS):
                                ins = nc.tensor.matmul(ps_o[tk, pr * 2 * VW:(pr + 1) * 2 * VW], probsT[:, pr, tk],
                                                       vpair[b][:, pr, :], start=True, stop=True)
                        ins.then_inc(pv_done, 1)
                    if on(t, N):
                        wait(pe, rotated, t + 1)
                        wait(pe, pT_ready, t)
                        transposes(ps_t, slots, 8).then_inc(qkT_done, 1)
                    if on(t - 1, N):
                        wait(pe, att_ready, t)
                        transposes(tr, att, DC).then_inc(aT_done, 1)
                    if on(t + 1, N):
                        embed(t + 1)
                    if on(t - 1, N):
                        wait(pe, aT_hi_ready, t)
                        wait(pe, aT_lo_ready, t)
                        split_matmul(nc, tr[:, :], both(aT_hi, aT_lo, P), wo_k).then_inc(wo_done, 1)

                pe.wait_ge(consts_in, 16 * CONSTANTS)
                pe.wait_ge(w_hi, 4)
                pe.wait_ge(w_lo, 3)
                pe.wait_ge(setup_pool, 5)
                embed(0)
                body(0)
                body(1)
                with pe.Fori(2, N - 1) as t:
                    body(t)
                body(N - 1)
                body(N)


def quantised_mlp(nc, A, S):
    h, w1q, w2q, b1, b2 = S["h"], S["w1q"], S["w2q"], S["b1"], S["b2"]
    bn, mv, rstd, neg_half, amax, wscale = (S["bn"], S["mv"], S["rstd"], S["neg_half"], S["amax"], S["wscale"])
    N = TILES
    CH = 4
    CHUNKS = N // CH
    W = CH * P
    with ExitStack() as c:
        def sb(name, shape, dt=F32):
            return S["sb"](name, shape, dt, c)

        def ps(name, shape, dt=F32):
            return S["ps"](name, shape, dt, c)

        hidden = sb("hidden", [P, HC, TOKENS])
        rounding = sb("rounding", [P, CH * DIM])
        xq = sb("xq", [P, CH * DIM], BF16)
        xqT = sb("xqT", [P, DC, W], BF16)
        hq = [sb(f"hq{u}", [P, HC, P], BF16) for u in range(2)]
        hmax = sb("hmax", [P, CHUNKS * 4])
        biased = sb("biased", [P, DIM])
        b1s = sb("b1s", [P, HC])
        scale_x, scale_h = sb("scale_x", [P, 5]), sb("scale_h", [P, 5])
        ps_x = ps("ps_x", [P, DC, W], BF16)
        ps_f = ps("ps_f", [P, 4, 512])
        ps_y = ps("ps_y", [P, 2, 512])
        s = {n: S["sem"](n) for n in (
            "x_max", "x_all", "x_scale", "xq_up", "xq_ready", "xT_done", "xqT_ready", "up_done", "gelu_ready",
            "hmax_ready", "h_max", "h_all", "h_scale", "hq_up", "hq_ready", "down_done", "biased_ready",
            "mlp_res", "mlp_bn", "mlp_var", "mlp_eps", "mlp_rstd", "mlp_norm")}

        with nc.Block() as block:

            @block.gpsimd
            def _(pool):
                for col, (ready, done) in ((scale_x, ("x_max", "x_all")), (scale_h, ("h_max", "h_all"))):
                    pool.wait_ge(s[ready], 1)
                    nc.gpsimd.partition_all_reduce(col[:, 1:2], col[:, 0:1], P,
                                                   bass.bass_isa.ReduceOp.max).then_inc(s[done], 1)

                def root(t):
                    wait(pool, s["mlp_var"], t + 1)
                    wait_apart(pool, s["mlp_norm"], t)
                    nc.gpsimd.tensor_scalar(rstd[:, :], mv[:, 1:2], EPS, None, ALU.add).then_inc(s["mlp_eps"], 1)
                    wait(pool, s["mlp_eps"], t + 1)
                    nc.gpsimd.tensor_tensor(rstd[:, :], rstd[:, :], neg_half[:, :],
                                            ALU.pow).then_inc(s["mlp_rstd"], 1)

                root(0)
                with pool.Fori(1, N) as t:
                    root(t)

            @block.vector
            def _(dve):
                def scales(col, data, w, mx, all_, done):
                    nc.vector.tensor_reduce(col[:, 0:1], data, AX.X, ALU.max).then_inc(s[mx], 1)
                    dve.wait_ge(s[all_], 1)
                    nc.vector.tensor_scalar(col[:, 2:3], col[:, 1:2], 1e-6, 1.0 / 127.0,
                                            ALU.max, ALU.mult).then_inc(s[done], 1)
                    dve.wait_ge(s[done], 1)
                    nc.vector.reciprocal(col[:, 3:4], col[:, 2:3]).then_inc(s[done], 1)
                    nc.vector.tensor_tensor(col[:, 4:5], col[:, 2:3], wscale[:, w:w + 1],
                                            ALU.mult).then_inc(s[done], 1)
                    dve.wait_ge(s[done], 3)

                scales(scale_x, amax[:, :], 0, "x_max", "x_all", "x_scale")
                nc.vector.tensor_scalar(b1s[:, :], b1[:, :], scale_x[:, 4:5], None,
                                        ALU.mult).then_inc(s["x_scale"], 1)

                def quantise(n):
                    src = h[:, bass.ts(n, CH), :].rearrange("p t d -> p (t d)")
                    nc.vector.tensor_scalar(rounding[:, :], src, scale_x[:, 3:4], ROUND,
                                            ALU.mult, ALU.add).then_inc(s["xq_up"], 1)
                    wait(dve, s["xq_up"], n + 1)
                    wait(dve, s["xT_done"], n)
                    nc.vector.tensor_scalar(xq[:, :], rounding[:, :], ROUND, None,
                                            ALU.subtract).then_inc(s["xq_ready"], 1)

                def gather(n):
                    wait(dve, s["xT_done"], n + 1)
                    wait(dve, s["up_done"], HC * n)
                    nc.vector.tensor_copy(xqT[:, :, :], ps_x[:, :, :]).then_inc(s["xqT_ready"], 1)

                def largest(n):
                    for f in range(0, HC, 2):
                        wait(dve, s["gelu_ready"], HC * n + f + 2)
                        col = n * 4 + f // 2
                        nc.vector.tensor_reduce(hmax[:, bass.ds(col, 1)], hidden[:, f:f + 2, bass.ts(n, W)],
                                                AX.XY, ALU.max, apply_absolute_value=True).then_inc(s["hmax_ready"], 1)

                quantise(0)
                gather(0)
                with dve.Fori(0, CHUNKS - 1) as n:
                    quantise(n + 1)
                    gather(n + 1)
                    largest(n)
                largest(CHUNKS - 1)
                dve.wait_ge(s["hmax_ready"], 4 * CHUNKS)
                scales(scale_h, hmax[:, :], 1, "h_max", "h_all", "h_scale")

                def quantise_hidden(t):
                    v = hidden[:, :, bass.ts(t, P)]
                    nc.vector.tensor_scalar(v, v, scale_h[:, 3:4], ROUND, ALU.mult, ALU.add).then_inc(s["hq_up"], 1)

                def finish(t, u):
                    wait(dve, s["down_done"], t + 1)
                    nc.vector.tensor_tensor(biased[:, :], ps_y[:, u, 0:DIM], b2[:, :],
                                            ALU.add).then_inc(s["biased_ready"], 1)
                    wait(dve, s["biased_ready"], t + 1)
                    nc.vector.scalar_tensor_tensor(h[:, t, :], biased[:, :], scale_h[:, 4:5], h[:, t, :],
                                                   ALU.mult, ALU.add).then_inc(s["mlp_res"], 1)
                    wait_apart(dve, s["mlp_res"], t + 1)
                    nc.vector.bn_stats(bn[:, :], h[:, t, :]).then_inc(s["mlp_bn"], 1)
                    wait_apart(dve, s["mlp_bn"], t + 1)
                    nc.vector.bn_aggr(mv[:, :], bn[:, :]).then_inc(s["mlp_var"], 1)

                def normalise(t):
                    wait(dve, s["mlp_rstd"], t + 1)
                    nc.vector.tensor_scalar(h[:, t, :], h[:, t, :], mv[:, 0:1], rstd[:, 0:1],
                                            ALU.subtract, ALU.mult).then_inc(s["mlp_norm"], 1)

                quantise_hidden(0)
                quantise_hidden(1)
                with dve.Fori(0, N // 2 - 1) as pair:
                    for u in range(2):
                        t = 2 * pair + u
                        finish(t, u)
                        quantise_hidden(t + 2)
                        normalise(t)
                for t in (N - 2, N - 1):
                    finish(t, t % 2)
                    normalise(t)

            @block.scalar
            def _(act):
                act.wait_ge(s["x_scale"], 4)
                with act.Fori(0, CHUNKS) as n:
                    for f in range(HC):
                        act.wait_ge(s["up_done"], n * HC + f + 1)
                        nc.scalar.activation(hidden[:, f, bass.ts(n, W)], ps_f[:, f % 4, :], ACT.Gelu,
                                             bias=b1s[:, f:f + 1], scale=scale_x[:, 4:5]).then_inc(s["gelu_ready"], 1)

                def lower(t, u):
                    wait(act, s["hq_up"], t + 1)
                    wait(act, s["down_done"], t - 1)
                    nc.scalar.activation(hq[u][:, :, :], hidden[:, :, bass.ts(t, P)], ACT.Copy,
                                         bias=-ROUND).then_inc(s["hq_ready"], 1)

                lower(0, 0)
                lower(1, 1)
                with act.Fori(1, N // 2) as pair:
                    lower(2 * pair, 0)
                    lower(2 * pair + 1, 1)

            @block.tensor
            def _(pe):
                def up(n):
                    wait(pe, s["xq_ready"], n + 1)
                    wait(pe, s["xqT_ready"], n)
                    for j in range(CH):
                        for k in range(DC):
                            ins = nc.tensor.transpose(ps_x[:, k, j * P:(j + 1) * P],
                                                      xq[:, j * DIM + k * P:j * DIM + (k + 1) * P],
                                                      S["ident_bf"][:, :])
                    ins.then_inc(s["xT_done"], 1)
                    wait(pe, s["xqT_ready"], n + 1)
                    for f in range(HC):
                        wait(pe, s["gelu_ready"], n * HC + f - 3)
                        for k in range(DC):
                            ins = nc.tensor.matmul(ps_f[:, f % 4, :], w1q[:, k, f * P:(f + 1) * P], xqT[:, k, :],
                                                   start=k == 0, stop=k == DC - 1)
                        ins.then_inc(s["up_done"], 1)

                def down(t, u):
                    wait(pe, s["hq_ready"], t + 1)
                    wait(pe, s["biased_ready"], t - 1)
                    for f in range(HC):
                        ins = nc.tensor.matmul(ps_y[:, u, 0:DIM], hq[u][:, f, :], w2q[:, f, :],
                                               start=f == 0, stop=f == HC - 1)
                    ins.then_inc(s["down_done"], 1)

                up(0)
                with pe.Fori(1, CHUNKS) as n:
                    up(n)
                down(0, 0)
                down(1, 1)
                with pe.Fori(1, N // 2) as pair:
                    down(2 * pair, 0)
                    down(2 * pair + 1, 1)


def cross_head_attention(nc, A, S):
    h, ident, ident_bf = S["h"], S["ident"], S["ident_bf"]
    bn, mv, rstd, neg_half = S["bn"], S["mv"], S["rstd"], S["neg_half"]
    MACRO = 2 * P
    M = TOKENS // MACRO
    GROUPS = MACRO // 4
    UNITS = M * 4
    UG = 16
    R = 3 * HEADS1 * DK1 // MACRO
    QKV = 3 * HEADS1 * DK1
    OC = HEADS1 * DK1 // P
    with ExitStack() as c:
        def sb(name, shape, dt=F32):
            return S["sb"](name, shape, dt, c)

        def ps(name, shape, dt=F32):
            return S["ps"](name, shape, dt, c)

        qkv = [sb(f"qkv{par}", [P, 3, GROUPS, HEADS1, 4]) for par in range(2)]
        w_hi, w_lo = sb("wqkv1_hi", [P, DC * QKV], BF16), sb("wqkv1_lo", [P, DC * QKV], BF16)
        wp_hi, wp_lo = sb("wp1_hi", [P, OC * DIM], BF16), sb("wp1_lo", [P, OC * DIM], BF16)
        stage = qkv[1][:, :, :, :, :].rearrange("p x g i t -> p (x g i t)")
        stage_w, stage_p = stage[:, 0:DC * QKV], stage[:, DC * QKV:DC * QKV + OC * DIM]
        mask = sb("mask1", [P, 512], BF16)
        mask_f = sb("mask1_f", [P, 512])
        bp = sb("bp", [P, DIM])
        hs = sb("hs", [P, 2, DIM])
        hT_hi = [sb(f"h1T_hi{u}", [P, DC, MACRO], BF16) for u in range(2)]
        hT_lo = [sb(f"h1T_lo{u}", [P, DC, MACRO], BF16) for u in range(2)]
        top = sb("top1", [P, 8])
        sums = sb("sums1", [P, 8])
        inv = sb("inv1", [P, 8])
        shifted = sb("shifted1", [P, 512])
        probs = sb("probs1", [P, 512])
        normed = sb("normed1", [P, 512])
        probsT = sb("probsT1", [P, 512])
        vdiag = sb("vdiag", [P, 8, P])
        oT_hi, oT_lo = sb("oT_hi", [P, OC, P], BF16), sb("oT_lo", [P, OC, P], BF16)

        ps_tr = ps("ps_tr1", [P, DC, MACRO])
        ps_p = [ps(f"ps_p{u}", [P, 2, MACRO]) for u in range(2)]
        ps_s = ps("ps_s1", [P, 512])
        ps_t = ps("ps_t1", [P, 512])
        ps_v = ps("ps_v1", [P, 512])
        ps_o = ps("ps_o1", [P, 512])
        ps_y = ps("ps_y1", [P, 512])

        s = {n: S["sem"](n) for n in (
            "a1_consts", "a1_weights", "a1_w_hi", "a1_w_lo", "a1_zero", "hs_ready", "hb_ready", "a1_tr_done",
            "a1_hT_hi", "a1_hT_lo", "proj_done", "proj_act", "proj_dve", "a1_scores", "a1_top", "a1_shift",
            "a1_probs", "a1_sum", "a1_inv", "a1_normed", "a1_pT_done", "a1_pT", "a1_vT_done", "vdiag_act",
            "vdiag_dve", "a1_pv", "oT_hi_ready", "oT_lo_ready", "a1_out", "a1_res", "a1_bn", "a1_var", "a1_eps",
            "a1_rstd", "a1_norm")}

        def rows(m):
            return h[:, 2 * m:2 * m + 2, :] if isinstance(m, int) else h[:, bass.ts(m, 2), :]

        def sequence(eng, body):
            body(0, 0)
            body(1, 1)
            with eng.Fori(1, M // 2 - 1) as pair:
                body(2 * pair, 0)
                body(2 * pair + 1, 1)
            for m in range(M - 2, M + 2):
                body(m, m % 2)

        with nc.Block() as block:

            @block.sync
            def _(sp):
                sp.dma_start(mask_f[:, :], A["mask1"]).then_inc(s["a1_consts"], 16)
                sp.dma_start(bp[:, :], A["bp"]).then_inc(s["a1_consts"], 16)
                sp.dma_start(stage_w, A["wqkv1"]).then_inc(s["a1_weights"], 16)
                sp.dma_start(stage_p, A["wp1"]).then_inc(s["a1_weights"], 16)

            def slot_index(m, u):
                return 4 * (m - 1) + u

            def tile_index(m, u):
                return 2 * m - 3 + (u - 1) // 2

            @block.scalar
            def _(act):
                act.wait_ge(s["a1_consts"], 32)
                nc.scalar.copy(mask[:, :], mask_f[:, :])
                act.wait_ge(s["a1_weights"], 32)
                nc.scalar.copy(w_hi[:, :], stage_w).then_inc(s["a1_w_hi"], 1)
                nc.scalar.copy(wp_hi[:, :], stage_p).then_inc(s["a1_w_hi"], 1)

                def transposed(m, par):
                    wait(act, s["a1_tr_done"], m + 1)
                    wait(act, s["proj_done"], R * (m - 1))
                    nc.scalar.copy(hT_hi[par][:, :, :], ps_tr[:, :, :]).then_inc(s["a1_hT_hi"], 1)

                def evacuate(m, par, r):
                    wait(act, s["proj_done"], R * m + r + 1)
                    if r == 0:
                        wait(act, s["a1_vT_done"], 4 * (m - 1))
                        if isinstance(m, int) and m == 1:
                            act.wait_ge(s["a1_w_lo"], 2)
                    i = 4 * (r % 4)
                    nc.scalar.copy(qkv[par][0:64, r // 4, :, i:i + 3:2, :].rearrange("p g a t -> p a g t"),
                                   ps_p[r % 2][0:64, :, :].rearrange("p a (g t) -> p a g t", t=4)
                                   ).then_inc(s["proj_act"], 1)

                def body(m, par):
                    for u in range(4):
                        k = slot_index(m, u)
                        if on(m, M):
                            evacuate(m, par, 3 * u)
                        if on(k, UNITS):
                            wait(act, s["a1_shift"], k + 1)
                            wait(act, s["a1_normed"], k)
                            nc.scalar.activation(probs[:, :], shifted[:, :], ACT.Exp,
                                                 scale=float(DK1) ** -0.5).then_inc(s["a1_probs"], 1)
                        if on(k - 1, UNITS):
                            wait(act, s["a1_pT_done"], k)
                            wait(act, s["a1_pv"], k - 1)
                            nc.scalar.copy(probsT[:, :], ps_t[:, :]).then_inc(s["a1_pT"], 1)
                        if on(m, M):
                            evacuate(m, par, 3 * u + 1)
                        if on(k - 1, UNITS):
                            wait(act, s["a1_pv"], k)
                            if (u - 1) % 2 == 0:
                                wait(act, s["a1_out"], 2 * m - 3 + (u + 1) // 2)
                            src = ps_o[:, :].rearrange("p (ca m two t) -> p two m ca t", ca=8, two=2, t=4)
                            half = slice(64 * ((u - 1) % 2), 64 * ((u - 1) % 2) + 64)
                            dst = oT_hi[:, :, half].rearrange("p m (ca pp t) -> p pp m ca t", pp=2, t=4)
                            for pp in range(2):
                                for ip in range(2):
                                    ins = nc.scalar.copy(dst[64 * ip:64 * ip + 64, pp], src[64 * pp:64 * pp + 64, ip])
                            ins.then_inc(s["oT_hi_ready"], 1)
                        if on(k, UNITS):
                            wait(act, s["a1_vT_done"], k + 1)
                            wait(act, s["a1_pv"], k)
                            nc.scalar.copy(vdiag[0:64, :, 0:64],
                                           ps_v[0:64, :].rearrange("p (a d) -> p a d", d=64)
                                           ).then_inc(s["vdiag_act"], 1)
                        if on(m, M):
                            evacuate(m, par, 3 * u + 2)
                        if u == 1 and on(m + 1, M):
                            transposed(m + 1, 1 - par)

                transposed(0, 0)
                sequence(act, body)

            @block.gpsimd
            def _(pool):
                nc.gpsimd.memset(vdiag[:, :, :], 0.0).then_inc(s["a1_zero"], 1)

                def fetch(m):
                    wait(pool, s["a1_tr_done"], m)
                    nc.gpsimd.tensor_copy(hs[:, :, :], rows(m)).then_inc(s["hs_ready"], 1)
                    nc.gpsimd.tensor_tensor(rows(m), rows(m), bp[:, :].unsqueeze(1).to_broadcast([P, 2, DIM]),
                                            ALU.add).then_inc(s["hb_ready"], 1)

                def body(m, par):
                    for u in range(4):
                        k = slot_index(m, u)
                        if u == 1 and on(m + 1, M):
                            fetch(m + 1)
                        if on(k, UNITS):
                            wait(pool, s["a1_inv"], k + 1)
                            wait(pool, s["a1_pT_done"], k)
                            nc.gpsimd.tensor_tensor(normed[:, :].rearrange("p (a b) -> p a b", b=64),
                                                    probs[:, :].rearrange("p (a b) -> p a b", b=64),
                                                    inv[:, :].unsqueeze(2).to_broadcast([P, 8, 64]),
                                                    ALU.mult).then_inc(s["a1_normed"], 1)
                        if u % 2 and on(tile_index(m, u), TILES):
                            j = tile_index(m, u)
                            wait(pool, s["a1_var"], j + 1)
                            wait_apart(pool, s["a1_norm"], j)
                            nc.gpsimd.tensor_scalar(rstd[:, :], mv[:, 1:2], EPS, None,
                                                    ALU.add).then_inc(s["a1_eps"], 1)
                            wait(pool, s["a1_eps"], j + 1)
                            nc.gpsimd.tensor_tensor(rstd[:, :], rstd[:, :], neg_half[:, :],
                                                    ALU.pow).then_inc(s["a1_rstd"], 1)

                pool.wait_ge(s["a1_consts"], 32)
                fetch(0)
                sequence(pool, body)

            @block.vector
            def _(dve):
                for n, (lo, hi, w) in enumerate(((w_lo, w_hi, stage_w), (wp_lo, wp_hi, stage_p))):
                    dve.wait_ge(s["a1_w_hi"], n + 1)
                    nc.vector.tensor_tensor(lo[:, :], w, hi[:, :], ALU.subtract).then_inc(s["a1_w_lo"], 1)

                def transposed(m, par):
                    wait(dve, s["a1_hT_hi"], m + 1)
                    wait(dve, s["proj_done"], R * (m - 1))
                    nc.vector.tensor_tensor(hT_lo[par][:, :, :], ps_tr[:, :, :], hT_hi[par][:, :, :],
                                            ALU.subtract).then_inc(s["a1_hT_lo"], 1)

                def evacuate(m, par, r):
                    wait(dve, s["proj_done"], R * m + r + 1)
                    if r == 0:
                        wait(dve, s["a1_vT_done"], 4 * (m - 1))
                    i = 4 * (r % 4) + 1
                    nc.vector.tensor_copy(qkv[par][0:64, r // 4, :, i:i + 3:2, :].rearrange("p g a t -> p a g t"),
                                          ps_p[r % 2][64:128, :, :].rearrange("p a (g t) -> p a g t", t=4)
                                          ).then_inc(s["proj_dve"], 1)

                def body(m, par):
                    for u in range(4):
                        k = slot_index(m, u)
                        s3 = ps_s[:, :].rearrange("p (a b) -> p a b", b=64)
                        if on(k, UNITS):
                            wait(dve, s["a1_scores"], k + 1)
                            nc.vector.tensor_reduce(top[:, :], s3, AX.X, ALU.max).then_inc(s["a1_top"], 1)
                            wait(dve, s["a1_top"], k + 1)
                            wait(dve, s["a1_probs"], k)
                            nc.vector.tensor_tensor(shifted[:, :].rearrange("p (a b) -> p a b", b=64), s3,
                                                    top[:, :].unsqueeze(2).to_broadcast([P, 8, 64]),
                                                    ALU.subtract).then_inc(s["a1_shift"], 1)
                        if on(m, M):
                            evacuate(m, par, 3 * u)
                        if u % 2 and on(tile_index(m, u), TILES):
                            j = tile_index(m, u)
                            wait(dve, s["a1_out"], j + 1)
                            nc.vector.tensor_tensor(h[:, j, :], ps_y[:, 0:DIM], h[:, j, :],
                                                    ALU.add).then_inc(s["a1_res"], 1)
                            wait_apart(dve, s["a1_res"], j + 1)
                            nc.vector.bn_stats(bn[:, :], h[:, j, :]).then_inc(s["a1_bn"], 1)
                            wait_apart(dve, s["a1_bn"], j + 1)
                            nc.vector.bn_aggr(mv[:, :], bn[:, :]).then_inc(s["a1_var"], 1)
                        if on(k, UNITS):
                            wait(dve, s["a1_probs"], k + 1)
                            nc.vector.tensor_reduce(sums[:, :], probs[:, :].rearrange("p (a b) -> p a b", b=64),
                                                    AX.X, ALU.add).then_inc(s["a1_sum"], 1)
                            wait(dve, s["a1_sum"], k + 1)
                            wait(dve, s["a1_normed"], k)
                            nc.vector.reciprocal(inv[:, :], sums[:, :]).then_inc(s["a1_inv"], 1)
                        if on(m, M):
                            evacuate(m, par, 3 * u + 1)
                        if on(k - 1, UNITS):
                            wait(dve, s["oT_hi_ready"], k)
                            if (u - 1) % 2 == 0:
                                wait(dve, s["a1_out"], 2 * m - 3 + (u + 1) // 2)
                            src = ps_o[:, :].rearrange("p (ca m two t) -> p two m ca t", ca=8, two=2, t=4)
                            half = slice(64 * ((u - 1) % 2), 64 * ((u - 1) % 2) + 64)
                            hi = oT_hi[:, :, half].rearrange("p m (ca pp t) -> p pp m ca t", pp=2, t=4)
                            lo = oT_lo[:, :, half].rearrange("p m (ca pp t) -> p pp m ca t", pp=2, t=4)
                            for pp in range(2):
                                for ip in range(2):
                                    q = slice(64 * ip, 64 * ip + 64)
                                    ins = nc.vector.tensor_tensor(lo[q, pp], src[64 * pp:64 * pp + 64, ip],
                                                                  hi[q, pp], ALU.subtract)
                            ins.then_inc(s["oT_lo_ready"], 1)
                        if on(k, UNITS):
                            wait(dve, s["a1_vT_done"], k + 1)
                            wait(dve, s["a1_pv"], k)
                            nc.vector.tensor_copy(vdiag[64:128, :, 64:128],
                                                  ps_v[64:128, :].rearrange("p (a d) -> p a d", d=64)
                                                  ).then_inc(s["vdiag_dve"], 1)
                        if on(m, M):
                            evacuate(m, par, 3 * u + 2)
                        if u == 1 and on(m + 1, M):
                            transposed(m + 1, 1 - par)
                        if u % 2 and on(tile_index(m, u), TILES):
                            j = tile_index(m, u)
                            wait(dve, s["a1_rstd"], j + 1)
                            nc.vector.tensor_scalar(h[:, j, :], h[:, j, :], mv[:, 0:1], rstd[:, 0:1],
                                                    ALU.subtract, ALU.mult).then_inc(s["a1_norm"], 1)

                dve.wait_ge(s["a1_zero"], 1)
                transposed(0, 0)
                sequence(dve, body)

            @block.tensor
            def _(pe):
                def transposes(m):
                    wait(pe, s["hs_ready"], m + 1)
                    wait(pe, s["a1_hT_lo"], m)
                    for j in range(2):
                        for kk in range(DC):
                            ins = nc.tensor.transpose(ps_tr[:, kk, j * P:(j + 1) * P],
                                                      hs[:, j, kk * P:(kk + 1) * P], ident[:, :])
                    ins.then_inc(s["a1_tr_done"], 1)

                def project(m, par, r):
                    if r == 0:
                        wait(pe, s["a1_hT_hi"], m + 1)
                        wait(pe, s["a1_hT_lo"], m + 1)
                    wait(pe, s["proj_act"], R * m + r - 1)
                    wait(pe, s["proj_dve"], R * m + r - 1)
                    x = [(hT_hi[par][:, kk, :], hT_lo[par][:, kk, :]) for kk in range(DC)]
                    for a in range(2):
                        col = (2 * r + a) * P
                        w = [(w_hi[:, kk * QKV + col:kk * QKV + col + P], w_lo[:, kk * QKV + col:kk * QKV + col + P])
                             for kk in range(DC)]
                        ins = split_matmul(nc, ps_p[r % 2][:, a, :], w, x)
                    ins.then_inc(s["proj_done"], 1)

                def body(m, par):
                    prev = qkv[1 - par]
                    for u in range(4):
                        k = slot_index(m, u)
                        if on(k, UNITS):
                            if u == 0:
                                wait(pe, s["proj_act"], R * m)
                                wait(pe, s["proj_dve"], R * m)
                            wait(pe, s["a1_shift"], k)
                            nc.tensor.matmul(ps_s[:, :], ident_bf[:, :], mask[:, :], start=True, stop=False,
                                             skip_group_check=True)
                            for g in range(UG):
                                cc, ab, pp = g // 4, g // 2 % 2, g % 2
                                q, kx = (prev[0:64, x, UG * u + g, :, :].rearrange("p i t -> p (i t)") for x in (0, 1))
                                ins = nc.tensor.matmul(ps_s[64 * ab:64 * ab + 64, (2 * cc + pp) * 64:(2 * cc + pp + 1) * 64],
                                                       q, kx, start=False, stop=g >= UG - 4, skip_group_check=True)
                            ins.then_inc(s["a1_scores"], 1)
                        if on(m, M):
                            project(m, par, 3 * u)
                        if u % 2 and on(tile_index(m, u), TILES):
                            j = tile_index(m, u)
                            wait(pe, s["oT_hi_ready"], 2 * j + 2)
                            wait(pe, s["oT_lo_ready"], 2 * j + 2)
                            wait(pe, s["a1_res"], j)
                            split_matmul(nc, ps_y[:, 0:DIM],
                                         [(oT_hi[:, n, :], oT_lo[:, n, :]) for n in range(OC)],
                                         [(wp_hi[:, n * DIM:(n + 1) * DIM], wp_lo[:, n * DIM:(n + 1) * DIM])
                                          for n in range(OC)]).then_inc(s["a1_out"], 1)
                        if on(k - 1, UNITS):
                            wait(pe, s["a1_normed"], k)
                            wait(pe, s["a1_pT"], k - 1)
                            for cc in range(4):
                                ins = nc.tensor.transpose(ps_t[:, cc * P:(cc + 1) * P], normed[:, cc * P:(cc + 1) * P],
                                                          ident[:, :])
                            ins.then_inc(s["a1_pT_done"], 1)
                        if on(m, M):
                            project(m, par, 3 * u + 1)
                        if on(k - 1, UNITS):
                            wait(pe, s["a1_pT"], k)
                            wait(pe, s["vdiag_act"], k)
                            wait(pe, s["vdiag_dve"], k)
                            wait(pe, s["oT_lo_ready"], k - 1)
                            for ca in range(8):
                                ins = nc.tensor.matmul(ps_o[:, ca * 64:(ca + 1) * 64], vdiag[:, ca, :],
                                                       probsT[:, (ca // 2) * P + (ca % 2) * 64:
                                                              (ca // 2) * P + (ca % 2) * 64 + 64],
                                                       start=True, stop=True)
                            ins.then_inc(s["a1_pv"], 1)
                        if on(k, UNITS):
                            wait(pe, s["vdiag_act"], k)
                            wait_apart(pe, s["vdiag_dve"], k)
                            for ca in range(8):
                                g = UG * u + 2 * ca
                                ins = nc.tensor.transpose(ps_v[:, ca * 64:(ca + 1) * 64],
                                                          prev[0:64, 2, g:g + 2, :, :].rearrange("p g i t -> p (g i t)"),
                                                          ident[0:64, 0:64])
                            ins.then_inc(s["a1_vT_done"], 1)
                        if on(m, M):
                            project(m, par, 3 * u + 2)
                        if u == 1 and on(m + 1, M):
                            transposes(m + 1)

                pe.wait_ge(s["a1_consts"], 32)
                pe.wait_ge(s["a1_w_hi"], 2)
                pe.wait_ge(s["a1_w_lo"], 2)
                transposes(0)
                sequence(pe, body)


def experts(nc, A, S, out):
    h, ident, ident_bf = S["h"], S["ident"], S["ident_bf"]
    bn, mv, rstd, neg_half = S["bn"], S["mv"], S["rstd"], S["neg_half"]
    N = TILES
    E = EXPERTS
    SLOT_TILES = 2 * TOKENS // P + E
    FC = FF // P
    WCOLS = DC * 2 * FF
    RING = 4

    h_rows = nc.dram_tensor("h_rows", (TOKENS, DIM), F32, kind="Internal").ap()
    y_rows = nc.dram_tensor("y_rows", (SLOT_TILES * P, DIM), F32, kind="Internal").ap()
    bias_rows = nc.dram_tensor("bias_rows", (3, E * 2 * FF), BF16, kind="Internal").ap()

    with ExitStack() as c:
        def sb(name, shape, dt=F32, cc=c):
            return S["sb"](name, shape, dt, cc)

        w_hi, w_lo = sb("we_hi", [P, E, WCOLS], BF16), sb("we_lo", [P, E, WCOLS], BF16)
        wo_hi, wo_lo = sb("wo2_hi", [P, FC * DIM], BF16), sb("wo2_lo", [P, FC * DIM], BF16)
        bias3 = sb("bias3", [3, E * 2 * FF], BF16)
        ones3 = sb("ones3", [3, P], BF16)
        bo = sb("bo", [P, DIM])
        share = [sb(f"share{n}", [P, N]) for n in range(2)]
        slot = [sb(f"slot{n}", [P, N], U32) for n in range(2)]
        owner = sb("owner", [P, SLOT_TILES], mybir.dt.int32)
        source = sb("source", [P, SLOT_TILES], U32)
        s_gate = {n: S["sem"](n) for n in (
            "e_consts", "e_w_in", "e_w_hi", "e_w_lo", "e_small", "e_bias_dma", "h_out", "g_fetch", "g_trans",
            "g_hT", "g_logit", "g_exp", "g_chain", "g_pool", "g_count", "g_onehot", "g_inv")}

        with ExitStack() as cg:
            def gb(name, shape, dt=F32):
                return S["sb"](name, shape, dt, cg)

            stage = gb("stage_we", [P, RING, WCOLS])
            wo_f = gb("wo_f", [P, FC * DIM])
            wg = gb("wg", [P, DC * E])
            b1f = gb("b1f", [P, 64])
            b1r = gb("b1r", [P, 64])
            b1p = gb("b1p", [P, 3, 64], BF16)
            lower_f = gb("lower_f", [P, P])
            lower = gb("lower", [P, P], BF16)
            ones = gb("ones", [P, P], BF16)
            count = gb("count", [P, P])
            row = gb("row", [P, 1])
            rank = gb("rank", [P, E])
            tnum = gb("tnum", [P, N])
            hs = gb("hs2", [P, 2 * DIM])
            hT = gb("hT2", [P, 2 * DIM])
            big = {n: gb("g_" + n, [P, N, E]) for n in
                   ("p", "d", "pm", "cand", "oh0", "oh1", "cum_a", "cum_b", "cnt", "pos", "sel")}
            assigned = gb("assigned", [P, N, E], BF16)
            col = {n: gb("gc_" + n, [P, N]) for n in ("mx", "se", "cm", "v0", "v1", "slotf0", "slotf1", "hi", "lo")}
            exp8 = {n: gb("ge_" + n, [P, E]) for n in ("t", "end_a", "end_b", "off")}
            belongs = gb("belongs", [P, SLOT_TILES, E])
            ownf = gb("ownf", [P, SLOT_TILES])
            lo1 = gb("lo1", [P, N, P], BF16)
            hi1 = gb("hi1", [P, N, 2 * SLOT_TILES], BF16)
            ps_x = S["ps"]("ps_gx", [P, 512], F32, cg)
            ps_l = S["ps"]("ps_gl", [P, N, E], F32, cg)
            ps_pre = S["ps"]("ps_gpre", [P, N * E], F32, cg)
            ps_cnt = S["ps"]("ps_gcnt", [P, N * E], F32, cg)
            ps_inv = S["ps"]("ps_ginv", [P, 2 * SLOT_TILES], F32, cg)
            s = s_gate
            with nc.Block() as block:

                @block.sync
                def _(sp):
                    sp.dma_start(h_rows.rearrange("(t p) d -> p t d", p=P), h[:, :, :]).then_inc(s["h_out"], 16)
                    for e in range(E):
                        if e >= RING:
                            sp.wait_ge(s["e_w_lo"], e - RING + 1)
                        if e:
                            sp.wait_ge(s["e_w_in"], 16 * e)
                        sp.dma_start(stage[:, e % RING, :], A["we"][:, e, :]).then_inc(s["e_w_in"], 16)
                    sp.wait_ge(s["h_out"], 16)

                @block.scalar
                def _(act):
                    for dst, name in ((wg, "wg"), (b1f, "be"), (lower_f, "lower"), (count, "count"), (row, "row"),
                                      (rank, "rank"), (tnum, "tnum"), (bo, "bo"), (wo_f, "wo2")):
                        act.dma_start(dst[:, :], A[name]).then_inc(s["e_consts"], 16)
                    act.wait_ge(s["e_consts"], 16 * 9)
                    act.wait_ge(s["e_small"], 5)
                    act.dma_start(bias_rows.rearrange("n (p f) -> p n f", p=P), b1p[:, :, :]
                                  ).then_inc(s["e_bias_dma"], 16)
                    act.wait_ge(s["e_bias_dma"], 16)
                    act.dma_start(bias3[:, :], bias_rows).then_inc(s["e_bias_dma"], 16)
                    nc.scalar.copy(lower[:, :], lower_f[:, :])
                    nc.scalar.copy(wo_hi[:, :], wo_f[:, :]).then_inc(s["e_w_hi"], 1)
                    for e in range(2):
                        act.wait_ge(s["e_w_in"], 16 * (e + 1))
                        nc.scalar.copy(w_hi[:, e, :], stage[:, e % RING, :]).then_inc(s["e_w_hi"], 1)
                    act.wait_ge(s["g_chain"], 2)
                    nc.scalar.activation(big["p"][:, :, :], big["d"][:, :, :], ACT.Exp).then_inc(s["g_exp"], 1)
                    for e in range(2, E):
                        act.wait_ge(s["e_w_in"], 16 * (e + 1))
                        nc.scalar.copy(w_hi[:, e, :], stage[:, e % RING, :]).then_inc(s["e_w_hi"], 1)
                    act.wait_ge(s["e_bias_dma"], 32)

                @block.gpsimd
                def _(pool):
                    nc.gpsimd.memset(ones[:, :], 1.0)
                    nc.gpsimd.memset(ones3[:, :], 1.0).then_inc(s["g_pool"], 1)

                    def fetch(n):
                        wait(pool, s["g_trans"], n)
                        nc.gpsimd.tensor_copy(hs[:, :].rearrange("p (t d) -> p t d", t=2),
                                              h[:, bass.ts(n, 2), :]).then_inc(s["g_fetch"], 1)

                    fetch(0)
                    with pool.Fori(1, N // 2) as n:
                        fetch(n)
                    for e in range(E):
                        pool.wait_ge(s["e_w_hi"], e + 2)
                        nc.gpsimd.tensor_tensor(w_lo[:, e, :], stage[:, e % RING, :], w_hi[:, e, :],
                                                ALU.subtract).then_inc(s["e_w_lo"], 1)

                @block.tensor
                def _(pe):
                    pe.wait_ge(s["e_consts"], 16 * 9)
                    pe.wait_ge(s["g_pool"], 1)

                    def logits(n):
                        wait(pe, s["g_fetch"], n + 1)
                        wait(pe, s["g_hT"], n)
                        for k in range(4):
                            ins = nc.tensor.transpose(ps_x[:, k * P:(k + 1) * P], hs[:, k * P:(k + 1) * P],
                                                      ident[:, :])
                        ins.then_inc(s["g_trans"], 1)
                        wait(pe, s["g_hT"], n + 1)
                        for j in range(2):
                            for k in range(DC):
                                ins = nc.tensor.matmul(ps_l[:, bass.ds(2 * n + j, 1), :].rearrange("p a e -> p (a e)"),
                                                       hT[:, (2 * j + k) * P:(2 * j + k + 1) * P],
                                                       wg[:, k * E:(k + 1) * E], start=k == 0, stop=k == DC - 1)
                        ins.then_inc(s["g_logit"], 1)

                    logits(0)
                    with pe.Fori(1, N // 2) as n:
                        logits(n)
                    pe.wait_ge(s["e_w_hi"], 1)
                    pe.wait_ge(s["g_count"], 1)
                    a = assigned[:, :, :].rearrange("p t e -> p (t e)")
                    nc.tensor.matmul(ps_pre[:, :], lower[:, :], a, start=True, stop=True)
                    nc.tensor.matmul(ps_cnt[:, :], ones[:, :], a, start=True, stop=True).then_inc(s["g_count"], 1)
                    for ch in range(2):
                        pe.wait_ge(s["g_onehot"], ch + 1)
                        for t in range(N):
                            ins = nc.tensor.matmul(ps_inv[:, :], lo1[:, t, :], hi1[:, t, :],
                                                   start=ch == 0 and t == 0, stop=ch == 1 and t == N - 1)
                        ins.then_inc(s["g_inv"], 1)

                @block.vector
                def _(dve):
                    chain = [0]

                    def link(ins):
                        chain[0] += 1
                        ins.then_inc(s["g_chain"], 1)
                        dve.wait_ge(s["g_chain"], chain[0])

                    dve.wait_ge(s["e_consts"], 16 * 9)
                    small = 0
                    for part in range(3):
                        src = b1f if part == 0 else b1r
                        nc.vector.tensor_copy(b1p[:, part, :], src[:, :]).then_inc(s["e_small"], 1)
                        small += 1
                        dve.wait_ge(s["e_small"], small)
                        if part < 2:
                            nc.vector.tensor_tensor(b1r[:, :], src[:, :], b1p[:, part, :],
                                                    ALU.subtract).then_inc(s["e_small"], 1)
                            small += 1
                            dve.wait_ge(s["e_small"], small)
                    dve.wait_ge(s["e_w_hi"], 1)
                    nc.vector.tensor_tensor(wo_lo[:, :], wo_f[:, :], wo_hi[:, :], ALU.subtract).then_inc(s["e_small"], 1)

                    def transposed(n):
                        wait(dve, s["g_trans"], n + 1)
                        wait(dve, s["g_logit"], n)
                        nc.vector.tensor_copy(hT[:, :], ps_x[:, :]).then_inc(s["g_hT"], 1)

                    transposed(0)
                    with dve.Fori(1, N // 2) as n:
                        transposed(n)

                    def over_e(x):
                        return x[:, :].unsqueeze(2).to_broadcast([P, N, E])

                    def over_t(x):
                        return x[:, :].unsqueeze(1).to_broadcast([P, N, E])

                    def tt(o, a, b, op):
                        link(nc.vector.tensor_tensor(o, a, b, op))

                    def full(x):
                        return big[x][:, :, :]

                    dve.wait_ge(s["g_logit"], N // 2)
                    link(nc.vector.tensor_reduce(col["mx"][:, :], ps_l[:, :, :], AX.X, ALU.max))
                    tt(full("d"), ps_l[:, :, :], over_e(col["mx"]), ALU.subtract)
                    dve.wait_ge(s["g_exp"], 1)
                    link(nc.vector.tensor_reduce(col["se"][:, :], full("p"), AX.X, ALU.add))
                    link(nc.vector.reciprocal(col["se"][:, :], col["se"][:, :]))
                    tt(full("p"), full("p"), over_e(col["se"]), ALU.mult)
                    for ch in range(2):
                        pm, oh, v = full("p") if ch == 0 else full("pm"), full(f"oh{ch}"), col[f"v{ch}"]
                        link(nc.vector.tensor_reduce(v[:, :], pm, AX.X, ALU.max))
                        tt(full("cand"), pm, over_e(v), ALU.is_equal)
                        tt(full("cand"), full("cand"), over_t(rank), ALU.mult)
                        link(nc.vector.tensor_reduce(col["cm"][:, :], full("cand"), AX.X, ALU.max))
                        tt(oh, full("cand"), over_e(col["cm"]), ALU.is_equal)
                        if ch == 0:
                            link(nc.vector.scalar_tensor_tensor(full("pm"), oh, -4.0, full("p"), ALU.mult, ALU.add))
                    tt(col["se"][:, :], col["v0"][:, :], col["v1"][:, :], ALU.add)
                    link(nc.vector.tensor_scalar(col["se"][:, :], col["se"][:, :], 1e-9, None, ALU.add))
                    link(nc.vector.reciprocal(col["se"][:, :], col["se"][:, :]))
                    for ch in range(2):
                        tt(share[ch][:, :], col[f"v{ch}"][:, :], col["se"][:, :], ALU.mult)
                    nc.vector.tensor_tensor(assigned[:, :, :], full("oh0"), full("oh1"), ALU.add
                                            ).then_inc(s["g_count"], 1)
                    dve.wait_ge(s["g_count"], 2)
                    link(nc.vector.tensor_copy(full("cnt").rearrange("p t e -> p (t e)"), ps_cnt[:, :]))
                    a, b = "cnt", "cum_a"
                    step = 1
                    while step < N:
                        nc.vector.tensor_copy(big[b][:, 0:step, :], big[a][:, 0:step, :])
                        tt(big[b][:, step:N, :], big[a][:, step:N, :], big[a][:, 0:N - step, :], ALU.add)
                        a, b = b, "cum_b" if b == "cum_a" else "cum_a"
                        step *= 2
                    total = big[a][:, N - 1, :]
                    t8 = exp8["t"][:, :]
                    link(nc.vector.tensor_scalar(t8, total, 1.0 / P, 63.5 / P, ALU.mult, ALU.add))
                    link(nc.vector.tensor_scalar(t8, t8, ROUND, None, ALU.add))
                    link(nc.vector.tensor_scalar(t8, t8, ROUND, None, ALU.subtract))
                    x, y = "t", "end_a"
                    step = 1
                    while step < E:
                        nc.vector.tensor_copy(exp8[y][:, 0:step], exp8[x][:, 0:step])
                        tt(exp8[y][:, step:E], exp8[x][:, step:E], exp8[x][:, 0:E - step], ALU.add)
                        x, y = y, "end_b" if y == "end_a" else "end_a"
                        step *= 2
                    end = exp8[x]
                    tt(exp8["off"][:, :], end[:, :], t8, ALU.subtract)
                    link(nc.vector.tensor_scalar(exp8["off"][:, :], exp8["off"][:, :], float(P), None, ALU.mult))
                    tt(full("pos"), big[a][:, :, :], full("cnt"), ALU.subtract)
                    tt(full("pos"), full("pos"), over_t(exp8["off"]), ALU.add)
                    tt(full("pos").rearrange("p t e -> p (t e)"), ps_pre[:, :],
                       full("pos").rearrange("p t e -> p (t e)"), ALU.add)
                    tt(belongs[:, :, :], end[:, :].unsqueeze(1).to_broadcast([P, SLOT_TILES, E]),
                       count[:, 0:SLOT_TILES].unsqueeze(2).to_broadcast([P, SLOT_TILES, E]), ALU.is_le)
                    link(nc.vector.tensor_reduce(ownf[:, :], belongs[:, :, :], AX.X, ALU.add))
                    link(nc.vector.tensor_scalar(owner[:, :], ownf[:, :], float(E - 1), None, ALU.min))
                    for ch in range(2):
                        sf, hi, lo = col[f"slotf{ch}"][:, :], col["hi"], col["lo"]
                        tt(full("sel"), full(f"oh{ch}"), full("pos"), ALU.mult)
                        link(nc.vector.tensor_reduce(sf, full("sel"), AX.X, ALU.add))
                        link(nc.vector.tensor_copy(slot[ch][:, :], sf))
                        link(nc.vector.tensor_scalar(hi[:, :], sf, 1.0 / P, -63.5 / P, ALU.mult, ALU.add))
                        link(nc.vector.tensor_scalar(hi[:, :], hi[:, :], ROUND, None, ALU.add))
                        link(nc.vector.tensor_scalar(hi[:, :], hi[:, :], ROUND, None, ALU.subtract))
                        link(nc.vector.scalar_tensor_tensor(lo[:, :], hi[:, :], -float(P), sf, ALU.mult, ALU.add))
                        if ch:
                            dve.wait_ge(s["g_inv"], ch)
                        K = SLOT_TILES
                        nc.vector.tensor_tensor(lo1[:, :, :], count[:, :].unsqueeze(1).to_broadcast([P, N, P]),
                                                lo[:, :].unsqueeze(2).to_broadcast([P, N, P]), ALU.is_equal)
                        tt(hi1[:, :, K:2 * K], count[:, 0:K].unsqueeze(1).to_broadcast([P, N, K]),
                           hi[:, :].unsqueeze(2).to_broadcast([P, N, K]), ALU.is_equal)
                        tt(hi1[:, :, 0:K], hi1[:, :, K:2 * K], tnum[:, :].unsqueeze(2).to_broadcast([P, N, K]),
                           ALU.mult)
                        nc.vector.tensor_scalar(hi1[:, :, K:2 * K], hi1[:, :, K:2 * K], row[:, 0:1], None,
                                                ALU.mult).then_inc(s["g_onehot"], 1)
                    dve.wait_ge(s["g_inv"], 2)
                    link(nc.vector.tensor_scalar(ownf[:, :], ps_inv[:, 0:SLOT_TILES], float(P), None, ALU.mult))
                    nc.vector.tensor_tensor(source[:, :], ps_inv[:, SLOT_TILES:2 * SLOT_TILES], ownf[:, :],
                                            ALU.add).then_inc(s["e_small"], 1)

        slot_tiles(nc, S, c, dict(
            h_rows=h_rows, y_rows=y_rows, w_hi=w_hi, w_lo=w_lo, wo_hi=wo_hi, wo_lo=wo_lo, bias3=bias3, ones3=ones3,
            bo=bo, owner=owner, source=source, tiles=SLOT_TILES, wcols=WCOLS, fc=FC))
        combine(nc, S, c, out, y_rows, share, slot)


def slot_tiles(nc, S, c0, G):
    ident = S["ident"]
    n_tiles, FC = G["tiles"], G["fc"]
    with ExitStack() as c:
        def sb(name, shape, dt=F32):
            return S["sb"](name, shape, dt, c)

        index = [sb(f"index{u}", [P, 1], U32) for u in range(2)]
        x = [sb(f"x_rows{u}", [P, DIM]) for u in range(2)]
        xT_hi, xT_lo = sb("xT_hi", [P, DIM], BF16), sb("xT_lo", [P, DIM], BF16)
        sig = sb("sig", [P, FF])
        g = sb("g", [P, FF])
        gT_hi, gT_lo = sb("gT_hi", [P, FF], BF16), sb("gT_lo", [P, FF], BF16)
        y = [sb(f"y{u}", [P, DIM]) for u in range(2)]
        ps_x = S["ps"]("ps_ex", [P, DIM], F32, c)
        ps_a = S["ps"]("ps_ea", [P, FF], F32, c)
        ps_b = S["ps"]("ps_eb", [P, FF], F32, c)
        ps_g = S["ps"]("ps_eg", [P, FF], F32, c)
        ps_y = S["ps"]("ps_ey", [P, DIM], F32, c)
        s = {n: S["sem"](n) for n in (
            "m_index", "m_x_in0", "m_x_in1", "m_xT_done", "m_xT_hi", "m_xT_lo", "m_up", "m_sig", "m_g", "m_gT_done",
            "m_gT_hi", "m_gT_lo", "m_down", "m_y", "m_y_out0", "m_y_out1")}

        with nc.Block() as block:

            @block.gpsimd
            def _(pool):
                def step(i, u, pair):
                    wait(pool, s[f"m_x_in{u}"], 16 * pair)
                    nc.gpsimd.tensor_copy(index[u][:, :], G["source"][:, bass.ds(i, 1)]).then_inc(s["m_index"], 1)
                    wait(pool, s["m_index"], i + 1)
                    wait_apart(pool, s["m_xT_done"], i - 1)
                    nc.gpsimd.indirect_dma_start(x[u][:, :], None, G["h_rows"],
                                                 bass.IndirectOffsetOnAxis(ap=index[u][:, :], axis=0)
                                                 ).then_inc(s[f"m_x_in{u}"], 16)

                in_pairs(pool, step, n_tiles)

            @block.sync
            def _(sp):
                def step(i, u, pair):
                    wait(sp, s["m_y"], i + 1)
                    sp.dma_start(G["y_rows"][bass.ts(i, P), :], y[u][:, :]).then_inc(s[f"m_y_out{u}"], 16)

                in_pairs(sp, step, n_tiles)
                for u in range(2):
                    sp.wait_ge(s[f"m_y_out{u}"], 16 * (n_tiles // 2))

            @block.scalar
            def _(act):
                def high(i):
                    wait(act, s["m_xT_done"], i + 1)
                    wait(act, s["m_up"], i)
                    nc.scalar.copy(xT_hi[:, :], ps_x[:, :]).then_inc(s["m_xT_hi"], 1)

                def step(i, u, pair):
                    wait(act, s["m_up"], i + 1)
                    nc.scalar.activation(sig[:, :], ps_b[:, :], ACT.Sigmoid).then_inc(s["m_sig"], 1)
                    if on(i + 1, n_tiles):
                        high(i + 1)
                    wait(act, s["m_gT_done"], i + 1)
                    wait(act, s["m_down"], i)
                    nc.scalar.copy(gT_hi[:, :], ps_g[:, :]).then_inc(s["m_gT_hi"], 1)

                high(0)
                in_pairs(act, step, n_tiles)

            @block.vector
            def _(dve):
                def low(i):
                    wait(dve, s["m_xT_hi"], i + 1)
                    nc.vector.tensor_tensor(xT_lo[:, :], ps_x[:, :], xT_hi[:, :],
                                            ALU.subtract).then_inc(s["m_xT_lo"], 1)

                def finish(i, u, pair):
                    wait(dve, s["m_down"], i + 1)
                    wait(dve, s[f"m_y_out{u}"], 16 * pair)
                    nc.vector.tensor_tensor(y[u][:, :], ps_y[:, :], G["bo"][:, :], ALU.add).then_inc(s["m_y"], 1)

                def step(i, u, pair):
                    if on(i - 1, n_tiles):
                        finish(i - 1, 1 - u, pair - 1 if u == 0 else pair)
                    wait(dve, s["m_sig"], i + 1)
                    wait(dve, s["m_gT_done"], i)
                    nc.vector.tensor_tensor(g[:, :], ps_a[:, :], sig[:, :], ALU.mult).then_inc(s["m_g"], 1)
                    if on(i + 1, n_tiles):
                        low(i + 1)
                    wait(dve, s["m_gT_hi"], i + 1)
                    nc.vector.tensor_tensor(gT_lo[:, :], ps_g[:, :], gT_hi[:, :],
                                            ALU.subtract).then_inc(s["m_gT_lo"], 1)

                low(0)
                in_pairs(dve, step, n_tiles)
                finish(n_tiles - 1, 1, n_tiles // 2 - 1)

            @block.tensor
            def _(pe):
                def transposes(i, u, pair):
                    wait(pe, s[f"m_x_in{u}"], 16 * (pair + 1))
                    wait(pe, s["m_xT_lo"], i)
                    for k in range(DC):
                        ins = nc.tensor.transpose(ps_x[:, k * P:(k + 1) * P], x[u][:, k * P:(k + 1) * P], ident[:, :])
                    ins.then_inc(s["m_xT_done"], 1)

                def down(i):
                    wait(pe, s["m_gT_hi"], i + 1)
                    wait(pe, s["m_gT_lo"], i + 1)
                    wait(pe, s["m_y"], i)
                    split_matmul(nc, ps_y[:, :],
                                 [(gT_hi[:, k * P:(k + 1) * P], gT_lo[:, k * P:(k + 1) * P]) for k in range(FC)],
                                 [(G["wo_hi"][:, k * DIM:(k + 1) * DIM], G["wo_lo"][:, k * DIM:(k + 1) * DIM])
                                  for k in range(FC)]).then_inc(s["m_down"], 1)

                def step(i, u, pair):
                    e = pe.value_load(G["owner"][0:1, bass.ds(i, 1)], min_val=0, max_val=EXPERTS - 1)
                    wait(pe, s["m_xT_hi"], i + 1)
                    wait(pe, s["m_xT_lo"], i + 1)
                    wait(pe, s["m_g"], i)
                    xx = [(xT_hi[:, k * P:(k + 1) * P], xT_lo[:, k * P:(k + 1) * P]) for k in range(DC)]
                    for half, dst in ((1, ps_b), (0, ps_a)):
                        ww = []
                        for k in range(DC):
                            off = k * 2 * FF + half * FF
                            ww.append(tuple(w[:, bass.ds(e, 1), off:off + FF].rearrange("p a n -> p (a n)")
                                            for w in (G["w_hi"], G["w_lo"])))
                        split_matmul(nc, dst[:, :], xx, ww, last=False)
                        ins = nc.tensor.matmul(dst[:, :], G["ones3"][:, :],
                                               G["bias3"][:, bass.ds(e * (2 * FF) + half * FF, FF)],
                                               start=False, stop=True)
                    ins.then_inc(s["m_up"], 1)
                    if on(i - 1, n_tiles):
                        down(i - 1)
                    if on(i + 1, n_tiles):
                        transposes(i + 1, 1 - u, pair if u == 0 else pair + 1)
                    wait(pe, s["m_g"], i + 1)
                    wait(pe, s["m_gT_lo"], i)
                    for k in range(FC):
                        ins = nc.tensor.transpose(ps_g[:, k * P:(k + 1) * P], g[:, k * P:(k + 1) * P], ident[:, :])
                    ins.then_inc(s["m_gT_done"], 1)

                transposes(0, 0, 0)
                in_pairs(pe, step, n_tiles)
                down(n_tiles - 1)


def combine(nc, S, c0, out, y_rows, share, slot):
    h, bn, mv, rstd, neg_half = S["h"], S["bn"], S["mv"], S["rstd"], S["neg_half"]
    N = TILES
    with ExitStack() as c:
        def sb(name, shape, dt=F32):
            return S["sb"](name, shape, dt, c)

        index = [[sb(f"cindex{ch}{u}", [P, 1], U32) for u in range(2)] for ch in range(2)]
        y = [[sb(f"cy{ch}{u}", [P, DIM]) for u in range(2)] for ch in range(2)]
        mixed = [sb(f"mixed{u}", [P, DIM]) for u in range(2)]
        final = [sb(f"final{u}", [P, DIM]) for u in range(2)]
        s = {n: S["sem"](n) for n in (
            "c_index", "c_y_in0", "c_y_in1", "c_half", "c_mixed", "c_bn", "c_var", "c_eps", "c_rstd", "c_final",
            "c_out0", "c_out1")}

        with nc.Block() as block:

            @block.gpsimd
            def _(pool):
                def step(t, u, pair):
                    wait(pool, s[f"c_y_in{u}"], 32 * pair)
                    for ch in range(2):
                        ins = nc.gpsimd.tensor_copy(index[ch][u][:, :], slot[ch][:, bass.ds(t, 1)])
                    ins.then_inc(s["c_index"], 1)
                    wait(pool, s["c_index"], t + 1)
                    wait_apart(pool, s["c_mixed"], t - 1)
                    for ch in range(2):
                        nc.gpsimd.indirect_dma_start(y[ch][u][:, :], None, y_rows,
                                                     bass.IndirectOffsetOnAxis(ap=index[ch][u][:, :], axis=0)
                                                     ).then_inc(s[f"c_y_in{u}"], 16)
                    if on(t - 1, N):
                        root(t - 1)

                def root(t):
                    wait(pool, s["c_var"], t + 1)
                    wait_apart(pool, s["c_final"], t)
                    nc.gpsimd.tensor_scalar(rstd[:, :], mv[:, 1:2], EPS, None, ALU.add).then_inc(s["c_eps"], 1)
                    wait(pool, s["c_eps"], t + 1)
                    nc.gpsimd.tensor_tensor(rstd[:, :], rstd[:, :], neg_half[:, :], ALU.pow).then_inc(s["c_rstd"], 1)

                in_pairs(pool, step, N)
                root(N - 1)

            @block.vector
            def _(dve):
                def step(t, u, pair):
                    wait(dve, s[f"c_y_in{u}"], 32 * (pair + 1))
                    nc.vector.scalar_tensor_tensor(mixed[u][:, :], y[0][u][:, :], share[0][:, bass.ds(t, 1)],
                                                   h[:, t, :], ALU.mult, ALU.add).then_inc(s["c_half"], 1)
                    wait(dve, s["c_half"], t + 1)
                    nc.vector.scalar_tensor_tensor(mixed[u][:, :], y[1][u][:, :], share[1][:, bass.ds(t, 1)],
                                                   mixed[u][:, :], ALU.mult, ALU.add).then_inc(s["c_mixed"], 1)
                    wait(dve, s["c_mixed"], t + 1)
                    if on(t - 1, N):
                        finish(t - 1, 1 - u, pair - 1 if u == 0 else pair)
                    nc.vector.bn_stats(bn[:, :], mixed[u][:, :]).then_inc(s["c_bn"], 1)
                    wait_apart(dve, s["c_bn"], t + 1)
                    nc.vector.bn_aggr(mv[:, :], bn[:, :]).then_inc(s["c_var"], 1)

                def finish(t, u, pair):
                    wait(dve, s["c_rstd"], t + 1)
                    wait(dve, s[f"c_out{u}"], 16 * pair)
                    nc.vector.tensor_scalar(final[u][:, :], mixed[u][:, :], mv[:, 0:1], rstd[:, 0:1],
                                            ALU.subtract, ALU.mult).then_inc(s["c_final"], 1)

                in_pairs(dve, step, N)
                finish(N - 1, 1, N // 2 - 1)

            @block.sync
            def _(sp):
                def step(t, u, pair):
                    wait(sp, s["c_final"], t + 1)
                    sp.dma_start(out[bass.ts(t, P), :], final[u][:, :]).then_inc(s[f"c_out{u}"], 16)

                in_pairs(sp, step, N)
                for u in range(2):
                    sp.wait_ge(s[f"c_out{u}"], 16 * (N // 2))


def _rows(w, chunks):
    n = w.shape[1]
    return np.ascontiguousarray(w.reshape(chunks, P, n).transpose(1, 0, 2).reshape(P, chunks * n))


def _tables():
    grid = np.stack(np.meshgrid(np.arange(8), np.arange(8), indexing="ij"))
    q = DIM // 4
    factor = np.float32(10000.0) ** (np.arange(q, dtype=np.float32) / np.float32(q))
    a = grid[0].reshape(-1).astype(np.float32)[:, None] / factor
    b = grid[1].reshape(-1).astype(np.float32)[:, None] / factor
    pos = np.concatenate([np.sin(a), np.cos(a), np.sin(b), np.cos(b)], -1).astype(np.float32)
    inv = np.float32(1000.0) ** (np.float32(-2.0) * np.arange(DK0 // 2, dtype=np.float32) / np.float32(DK0))
    ang = (np.arange(TOK, dtype=np.float32)[:, None] * inv[None]).astype(np.float32)
    cos, sin = np.cos(ang), np.sin(ang)
    rc = np.repeat(cos, 2, axis=1)
    rs = np.stack([-sin, sin], -1).reshape(TOK, DK0)
    causal = np.where(np.tril(np.ones((TOK, TOK), bool)), 0.0, MASKED).astype(np.float32)
    order = np.array([(tk * HEADS1 + hd) for hd in range(HEADS1) for tk in range(4)])
    causal1 = causal[np.ix_(order, order)]
    return {
        "ident": np.eye(P, dtype=np.float32),
        "pos": np.tile(pos, (2, 1)),
        "rope_c": np.tile(rc, (2, 2 * HEADS0)).astype(np.float32),
        "rope_s": np.tile(rs, (2, 2 * HEADS0)).astype(np.float32),
        "lower": np.triu(np.ones((P, P)), 1).astype(np.float32),
        "count": np.tile(np.arange(P, dtype=np.float32)[None], (P, 1)),
        "row": np.arange(P, dtype=np.float32)[:, None],
        "rank": np.tile(EXPERTS - np.arange(EXPERTS, dtype=np.float32)[None], (P, 1)),
        "tnum": np.tile(np.arange(TILES, dtype=np.float32)[None], (P, 1)),
        "mask0": np.tile(causal, (2, 4)),
        "mask1": np.tile(causal1, (2, 8)),
    }


def _layout(i):
    x = i["x"].reshape(IMAGES, 3, 8, 16, 8, 16).transpose(0, 2, 4, 3, 5, 1).reshape(TOKENS, PATCH)
    a = {
        "patches": np.ascontiguousarray(
            x.reshape(TILES, P, PC, P).transpose(3, 0, 2, 1).reshape(P, TILES, PC * P)),
        "wp": _rows(i["L0_tok_Wp"].T, PC),
        "tok_b": np.tile(i["L0_tok_b"][None], (P, 1)),
        "wqkv": _rows(np.concatenate([i["L0_attn_wq"].T, i["L0_attn_wk"].T, i["L0_attn_wv"].T], 1), DC),
        "wo": _rows(i["L0_attn_wo"].T, DC),
        "w1": _rows(i["L0_ffn_w1"].T, DC),
        "b1": np.ascontiguousarray(i["L0_ffn_b1"].reshape(HC, P).T),
        "w2": _rows(i["L0_ffn_w2"].T, HC),
        "wqkv1": _rows(np.concatenate([i["L1_attn_" + n].transpose(1, 0, 2).reshape(DIM, HEADS1 * DK1)
                                       for n in ("Wq", "Wk", "Wv")], 1), DC),
        "wp1": _rows(i["L1_attn_proj_w"].T, HEADS1 * DK1 // P),
        "bp": np.tile(i["L1_attn_proj_b"][None], (P, 1)),
        "we": np.ascontiguousarray(i["L1_ffn_W1"].transpose(0, 2, 1).reshape(EXPERTS, DC, P, 2 * FF)
                                   .transpose(2, 0, 1, 3).reshape(P, EXPERTS, DC * 2 * FF)),
        "be": np.ascontiguousarray(i["L1_ffn_b1"].reshape(P, EXPERTS * 2 * FF // P)),
        "wg": _rows(i["L1_ffn_Wg"].T, DC),
        "wo2": _rows(i["L1_ffn_Wo"].T, FF // P),
        "bo": np.tile(i["L1_ffn_bo"][None], (P, 1)),
        "b2": np.tile(i["L0_ffn_b2"][None], (P, 1)),
    }
    t = _tables()
    a.update(t)
    return a


def kernel(**inputs):
    import concourse.bacc as bacc
    from concourse.bass_utils import run_bass_kernel_spmd

    nc = bacc.Bacc("TRN2", target_bir_lowering=False, num_devices=1)
    arrays = _layout({k: np.asarray(v) for k, v in inputs.items()})
    aps = {n: nc.dram_tensor(n + "_in", a.shape, mybir.dt.from_np(a.dtype), kind="ExternalInput").ap()
           for n, a in arrays.items()}
    out = nc.dram_tensor("tower_out", (TOKENS, DIM), F32, kind="ExternalOutput").ap()
    build(nc, aps, out)
    r = run_bass_kernel_spmd(nc, [{n + "_in": a for n, a in arrays.items()}], core_ids=[0])
    return r.results[0]["tower_out"].reshape(IMAGES, TOK, DIM)
```

```python
from contextlib import ExitStack

import numpy as np
import concourse.bass as bass
from concourse import mybir

F32 = mybir.dt.float32
BF16 = mybir.dt.bfloat16
U32 = mybir.dt.uint32
ALU = mybir.AluOpType
ACT = mybir.ActivationFunctionType
AX = mybir.AxisListType

P = 128
IMAGES, TOK, DIM = 64, 64, 256
TOKENS = IMAGES * TOK
TILES = TOKENS // P
PATCH = 768
PC = PATCH // P
DC = DIM // P
HEADS0, DK0 = 16, 16
SLOT = 32
PAIRS = HEADS0 // 2
VW = DK0 + 1
HID = 1024
HC = HID // P
HEADS1, DK1 = 16, 64
EXPERTS, FF = 8, 512
ROUND = 12582912.0
MASKED = -1.0e30
CONSTANTS = 6
EPS = 1e-5


def on(t, n):
    return not isinstance(t, int) or 0 <= t < n


def wait(eng, sem, value):
    if not isinstance(value, int) or value > 0:
        eng.wait_ge(sem, value)


def wait_apart(eng, sem, value):
    wait(eng, sem, value)
    eng.nop(nofuse=True)


def in_pairs(eng, step, n):
    for t in range(4):
        step(t, t % 2, t // 2)
    with eng.Fori(2, n // 2 - 1) as pair:
        step(2 * pair, 0, pair)
        step(2 * pair + 1, 1, pair)
    for t in (n - 2, n - 1):
        step(t, t % 2, n // 2 - 1)


def split_matmul(nc, out, stat, mov, first=True, last=True):
    n = len(stat)
    for k in range(n):
        (sh, sl), (mh, ml) = stat[k], mov[k]
        nc.tensor.matmul(out, sh, mh, start=first and k == 0, stop=False)
        nc.tensor.matmul(out, sh, ml, start=False, stop=False)
        ins = nc.tensor.matmul(out, sl, mh, start=False, stop=last and k == n - 1)
    return ins


def build(nc, A, out, upto=9):
    ctx = ExitStack()
    with ctx:
        def sb(name, shape, dt=F32, c=None):
            return (c or ctx).enter_context(nc.sbuf_tensor(name, shape, dt))

        def ps(name, shape, dt=F32, c=None):
            return (c or ctx).enter_context(nc.psum_tensor(name, shape, dt))

        def sem(name):
            return ctx.enter_context(nc.semaphore(name))

        h = sb("h", [P, TILES, DIM])
        w1q = sb("w1q", [P, DC, HID], BF16)
        w2q = sb("w2q", [P, HC, DIM], BF16)
        ident = sb("ident", [P, P])
        ident_bf = sb("ident_bf", [P, P], BF16)
        b1 = sb("b1", [P, HC])
        b2 = sb("b2", [P, DIM])
        bn = sb("bn", [P, 6])
        mv = sb("mv", [P, 2])
        rstd = sb("rstd", [P, 1])
        neg_half = sb("neg_half", [P, 1])
        amax = sb("amax", [P, TILES])
        wscale = sb("wscale", [P, 2])
        S = dict(sb=sb, ps=ps, sem=sem, h=h, w1q=w1q, w2q=w2q, ident=ident, ident_bf=ident_bf,
                 b1=b1, b2=b2, bn=bn, mv=mv, rstd=rstd, neg_half=neg_half, amax=amax, wscale=wscale)
        embed_and_rotary_attention(nc, A, S)
        if upto >= 2:
            quantised_mlp(nc, A, S)
        if upto >= 3:
            cross_head_attention(nc, A, S)
        if upto >= 4:
            experts(nc, A, S, out)
        else:
            store_h(nc, S, out)


def store_h(nc, S, out):
    stored = S["sem"]("stored")
    with nc.Block() as block:
        @block.sync
        def _(sp):
            sp.dma_start(out.rearrange("(t p) d -> p t d", p=P), S["h"][:, :, :]).then_inc(stored, 16)
            sp.wait_ge(stored, 16)


def embed_and_rotary_attention(nc, A, S):
    h, ident, ident_bf = S["h"], S["ident"], S["ident_bf"]
    bn, mv, rstd, neg_half, amax = S["bn"], S["mv"], S["rstd"], S["neg_half"], S["amax"]
    sem = S["sem"]
    N = TILES
    PT = N // 4
    with ExitStack() as c:
        def sb(name, shape, dt=F32):
            return S["sb"](name, shape, dt, c)

        def ps(name, shape, dt=F32):
            return S["ps"](name, shape, dt, c)

        patches = sb("patches", [P, 2 * PT, PC * P])
        whole = {}
        parts = {}
        for name, n in (("wp", PC * DIM), ("wqkv", DC * 3 * DIM), ("wo", DC * DIM)):
            whole[name] = sb(name, [P, n])
            parts[name] = (sb(name + "_hi", [P, n], BF16), sb(name + "_lo", [P, n], BF16))
        w1f = sb("w1f", [P, DC * HID])
        w2f = sb("w2f", [P, HC * DIM])
        posb = sb("posb", [P, DIM])
        tokb = sb("tokb", [P, DIM])
        rope_c = sb("rope_c", [P, 2 * DIM])
        rope_s = sb("rope_s", [P, 2 * DIM])
        mask = sb("mask", [P, DIM], BF16)
        mask_f = sb("mask_f", [P, DIM])
        wmax = sb("wmax", [P, 2])
        wall = sb("wall", [P, 2])
        winv = sb("winv", [P, 2])
        fresh = sb("fresh", [P, DIM])
        x_hi = sb("x_hi", [P, PC * P], BF16)
        x_lo = sb("x_lo", [P, PC * P], BF16)
        hT_hi = sb("hT_hi", [P, DC * P], BF16)
        hT_lo = sb("hT_lo", [P, DC * P], BF16)
        rot_a = sb("rot_a", [P, 2 * DIM])
        rot_b = sb("rot_b", [P, 2 * DIM])
        slots = sb("slots", [P, 2 * HEADS0 * SLOT])
        qkT = sb("qkT", [P, 8, P])
        vpair = [[sb(f"vpair{par}{b}", [P, PAIRS, 2 * VW]) for b in range(2)] for par in range(2)]
        top = sb("top", [P, HEADS0])
        shifted = sb("shifted", [P, HEADS0 * TOK])
        probs = sb("probs", [P, HEADS0 * TOK])
        probsT = sb("probsT", [P, PAIRS, P])
        rsum = sb("rsum", [P, HEADS0])
        att = sb("att", [P, DIM])
        aT_hi = sb("aT_hi", [P, DC * P], BF16)
        aT_lo = sb("aT_lo", [P, DC * P], BF16)

        ps_tr = ps("ps_tr", [P, 2 * DIM])
        tr, emb = ps_tr[:, 0:DIM], ps_tr[:, DIM:2 * DIM]
        ps_t = ps("ps_t", [P, 1024])
        out0 = ps_t[:, 512:512 + DIM]
        ps_sc = ps("ps_sc", [P, 1024])
        ps_s = ps_sc[:, :].rearrange("p (bank half n) -> p bank half n", bank=2, half=2)
        ps_p = ps("ps_p", [P, 4, DIM])
        ps_qk, ps_v = ps_p[:, 0:2, :], ps_p[:, 2:4, 0:P]
        ps_qkT = ps_p[:, :, :].rearrange("p a b -> p (a b)")
        ps_o = ps("ps_o", [P, HEADS0 * VW])

        consts_in, weights_in = sem("consts_in"), sem("weights_in")
        first_in, mlp_in = sem("first_in"), sem("mlp_in")
        patches_in = [sem(f"patches_in{n}") for n in range(4)]
        w_hi, w_lo, setup_dve, setup_pool = sem("w_hi"), sem("w_lo"), sem("setup_dve"), sem("setup_pool")
        wmax_ready, wall_ready, wq_round = sem("wmax_ready"), sem("wall_ready"), sem("wq_round")
        x_split_hi, x_split = sem("x_split_hi"), sem("x_split")
        emb_done, h0_saved, h0_ready = sem("emb_done"), sem("h0_saved"), sem("h0_ready")
        hT_done, hT_hi_ready, hT_lo_ready = sem("hT_done"), sem("hT_hi_ready"), sem("hT_lo_ready")
        qk_done, v_done = sem("qk_done"), sem("v_done")
        rot_parts, rotated, v_ready = sem("rot_parts"), sem("rotated"), sem("v_ready")
        qkT_done, qkT_ready = sem("qkT_done"), sem("qkT_ready")
        half_scores = sem("half_scores")
        scores_done, top_ready, shift_ready, probs_ready = (
            sem("scores_done"), sem("top_ready"), sem("shift_ready"), sem("probs_ready"))
        pT_done, pT_a_ready, pT_b_ready, pv_done = (
            sem("pT_done"), sem("pT_a_ready"), sem("pT_b_ready"), sem("pv_done"))
        rsum_ready, att_ready = sem("rsum_ready"), sem("att_ready")
        aT_done, aT_hi_ready, aT_lo_ready = sem("aT_done"), sem("aT_hi_ready"), sem("aT_lo_ready")
        wo_done, res_ready, bn_ready, var_ready = (
            sem("wo_done"), sem("res_ready"), sem("bn_ready"), sem("var_ready"))
        rstd_ready, ln_ready = sem("rstd_ready"), sem("ln_ready")

        def chunks(pair, n, k0=0):
            hi, lo = pair
            return lambda a, b: [(hi[:, k * n + a:k * n + b], lo[:, k * n + a:k * n + b])
                                 for k in range(hi.shape[1] // n)]

        def both(hi, lo, n, a=0, b=P):
            return [(hi[:, k * n + a:k * n + b], lo[:, k * n + a:k * n + b])
                    for k in range(hi.shape[1] // n)]

        wp_k = chunks(parts["wp"], DIM)(0, DIM)
        wqkv = chunks(parts["wqkv"], 3 * DIM)
        wo_k = chunks(parts["wo"], DIM)(0, DIM)

        with nc.Block() as block:

            @block.sync
            def _(sp):
                sp.dma_start(whole["wp"][:, :], A["wp"]).then_inc(weights_in, 16)
                sp.dma_start(patches[:, 0:1, :], A["patches"][:, 0:1, :]).then_inc(first_in, 16)
                for name in ("wqkv", "wo"):
                    sp.dma_start(whole[name][:, :], A[name]).then_inc(weights_in, 16)
                for part in range(4):
                    if part >= 2:
                        sp.wait_ge(x_split, (part - 1) * PT)
                    place = part % 2 * PT
                    skip = 1 if part == 0 else 0
                    sp.dma_start(patches[:, place + skip:place + PT, :],
                                 A["patches"][:, part * PT + skip:(part + 1) * PT, :]
                                 ).then_inc(patches_in[part], 16)
                    if part == 0:
                        for dst, name in ((w1f, "w1"), (w2f, "w2"), (S["b1"], "b1"), (S["b2"], "b2")):
                            sp.dma_start(dst[:, :], A[name]).then_inc(mlp_in, 16)

            @block.scalar
            def _(act):
                for dst, name in ((ident, "ident"), (posb, "pos"), (tokb, "tok_b"), (rope_c, "rope_c"),
                                  (rope_s, "rope_s"), (mask_f, "mask0")):
                    act.dma_start(dst[:, :], A[name]).then_inc(consts_in, 16)
                act.wait_ge(weights_in, 48)
                for name in ("wp", "wqkv", "wo"):
                    nc.scalar.copy(parts[name][0][:, :], whole[name][:, :]).then_inc(w_hi, 1)
                act.wait_ge(consts_in, 16 * CONSTANTS)
                nc.scalar.copy(mask[:, :], mask_f[:, :])
                nc.scalar.copy(ident_bf[:, :], ident[:, :]).then_inc(w_hi, 1)

                def body(t, par, _):
                    if on(t - 2, N):
                        wait(act, aT_done, t - 1)
                        wait(act, wo_done, t - 2)
                        nc.scalar.copy(aT_hi[:, :], ps_t[:, 0:DIM]).then_inc(aT_hi_ready, 1)
                    if on(t, N):
                        wait(act, hT_done, t + 1)
                        wait(act, v_done, t)
                        nc.scalar.copy(hT_hi[:, :], tr[:, :]).then_inc(hT_hi_ready, 1)
                    if on(t - 1, N):
                        wait(act, shift_ready, t)
                        wait(act, pT_done, t - 1)
                        nc.scalar.activation(probs[:, :], shifted[:, :], ACT.Exp,
                                             scale=float(DK0) ** -0.5).then_inc(probs_ready, 1)
                    if on(t, N):
                        wait(act, v_done, t + 1)
                        if on(t - 2, N):
                            wait(act, pv_done, t - 1)
                        for b in range(2):
                            for half in range(2):
                                q = slice(64 * half, 64 * half + 64)
                                ins = nc.scalar.copy(vpair[par][b][q, :, half * VW:half * VW + DK0],
                                                     ps_v[q, b, :].rearrange("p (pr d) -> p pr d", d=DK0))
                        ins.then_inc(v_ready, 1)
                    if on(t - 1, N):
                        wait(act, pT_done, t)
                        wait(act, pv_done, t - 1)
                        nc.scalar.copy(probsT[:, 0:4, :].rearrange("p a b -> p (a b)"),
                                       ps_t[:, 0:512]).then_inc(pT_a_ready, 1)
                    if on(t, N):
                        wait(act, qkT_done, t + 1)
                        wait(act, scores_done, t)
                        nc.scalar.copy(qkT[:, :, :].rearrange("p a b -> p (a b)"),
                                       ps_qkT).then_inc(qkT_ready, 1)

                in_pairs(act, body, N)
                body(N, 0, 0)
                body(N + 1, 1, 0)

            @block.gpsimd
            def _(pool):
                nc.gpsimd.memset(neg_half[:, :], -0.5)
                for tile in range(2):
                    for b in range(2):
                        nc.gpsimd.memset(vpair[tile][b][:, :, :], 0.0)
                nc.gpsimd.memset(slots[:, :], 0.0).then_inc(setup_pool, 1)
                pool.wait_ge(setup_pool, 1)
                n = 1
                for tile in range(2):
                    for b in range(2):
                        for half in range(2):
                            col = half * VW + DK0
                            nc.gpsimd.memset(vpair[tile][b][64 * half:64 * half + 64, :, col:col + 1],
                                             1.0).then_inc(setup_pool, 1)
                            n += 1
                            pool.wait_ge(setup_pool, n)

                def split(t, part):
                    src = patches[:, t - (part - part % 2) * PT, :]
                    wait(pool, emb_done, t)
                    nc.gpsimd.tensor_copy(x_hi[:, :], src).then_inc(x_split_hi, 1)
                    wait_apart(pool, x_split_hi, t + 1)
                    nc.gpsimd.tensor_tensor(x_lo[:, :], src, x_hi[:, :],
                                            ALU.subtract).then_inc(x_split, 1)

                def save(t):
                    wait(pool, h0_ready, t + 1)
                    nc.gpsimd.tensor_copy(h[:, t, :], fresh[:, :]).then_inc(h0_saved, 1)

                def norm(t):
                    wait(pool, var_ready, t + 1)
                    wait_apart(pool, ln_ready, t)
                    nc.gpsimd.tensor_scalar(rstd[:, :], mv[:, 1:2], EPS, None, ALU.add).then_inc(rstd_ready, 1)
                    wait(pool, rstd_ready, 2 * t + 1)
                    nc.gpsimd.tensor_tensor(rstd[:, :], rstd[:, :], neg_half[:, :],
                                            ALU.pow).then_inc(rstd_ready, 1)

                pool.wait_ge(first_in, 16)
                split(0, 0)
                save(0)
                for part in range(4):
                    pool.wait_ge(patches_in[part], 16)
                    if part == 0:
                        for t in (1, 2, 3):
                            split(t, 0)
                            save(t)
                            if t == 3:
                                pool.wait_ge(wmax_ready, 2)
                                nc.gpsimd.partition_all_reduce(wall[:, :], wmax[:, :], P,
                                                               bass.bass_isa.ReduceOp.max
                                                               ).then_inc(wall_ready, 1)
                                norm(0)
                    with pool.Fori(max(4, part * PT), (part + 1) * PT) as t:
                        split(t, part)
                        save(t)
                        norm(t - 3)
                for t in (N - 3, N - 2, N - 1):
                    norm(t)

            @block.vector
            def _(dve):
                dve.wait_ge(weights_in, 48)
                for n, name in enumerate(("wp", "wqkv", "wo")):
                    dve.wait_ge(w_hi, n + 1)
                    nc.vector.tensor_tensor(parts[name][1][:, :], whole[name][:, :], parts[name][0][:, :],
                                            ALU.subtract).then_inc(w_lo, 1)
                dve.wait_ge(consts_in, 16 * CONSTANTS)
                nc.vector.tensor_tensor(posb[:, :], posb[:, :], tokb[:, :], ALU.add).then_inc(setup_dve, 1)

                def largest(n):
                    nc.vector.tensor_reduce(wmax[:, n:n + 1], (w1f, w2f)[n][:, :], AX.X, ALU.max,
                                            apply_absolute_value=True).then_inc(wmax_ready, 1)

                def scales():
                    dve.wait_ge(wall_ready, 1)
                    nc.vector.tensor_scalar(S["wscale"][:, :], wall[:, :], 1e-6, 1.0 / 127.0,
                                            ALU.max, ALU.mult).then_inc(setup_dve, 1)
                    dve.wait_ge(setup_dve, 2)
                    nc.vector.reciprocal(winv[:, :], S["wscale"][:, :]).then_inc(setup_dve, 1)
                    dve.wait_ge(setup_dve, 3)

                def quantise(n):
                    w, q = ((w1f, S["w1q"]), (w2f, S["w2q"]))[n]
                    nc.vector.tensor_scalar(w[:, :], w[:, :], winv[:, n:n + 1], ROUND,
                                            ALU.mult, ALU.add).then_inc(wq_round, 1)
                    dve.wait_ge(wq_round, n + 1)
                    nc.vector.tensor_scalar(q[:, :, :].rearrange("p a b -> p (a b)"), w[:, :], ROUND, None,
                                            ALU.subtract).then_inc(setup_dve, 1)

                def embedded(t):
                    wait(dve, emb_done, t + 1)
                    wait(dve, h0_saved, t)
                    wait(dve, hT_done, t)
                    nc.vector.tensor_tensor(fresh[:, :], emb, posb[:, :], ALU.add).then_inc(h0_ready, 1)

                def normalise(t):
                    wait(dve, rstd_ready, 2 * t + 2)
                    nc.vector.tensor_scalar(h[:, t, :], h[:, t, :], mv[:, 0:1], rstd[:, 0:1],
                                            ALU.subtract, ALU.mult).then_inc(ln_ready, 1)
                    wait(dve, ln_ready, t + 1)
                    nc.vector.tensor_reduce(amax[:, bass.ds(t, 1)] if not isinstance(t, int) else amax[:, t:t + 1],
                                            h[:, t, :], AX.X, ALU.max,
                                            apply_absolute_value=True)

                def body(t, par, _):
                    if on(t - 2, N):
                        wait(dve, aT_hi_ready, t - 1)
                        wait(dve, wo_done, t - 2)
                        nc.vector.tensor_tensor(aT_lo[:, :], ps_t[:, 0:DIM], aT_hi[:, :],
                                                ALU.subtract).then_inc(aT_lo_ready, 1)
                    if on(t, N):
                        wait(dve, hT_hi_ready, t + 1)
                        wait(dve, v_done, t)
                        nc.vector.tensor_tensor(hT_lo[:, :], tr[:, :], hT_hi[:, :],
                                                ALU.subtract).then_inc(hT_lo_ready, 1)
                    if on(t - 1, N):
                        s4 = ps_s.rearrange("p bank half (a b) -> p (bank half) a b", b=TOK)
                        t3 = top[:, :].rearrange("p (j a) -> p j a", j=4)
                        wait(dve, scores_done, t)
                        nc.vector.tensor_reduce(t3, s4, AX.X, ALU.max).then_inc(top_ready, 1)
                        wait(dve, top_ready, t)
                        wait(dve, probs_ready, t - 1)
                        nc.vector.tensor_tensor(shifted[:, :].rearrange("p (j a b) -> p j a b", j=4, b=TOK), s4,
                                                t3.unsqueeze(3).to_broadcast([P, 4, 4, TOK]),
                                                ALU.subtract).then_inc(shift_ready, 1)
                    if on(t - 2, N):
                        wait(dve, wo_done, t - 1)
                        wait(dve, h0_saved, t - 1)
                        nc.vector.tensor_tensor(h[:, t - 2, :], out0, h[:, t - 2, :],
                                                ALU.add).then_inc(res_ready, 1)
                    if on(t, N):
                        wait(dve, qk_done, t + 1)
                        nc.vector.tensor_tensor(rot_a[:, :].rearrange("p (s n) -> p s n", s=2), ps_qk,
                                                rope_c[:, :].rearrange("p (s n) -> p s n", s=2), ALU.mult)
                        pair = ps_qk.rearrange("p s (n two) -> p s n two", two=2)
                        sgn = rope_s[:, :].rearrange("p (s n two) -> p s n two", s=2, two=2)
                        dst = rot_b[:, :].rearrange("p (s n two) -> p s n two", s=2, two=2)
                        nc.vector.tensor_tensor(dst[:, :, :, 0], pair[:, :, :, 1], sgn[:, :, :, 0], ALU.mult)
                        nc.vector.tensor_tensor(dst[:, :, :, 1], pair[:, :, :, 0], sgn[:, :, :, 1],
                                                ALU.mult).then_inc(rot_parts, 1)
                        wait(dve, rot_parts, t + 1)
                        wait(dve, qkT_done, t)
                        s = slots[:, :].rearrange("p (n s) -> p n s", s=SLOT)
                        nc.vector.tensor_tensor(s[:, :, 0:DK0], rot_a[:, :].rearrange("p (n d) -> p n d", d=DK0),
                                                rot_b[:, :].rearrange("p (n d) -> p n d", d=DK0),
                                                ALU.add).then_inc(rotated, 1)
                    if on(t - 2, N):
                        wait_apart(dve, res_ready, t - 1)
                        nc.vector.bn_stats(bn[:, :], h[:, t - 2, :]).then_inc(bn_ready, 1)
                        wait_apart(dve, bn_ready, t - 1)
                        nc.vector.bn_aggr(mv[:, :], bn[:, :]).then_inc(var_ready, 1)
                    if on(t + 1, N):
                        embedded(t + 1)
                    if on(t - 1, N):
                        wait(dve, pT_done, t)
                        wait(dve, pv_done, t - 1)
                        nc.vector.tensor_copy(probsT[:, 4:8, :].rearrange("p a b -> p (a b)"),
                                              ps_t[:, 512:1024]).then_inc(pT_b_ready, 1)
                        o3 = ps_o[:, :].rearrange("p (n d) -> p n d", d=VW)
                        wait(dve, pv_done, t)
                        nc.vector.reciprocal(rsum[:, :], o3[:, :, DK0]).then_inc(rsum_ready, 1)
                        wait(dve, rsum_ready, t)
                        wait(dve, aT_done, t - 1)
                        nc.vector.tensor_tensor(att[:, :].rearrange("p (a j d) -> p j a d", j=4, d=DK0),
                                                o3[:, :, 0:DK0].rearrange("p (j a) d -> p j a d", j=4),
                                                rsum[:, :].rearrange("p (j a) -> p j a", j=4).unsqueeze(3)
                                                .to_broadcast([P, 4, 4, DK0]),
                                                ALU.mult).then_inc(att_ready, 1)
                    if on(t - 2, N):
                        normalise(t - 2)
                    if isinstance(t, int) and t in (0, 1, 2):
                        if t == 0:
                            dve.wait_ge(mlp_in, 64)
                        if t < 2:
                            largest(t)
                        else:
                            scales()
                            quantise(0)
                    elif isinstance(t, int) and t == 3:
                        quantise(1)

                dve.wait_ge(setup_dve, 1)
                dve.wait_ge(setup_pool, 1)
                embedded(0)
                in_pairs(dve, body, N)
                body(N, 0, 0)
                body(N + 1, 1, 0)

            @block.tensor
            def _(pe):
                def embed(t):
                    wait(pe, x_split, t + 1)
                    wait(pe, h0_ready, t)
                    split_matmul(nc, emb, both(x_hi, x_lo, P), wp_k).then_inc(emb_done, 1)

                def transposes(dst, src, n):
                    for k in range(n):
                        ins = nc.tensor.transpose(dst[:, k * P:(k + 1) * P], src[:, k * P:(k + 1) * P], ident[:, :])
                    return ins

                def scores(half):
                    for bank in range(2):
                        nc.tensor.matmul(ps_s[:, bank, half, :], ident_bf[:, :], mask[:, :], start=True, stop=False,
                                         skip_group_check=True)
                    for blk in range(4):
                        for bank in range(2):
                            j = 2 * bank + half
                            q = slice(SLOT * j, SLOT * j + SLOT)
                            for b in range(2):
                                tk = slice(64 * b, 64 * b + 64)
                                ins = nc.tensor.matmul(ps_s[tk, bank, half, blk * TOK:(blk + 1) * TOK],
                                                       qkT[q, blk, tk], qkT[q, 4 + blk, tk], start=False,
                                                       stop=blk == 3, skip_group_check=True)
                    return ins

                def body(t, par, _):
                    if on(t - 1, N):
                        wait(pe, qkT_ready, t)
                        wait(pe, shift_ready, t - 1)
                        scores(0).then_inc(half_scores, 1)
                    if on(t - 2, N):
                        wait(pe, att_ready, t - 1)
                        transposes(ps_t, att, DC).then_inc(aT_done, 1)
                    if on(t, N):
                        wait(pe, h0_ready, t + 1)
                        transposes(tr, fresh, DC).then_inc(hT_done, 1)
                    if on(t - 1, N):
                        wait(pe, half_scores, t)
                        scores(1).then_inc(scores_done, 1)
                    if on(t - 2, N):
                        wait(pe, aT_hi_ready, t - 1)
                        wait(pe, aT_lo_ready, t - 1)
                        split_matmul(nc, out0, both(aT_hi, aT_lo, P), wo_k).then_inc(wo_done, 1)
                    if on(t, N):
                        wait(pe, hT_hi_ready, t + 1)
                        wait(pe, hT_lo_ready, t + 1)
                        wait(pe, qkT_ready, t)
                        for n in range(2):
                            ins = split_matmul(nc, ps_qk[:, n, :], both(hT_hi, hT_lo, P), wqkv(n * DIM, (n + 1) * DIM))
                        ins.then_inc(qk_done, 1)
                    if on(t + 1, N):
                        embed(t + 1)
                    if on(t, N):
                        for b in range(2):
                            for half in range(2):
                                col = 2 * DIM + half * P
                                ins = split_matmul(nc, ps_v[64 * half:64 * half + 64, b, :],
                                                   both(hT_hi, hT_lo, P, 64 * b, 64 * b + 64),
                                                   wqkv(col, col + P))
                        ins.then_inc(v_done, 1)
                    if on(t - 1, N):
                        wait(pe, probs_ready, t)
                        wait(pe, res_ready, t - 1)
                        transposes(ps_t, probs, PAIRS).then_inc(pT_done, 1)
                    if on(t, N):
                        wait(pe, rotated, t + 1)
                        wait(pe, v_ready, t + 1)
                        transposes(ps_qkT, slots, 8).then_inc(qkT_done, 1)
                    if on(t - 1, N):
                        wait(pe, pT_a_ready, t)
                        wait(pe, pT_b_ready, t)
                        wait(pe, v_ready, t)
                        wait(pe, att_ready, t - 1)
                        for b in range(2):
                            tk = slice(64 * b, 64 * b + 64)
                            for pr in range(PAIRS):
                                ins = nc.tensor.matmul(ps_o[tk, pr * 2 * VW:(pr + 1) * 2 * VW], probsT[:, pr, tk],
                                                       vpair[1 - par][b][:, pr, :], start=True, stop=True)
                        ins.then_inc(pv_done, 1)

                pe.wait_ge(consts_in, 16 * CONSTANTS)
                pe.wait_ge(w_hi, 4)
                pe.wait_ge(w_lo, 3)
                pe.wait_ge(setup_pool, 9)
                embed(0)
                in_pairs(pe, body, N)
                body(N, 0, 0)
                body(N + 1, 1, 0)


def quantised_mlp(nc, A, S):
    h, w1q, w2q, b1, b2 = S["h"], S["w1q"], S["w2q"], S["b1"], S["b2"]
    bn, mv, rstd, neg_half, amax, wscale = (S["bn"], S["mv"], S["rstd"], S["neg_half"], S["amax"], S["wscale"])
    N = TILES
    CH = 4
    CHUNKS = N // CH
    W = CH * P
    with ExitStack() as c:
        def sb(name, shape, dt=F32):
            return S["sb"](name, shape, dt, c)

        def ps(name, shape, dt=F32):
            return S["ps"](name, shape, dt, c)

        hidden = sb("hidden", [P, HC, TOKENS])
        rounding = sb("rounding", [P, CH * DIM])
        xq = sb("xq", [P, CH * DIM], BF16)
        xqT = sb("xqT", [P, DC, W], BF16)
        hq = [sb(f"hq{u}", [P, HC, P], BF16) for u in range(2)]
        hmax = sb("hmax", [P, CHUNKS * 4])
        biased = sb("biased", [P, DIM])
        b1s = sb("b1s", [P, HC])
        scale_x, scale_h = sb("scale_x", [P, 5]), sb("scale_h", [P, 5])
        ps_x = ps("ps_x", [P, DC, W], BF16)
        ps_f = ps("ps_f", [P, 4, 512])
        ps_y = ps("ps_y", [P, 2, 512])
        s = {n: S["sem"](n) for n in (
            "x_max", "x_all", "x_scale", "xq_up", "xq_ready", "xT_done", "xqT_ready", "up_done", "gelu_ready",
            "hmax_ready", "h_max", "h_all", "h_scale", "hq_up", "hq_ready", "down_done", "biased_ready",
            "mlp_res", "mlp_bn", "mlp_var", "mlp_rstd", "mlp_norm")}

        with nc.Block() as block:

            @block.gpsimd
            def _(pool):
                for col, (ready, done) in ((scale_x, ("x_max", "x_all")), (scale_h, ("h_max", "h_all"))):
                    pool.wait_ge(s[ready], 1)
                    nc.gpsimd.partition_all_reduce(col[:, 1:2], col[:, 0:1], P,
                                                   bass.bass_isa.ReduceOp.max).then_inc(s[done], 1)

                def root(t):
                    wait(pool, s["mlp_var"], t + 1)
                    wait_apart(pool, s["mlp_norm"], t)
                    nc.gpsimd.tensor_scalar(rstd[:, :], mv[:, 1:2], EPS, None, ALU.add).then_inc(s["mlp_rstd"], 1)
                    wait(pool, s["mlp_rstd"], 2 * t + 1)
                    nc.gpsimd.tensor_tensor(rstd[:, :], rstd[:, :], neg_half[:, :],
                                            ALU.pow).then_inc(s["mlp_rstd"], 1)

                root(0)
                with pool.Fori(1, N) as t:
                    root(t)

            @block.vector
            def _(dve):
                def scales(col, data, w, mx, all_, done):
                    nc.vector.tensor_reduce(col[:, 0:1], data, AX.X, ALU.max).then_inc(s[mx], 1)
                    dve.wait_ge(s[all_], 1)
                    nc.vector.tensor_scalar(col[:, 2:3], col[:, 1:2], 1e-6, 1.0 / 127.0,
                                            ALU.max, ALU.mult).then_inc(s[done], 1)
                    dve.wait_ge(s[done], 1)
                    nc.vector.reciprocal(col[:, 3:4], col[:, 2:3]).then_inc(s[done], 1)
                    nc.vector.tensor_tensor(col[:, 4:5], col[:, 2:3], wscale[:, w:w + 1],
                                            ALU.mult).then_inc(s[done], 1)
                    dve.wait_ge(s[done], 3)

                scales(scale_x, amax[:, :], 0, "x_max", "x_all", "x_scale")
                nc.vector.tensor_scalar(b1s[:, :], b1[:, :], scale_x[:, 4:5], None,
                                        ALU.mult).then_inc(s["x_scale"], 1)

                def quantise(n):
                    src = h[:, bass.ts(n, CH), :].rearrange("p t d -> p (t d)")
                    nc.vector.tensor_scalar(rounding[:, :], src, scale_x[:, 3:4], ROUND,
                                            ALU.mult, ALU.add).then_inc(s["xq_up"], 1)
                    wait(dve, s["xq_up"], n + 1)
                    wait(dve, s["xT_done"], n)
                    nc.vector.tensor_scalar(xq[:, :], rounding[:, :], ROUND, None,
                                            ALU.subtract).then_inc(s["xq_ready"], 1)

                def gather(n):
                    wait(dve, s["xT_done"], n + 1)
                    wait(dve, s["up_done"], HC * n)
                    nc.vector.tensor_copy(xqT[:, :, :], ps_x[:, :, :]).then_inc(s["xqT_ready"], 1)

                def largest(n):
                    for f in range(0, HC, 2):
                        wait(dve, s["gelu_ready"], HC * n + f + 2)
                        col = n * 4 + f // 2
                        nc.vector.tensor_reduce(hmax[:, bass.ds(col, 1)], hidden[:, f:f + 2, bass.ts(n, W)],
                                                AX.XY, ALU.max, apply_absolute_value=True).then_inc(s["hmax_ready"], 1)

                quantise(0)
                gather(0)
                with dve.Fori(0, CHUNKS - 1) as n:
                    quantise(n + 1)
                    gather(n + 1)
                    largest(n)
                largest(CHUNKS - 1)
                dve.wait_ge(s["hmax_ready"], 4 * CHUNKS)
                scales(scale_h, hmax[:, :], 1, "h_max", "h_all", "h_scale")

                def quantise_hidden(t):
                    v = hidden[:, :, bass.ts(t, P)]
                    nc.vector.tensor_scalar(v, v, scale_h[:, 3:4], ROUND, ALU.mult, ALU.add).then_inc(s["hq_up"], 1)

                def finish(t, u):
                    wait(dve, s["down_done"], t + 1)
                    nc.vector.tensor_tensor(biased[:, :], ps_y[:, u, 0:DIM], b2[:, :],
                                            ALU.add).then_inc(s["biased_ready"], 1)
                    wait(dve, s["biased_ready"], t + 1)
                    nc.vector.scalar_tensor_tensor(h[:, t, :], biased[:, :], scale_h[:, 4:5], h[:, t, :],
                                                   ALU.mult, ALU.add).then_inc(s["mlp_res"], 1)
                    wait_apart(dve, s["mlp_res"], t + 1)
                    nc.vector.bn_stats(bn[:, :], h[:, t, :]).then_inc(s["mlp_bn"], 1)
                    wait_apart(dve, s["mlp_bn"], t + 1)
                    nc.vector.bn_aggr(mv[:, :], bn[:, :]).then_inc(s["mlp_var"], 1)

                def normalise(t):
                    wait(dve, s["mlp_rstd"], 2 * t + 2)
                    nc.vector.tensor_scalar(h[:, t, :], h[:, t, :], mv[:, 0:1], rstd[:, 0:1],
                                            ALU.subtract, ALU.mult).then_inc(s["mlp_norm"], 1)

                quantise_hidden(0)
                quantise_hidden(1)
                with dve.Fori(0, N // 2 - 1) as pair:
                    for u in range(2):
                        t = 2 * pair + u
                        finish(t, u)
                        quantise_hidden(t + 2)
                        normalise(t)
                for t in (N - 2, N - 1):
                    finish(t, t % 2)
                    normalise(t)

            @block.scalar
            def _(act):
                act.wait_ge(s["x_scale"], 4)
                with act.Fori(0, CHUNKS) as n:
                    for f in range(HC):
                        act.wait_ge(s["up_done"], n * HC + f + 1)
                        nc.scalar.activation(hidden[:, f, bass.ts(n, W)], ps_f[:, f % 4, :], ACT.Gelu,
                                             bias=b1s[:, f:f + 1], scale=scale_x[:, 4:5]).then_inc(s["gelu_ready"], 1)

                def lower(t, u):
                    wait(act, s["hq_up"], t + 1)
                    wait(act, s["down_done"], t - 1)
                    nc.scalar.activation(hq[u][:, :, :], hidden[:, :, bass.ts(t, P)], ACT.Copy,
                                         bias=-ROUND).then_inc(s["hq_ready"], 1)

                lower(0, 0)
                lower(1, 1)
                with act.Fori(1, N // 2) as pair:
                    lower(2 * pair, 0)
                    lower(2 * pair + 1, 1)

            @block.tensor
            def _(pe):
                def up(n):
                    wait(pe, s["xq_ready"], n + 1)
                    wait(pe, s["xqT_ready"], n)
                    for j in range(CH):
                        for k in range(DC):
                            ins = nc.tensor.transpose(ps_x[:, k, j * P:(j + 1) * P],
                                                      xq[:, j * DIM + k * P:j * DIM + (k + 1) * P],
                                                      S["ident_bf"][:, :])
                    ins.then_inc(s["xT_done"], 1)
                    wait(pe, s["xqT_ready"], n + 1)
                    for f in range(HC):
                        wait(pe, s["gelu_ready"], n * HC + f - 3)
                        for k in range(DC):
                            ins = nc.tensor.matmul(ps_f[:, f % 4, :], w1q[:, k, f * P:(f + 1) * P], xqT[:, k, :],
                                                   start=k == 0, stop=k == DC - 1)
                        ins.then_inc(s["up_done"], 1)

                def down(t, u):
                    wait(pe, s["hq_ready"], t + 1)
                    wait(pe, s["biased_ready"], t - 1)
                    for f in range(HC):
                        ins = nc.tensor.matmul(ps_y[:, u, 0:DIM], hq[u][:, f, :], w2q[:, f, :],
                                               start=f == 0, stop=f == HC - 1)
                    ins.then_inc(s["down_done"], 1)

                up(0)
                with pe.Fori(1, CHUNKS) as n:
                    up(n)
                down(0, 0)
                down(1, 1)
                with pe.Fori(1, N // 2) as pair:
                    down(2 * pair, 0)
                    down(2 * pair + 1, 1)


def cross_head_attention(nc, A, S):
    h, ident, ident_bf = S["h"], S["ident"], S["ident_bf"]
    bn, mv, rstd, neg_half = S["bn"], S["mv"], S["rstd"], S["neg_half"]
    MACRO = 2 * P
    M = TOKENS // MACRO
    GROUPS = MACRO // 4
    UNITS = M * 4
    UG = 16
    R = 3 * HEADS1 * DK1 // MACRO
    QKV = 3 * HEADS1 * DK1
    OC = HEADS1 * DK1 // P
    with ExitStack() as c:
        def sb(name, shape, dt=F32):
            return S["sb"](name, shape, dt, c)

        def ps(name, shape, dt=F32):
            return S["ps"](name, shape, dt, c)

        qkv = [sb(f"qkv{par}", [P, 3, GROUPS, HEADS1, 4]) for par in range(2)]
        w_hi, w_lo = sb("wqkv1_hi", [P, DC * QKV], BF16), sb("wqkv1_lo", [P, DC * QKV], BF16)
        wp_hi, wp_lo = sb("wp1_hi", [P, OC * DIM], BF16), sb("wp1_lo", [P, OC * DIM], BF16)
        stage = qkv[1][:, :, :, :, :].rearrange("p x g i t -> p (x g i t)")
        stage_w = stage[:, 0:DC * QKV].rearrange("p (kk n) -> p kk n", kk=DC)
        stage_p = stage[:, DC * QKV:DC * QKV + OC * DIM]

        def weights(n, w, p):
            if n == 3:
                return p
            w = w.rearrange("p (kk n) -> p kk n", kk=DC) if len(w.shape) == 2 else w
            return w[:, :, n * QKV // 3:(n + 1) * QKV // 3]
        mask = sb("mask1", [P, 512], BF16)
        mask_f = sb("mask1_f", [P, 512])
        bp = sb("bp", [P, DIM])
        hs = sb("hs", [P, 2, DIM])
        hT_hi = [sb(f"h1T_hi{u}", [P, DC, MACRO], BF16) for u in range(2)]
        hT_lo = [sb(f"h1T_lo{u}", [P, DC, MACRO], BF16) for u in range(2)]
        top = sb("top1", [P, 8])
        sums = sb("sums1", [P, 8])
        inv = sb("inv1", [P, 8])
        shifted = sb("shifted1", [P, 512])
        probs = sb("probs1", [P, 512])
        normed = sb("normed1", [P, 512])
        probsT = sb("probsT1", [P, 512])
        vdiag = sb("vdiag", [P, 8, P])
        oT_hi, oT_lo = sb("oT_hi", [P, OC, P], BF16), sb("oT_lo", [P, OC, P], BF16)

        ps_tr = ps("ps_tr1", [P, DC, MACRO])
        ps_p = [ps(f"ps_p{u}", [P, 2, MACRO]) for u in range(2)]
        ps_s = ps("ps_s1", [P, 512])
        ps_t = ps("ps_t1", [P, 512])
        ps_v = ps("ps_v1", [P, 512])
        ps_o = ps("ps_o1", [P, 512])
        ps_y = ps("ps_y1", [P, 512])

        w_in = [S["sem"](f"a1_w_in{n}") for n in range(4)]
        s = {n: S["sem"](n) for n in (
            "a1_consts", "mask_ready", "a1_w_hi", "a1_w_lo", "a1_zero", "hs_ready", "hb_ready", "a1_tr_done",
            "a1_hT_hi", "a1_hT_lo", "proj_done", "proj_act", "proj_dve", "a1_scores", "a1_top", "a1_shift",
            "a1_probs", "a1_sum", "a1_inv", "a1_normed", "a1_pT_done", "a1_pT", "a1_vT_done", "vdiag_act",
            "vdiag_dve", "a1_pv", "oT_hi_ready", "oT_lo_ready", "a1_out", "a1_res", "a1_bn", "a1_var",
            "a1_rstd", "a1_norm")}

        def rows(m):
            return h[:, 2 * m:2 * m + 2, :] if isinstance(m, int) else h[:, bass.ts(m, 2), :]

        def sequence(eng, body):
            body(0, 0)
            body(1, 1)
            with eng.Fori(1, M // 2 - 1) as pair:
                body(2 * pair, 0)
                body(2 * pair + 1, 1)
            for m in range(M - 2, M + 2):
                body(m, m % 2)

        with nc.Block() as block:

            @block.sync
            def _(sp):
                for n in range(4):
                    if n == 1:
                        sp.dma_start(bp[:, :], A["bp"]).then_inc(s["a1_consts"], 16)
                        sp.dma_start(mask_f[:, :], A["mask1"]).then_inc(s["a1_consts"], 16)
                    sp.dma_start(weights(n, stage_w, stage_p),
                                 weights(n, A["wqkv1"], A["wp1"])).then_inc(w_in[n], 16)

            def slot_index(m, u):
                return 4 * (m - 1) + u

            def tile_index(m, u):
                return 2 * m - 3 + (u - 1) // 2

            @block.scalar
            def _(act):
                def high(n):
                    act.wait_ge(w_in[n], 16)
                    nc.scalar.copy(weights(n, w_hi[:, :], wp_hi[:, :]),
                                   weights(n, stage_w, stage_p)).then_inc(s["a1_w_hi"], 1)

                def transposed(m, par):
                    wait(act, s["a1_tr_done"], m + 1)
                    wait(act, s["proj_done"], R * (m - 1))
                    nc.scalar.copy(hT_hi[par][:, :, :], ps_tr[:, :, :]).then_inc(s["a1_hT_hi"], 1)

                def evacuate(m, par, r):
                    wait(act, s["proj_done"], R * m + r + 1)
                    if r == 0:
                        wait(act, s["a1_vT_done"], 4 * (m - 1))
                        if isinstance(m, int) and m == 1:
                            act.wait_ge(s["a1_w_lo"], 4)
                    i = 4 * (r % 4)
                    nc.scalar.copy(qkv[par][0:64, r // 4, :, i:i + 3:2, :].rearrange("p g a t -> p a g t"),
                                   ps_p[r % 2][0:64, :, :].rearrange("p a (g t) -> p a g t", t=4)
                                   ).then_inc(s["proj_act"], 1)

                def body(m, par):
                    for u in range(4):
                        k = slot_index(m, u)
                        if on(m, M):
                            evacuate(m, par, 3 * u)
                            if isinstance(m, int) and m == 0 and u < 3:
                                high(u + 1)
                        if on(k, UNITS):
                            wait(act, s["a1_shift"], k + 1)
                            wait(act, s["a1_normed"], k)
                            nc.scalar.activation(probs[:, :], shifted[:, :], ACT.Exp,
                                                 scale=float(DK1) ** -0.5).then_inc(s["a1_probs"], 1)
                        if on(k - 1, UNITS):
                            wait(act, s["a1_pT_done"], k)
                            wait(act, s["a1_pv"], k - 1)
                            nc.scalar.copy(probsT[:, :], ps_t[:, :]).then_inc(s["a1_pT"], 1)
                        if on(m, M):
                            evacuate(m, par, 3 * u + 1)
                        if on(k - 1, UNITS):
                            wait(act, s["a1_pv"], k)
                            if (u - 1) % 2 == 0:
                                wait(act, s["a1_out"], 2 * m - 3 + (u + 1) // 2)
                            src = ps_o[:, :].rearrange("p (ca m two t) -> p two m ca t", ca=8, two=2, t=4)
                            half = slice(64 * ((u - 1) % 2), 64 * ((u - 1) % 2) + 64)
                            dst = oT_hi[:, :, half].rearrange("p m (ca pp t) -> p pp m ca t", pp=2, t=4)
                            for pp in range(2):
                                for ip in range(2):
                                    ins = nc.scalar.copy(dst[64 * ip:64 * ip + 64, pp], src[64 * pp:64 * pp + 64, ip])
                            ins.then_inc(s["oT_hi_ready"], 1)
                        if on(k, UNITS):
                            wait(act, s["a1_vT_done"], k + 1)
                            wait(act, s["a1_pv"], k)
                            nc.scalar.copy(vdiag[0:64, :, 0:64],
                                           ps_v[0:64, :].rearrange("p (a d) -> p a d", d=64)
                                           ).then_inc(s["vdiag_act"], 1)
                        if on(m, M):
                            evacuate(m, par, 3 * u + 2)
                        if u == 1 and on(m + 1, M):
                            transposed(m + 1, 1 - par)

                high(0)
                transposed(0, 0)
                act.wait_ge(s["a1_consts"], 32)
                nc.scalar.copy(mask[:, :], mask_f[:, :]).then_inc(s["mask_ready"], 1)
                sequence(act, body)

            @block.gpsimd
            def _(pool):
                def fetch(m):
                    wait(pool, s["a1_tr_done"], m)
                    nc.gpsimd.tensor_copy(hs[:, :, :], rows(m)).then_inc(s["hs_ready"], 1)
                    if isinstance(m, int) and m == 0:
                        pool.wait_ge(s["a1_consts"], 32)
                    nc.gpsimd.tensor_tensor(rows(m), rows(m), bp[:, :].unsqueeze(1).to_broadcast([P, 2, DIM]),
                                            ALU.add).then_inc(s["hb_ready"], 1)

                def body(m, par):
                    for u in range(4):
                        k = slot_index(m, u)
                        if u == 1 and on(m + 1, M):
                            fetch(m + 1)
                        if on(k, UNITS):
                            wait(pool, s["a1_inv"], k + 1)
                            wait(pool, s["a1_pT_done"], k)
                            nc.gpsimd.tensor_tensor(normed[:, :].rearrange("p (a b) -> p a b", b=64),
                                                    probs[:, :].rearrange("p (a b) -> p a b", b=64),
                                                    inv[:, :].unsqueeze(2).to_broadcast([P, 8, 64]),
                                                    ALU.mult).then_inc(s["a1_normed"], 1)
                        if u % 2 and on(tile_index(m, u), TILES):
                            j = tile_index(m, u)
                            wait(pool, s["a1_var"], j + 1)
                            wait_apart(pool, s["a1_norm"], j)
                            nc.gpsimd.tensor_scalar(rstd[:, :], mv[:, 1:2], EPS, None,
                                                    ALU.add).then_inc(s["a1_rstd"], 1)
                            wait(pool, s["a1_rstd"], 2 * j + 1)
                            nc.gpsimd.tensor_tensor(rstd[:, :], rstd[:, :], neg_half[:, :],
                                                    ALU.pow).then_inc(s["a1_rstd"], 1)

                fetch(0)
                nc.gpsimd.memset(vdiag[:, :, :], 0.0).then_inc(s["a1_zero"], 1)
                sequence(pool, body)

            @block.vector
            def _(dve):
                def low(n):
                    dve.wait_ge(s["a1_w_hi"], n + 1)
                    nc.vector.tensor_tensor(weights(n, w_lo[:, :], wp_lo[:, :]),
                                            weights(n, stage_w, stage_p),
                                            weights(n, w_hi[:, :], wp_hi[:, :]),
                                            ALU.subtract).then_inc(s["a1_w_lo"], 1)

                def transposed(m, par):
                    wait(dve, s["a1_hT_hi"], m + 1)
                    wait(dve, s["proj_done"], R * (m - 1))
                    nc.vector.tensor_tensor(hT_lo[par][:, :, :], ps_tr[:, :, :], hT_hi[par][:, :, :],
                                            ALU.subtract).then_inc(s["a1_hT_lo"], 1)

                def evacuate(m, par, r):
                    wait(dve, s["proj_done"], R * m + r + 1)
                    if r == 0:
                        wait(dve, s["a1_vT_done"], 4 * (m - 1))
                    i = 4 * (r % 4) + 1
                    nc.vector.tensor_copy(qkv[par][0:64, r // 4, :, i:i + 3:2, :].rearrange("p g a t -> p a g t"),
                                          ps_p[r % 2][64:128, :, :].rearrange("p a (g t) -> p a g t", t=4)
                                          ).then_inc(s["proj_dve"], 1)

                def body(m, par):
                    for u in range(4):
                        k = slot_index(m, u)
                        s3 = ps_s[:, :].rearrange("p (a b) -> p a b", b=64)
                        if on(k, UNITS):
                            wait(dve, s["a1_scores"], k + 1)
                            nc.vector.tensor_reduce(top[:, :], s3, AX.X, ALU.max).then_inc(s["a1_top"], 1)
                            wait(dve, s["a1_top"], k + 1)
                            wait(dve, s["a1_probs"], k)
                            nc.vector.tensor_tensor(shifted[:, :].rearrange("p (a b) -> p a b", b=64), s3,
                                                    top[:, :].unsqueeze(2).to_broadcast([P, 8, 64]),
                                                    ALU.subtract).then_inc(s["a1_shift"], 1)
                        if on(m, M):
                            evacuate(m, par, 3 * u)
                            if isinstance(m, int) and m == 0 and u < 3:
                                low(u + 1)
                        if u % 2 and on(tile_index(m, u), TILES):
                            j = tile_index(m, u)
                            wait(dve, s["a1_out"], j + 1)
                            nc.vector.tensor_tensor(h[:, j, :], ps_y[:, 0:DIM], h[:, j, :],
                                                    ALU.add).then_inc(s["a1_res"], 1)
                            wait_apart(dve, s["a1_res"], j + 1)
                            nc.vector.bn_stats(bn[:, :], h[:, j, :]).then_inc(s["a1_bn"], 1)
                            wait_apart(dve, s["a1_bn"], j + 1)
                            nc.vector.bn_aggr(mv[:, :], bn[:, :]).then_inc(s["a1_var"], 1)
                        if on(k, UNITS):
                            wait(dve, s["a1_probs"], k + 1)
                            nc.vector.tensor_reduce(sums[:, :], probs[:, :].rearrange("p (a b) -> p a b", b=64),
                                                    AX.X, ALU.add).then_inc(s["a1_sum"], 1)
                            wait(dve, s["a1_sum"], k + 1)
                            wait(dve, s["a1_normed"], k)
                            nc.vector.reciprocal(inv[:, :], sums[:, :]).then_inc(s["a1_inv"], 1)
                        if on(m, M):
                            evacuate(m, par, 3 * u + 1)
                        if on(k - 1, UNITS):
                            wait(dve, s["oT_hi_ready"], k)
                            if (u - 1) % 2 == 0:
                                wait(dve, s["a1_out"], 2 * m - 3 + (u + 1) // 2)
                            src = ps_o[:, :].rearrange("p (ca m two t) -> p two m ca t", ca=8, two=2, t=4)
                            half = slice(64 * ((u - 1) % 2), 64 * ((u - 1) % 2) + 64)
                            hi = oT_hi[:, :, half].rearrange("p m (ca pp t) -> p pp m ca t", pp=2, t=4)
                            lo = oT_lo[:, :, half].rearrange("p m (ca pp t) -> p pp m ca t", pp=2, t=4)
                            for pp in range(2):
                                for ip in range(2):
                                    q = slice(64 * ip, 64 * ip + 64)
                                    ins = nc.vector.tensor_tensor(lo[q, pp], src[64 * pp:64 * pp + 64, ip],
                                                                  hi[q, pp], ALU.subtract)
                            ins.then_inc(s["oT_lo_ready"], 1)
                        if on(k, UNITS):
                            wait(dve, s["a1_vT_done"], k + 1)
                            wait(dve, s["a1_pv"], k)
                            nc.vector.tensor_copy(vdiag[64:128, :, 64:128],
                                                  ps_v[64:128, :].rearrange("p (a d) -> p a d", d=64)
                                                  ).then_inc(s["vdiag_dve"], 1)
                        if on(m, M):
                            evacuate(m, par, 3 * u + 2)
                        if u == 1 and on(m + 1, M):
                            transposed(m + 1, 1 - par)
                        if u % 2 and on(tile_index(m, u), TILES):
                            j = tile_index(m, u)
                            wait(dve, s["a1_rstd"], 2 * j + 2)
                            nc.vector.tensor_scalar(h[:, j, :], h[:, j, :], mv[:, 0:1], rstd[:, 0:1],
                                                    ALU.subtract, ALU.mult).then_inc(s["a1_norm"], 1)

                low(0)
                transposed(0, 0)
                dve.wait_ge(s["a1_zero"], 1)
                sequence(dve, body)

            @block.tensor
            def _(pe):
                def transposes(m):
                    wait(pe, s["hs_ready"], m + 1)
                    wait(pe, s["a1_hT_lo"], m)
                    for j in range(2):
                        for kk in range(DC):
                            ins = nc.tensor.transpose(ps_tr[:, kk, j * P:(j + 1) * P],
                                                      hs[:, j, kk * P:(kk + 1) * P], ident[:, :])
                    ins.then_inc(s["a1_tr_done"], 1)

                def project(m, par, r):
                    if r == 0:
                        wait(pe, s["a1_hT_hi"], m + 1)
                        wait(pe, s["a1_hT_lo"], m + 1)
                    if isinstance(m, int) and m == 0 and r % 4 == 0:
                        pe.wait_ge(s["a1_w_lo"], r // 4 + 1)
                    wait(pe, s["proj_act"], R * m + r - 1)
                    wait(pe, s["proj_dve"], R * m + r - 1)
                    x = [(hT_hi[par][:, kk, :], hT_lo[par][:, kk, :]) for kk in range(DC)]
                    for a in range(2):
                        col = (2 * r + a) * P
                        w = [(w_hi[:, kk * QKV + col:kk * QKV + col + P], w_lo[:, kk * QKV + col:kk * QKV + col + P])
                             for kk in range(DC)]
                        ins = split_matmul(nc, ps_p[r % 2][:, a, :], w, x)
                    ins.then_inc(s["proj_done"], 1)

                def body(m, par):
                    prev = qkv[1 - par]
                    for u in range(4):
                        k = slot_index(m, u)
                        if on(k, UNITS):
                            if isinstance(m, int) and m == 1 and u == 0:
                                pe.wait_ge(s["mask_ready"], 1)
                                pe.wait_ge(s["a1_w_lo"], 4)
                            if u == 0:
                                wait(pe, s["proj_act"], R * (m - 1) + 8)
                                wait(pe, s["proj_dve"], R * (m - 1) + 8)
                            wait(pe, s["a1_shift"], k)
                            nc.tensor.matmul(ps_s[:, :], ident_bf[:, :], mask[:, :], start=True, stop=False,
                                             skip_group_check=True)
                            for g in range(UG):
                                cc, ab, pp = g // 4, g // 2 % 2, g % 2
                                q, kx = (prev[0:64, x, UG * u + g, :, :].rearrange("p i t -> p (i t)") for x in (0, 1))
                                ins = nc.tensor.matmul(ps_s[64 * ab:64 * ab + 64, (2 * cc + pp) * 64:(2 * cc + pp + 1) * 64],
                                                       q, kx, start=False, stop=g >= UG - 4, skip_group_check=True)
                            ins.then_inc(s["a1_scores"], 1)
                        if on(m, M):
                            project(m, par, 3 * u)
                        if u % 2 and on(tile_index(m, u), TILES):
                            j = tile_index(m, u)
                            wait(pe, s["oT_hi_ready"], 2 * j + 2)
                            wait(pe, s["oT_lo_ready"], 2 * j + 2)
                            wait(pe, s["a1_res"], j)
                            split_matmul(nc, ps_y[:, 0:DIM],
                                         [(oT_hi[:, n, :], oT_lo[:, n, :]) for n in range(OC)],
                                         [(wp_hi[:, n * DIM:(n + 1) * DIM], wp_lo[:, n * DIM:(n + 1) * DIM])
                                          for n in range(OC)]).then_inc(s["a1_out"], 1)
                        if on(k - 1, UNITS):
                            wait(pe, s["a1_normed"], k)
                            wait(pe, s["a1_pT"], k - 1)
                            for cc in range(4):
                                ins = nc.tensor.transpose(ps_t[:, cc * P:(cc + 1) * P], normed[:, cc * P:(cc + 1) * P],
                                                          ident[:, :])
                            ins.then_inc(s["a1_pT_done"], 1)
                        if on(m, M):
                            project(m, par, 3 * u + 1)
                        if on(k - 1, UNITS):
                            wait(pe, s["a1_pT"], k)
                            wait(pe, s["vdiag_act"], k)
                            wait(pe, s["vdiag_dve"], k)
                            wait(pe, s["oT_lo_ready"], k - 1)
                            for ca in range(8):
                                ins = nc.tensor.matmul(ps_o[:, ca * 64:(ca + 1) * 64], vdiag[:, ca, :],
                                                       probsT[:, (ca // 2) * P + (ca % 2) * 64:
                                                              (ca // 2) * P + (ca % 2) * 64 + 64],
                                                       start=True, stop=True)
                            ins.then_inc(s["a1_pv"], 1)
                        if on(k, UNITS):
                            wait(pe, s["vdiag_act"], k)
                            if u == 0:
                                wait(pe, s["proj_act"], R * m)
                                wait(pe, s["proj_dve"], R * m)
                            wait_apart(pe, s["vdiag_dve"], k)
                            for ca in range(8):
                                g = UG * u + 2 * ca
                                ins = nc.tensor.transpose(ps_v[:, ca * 64:(ca + 1) * 64],
                                                          prev[0:64, 2, g:g + 2, :, :].rearrange("p g i t -> p (g i t)"),
                                                          ident[0:64, 0:64])
                            ins.then_inc(s["a1_vT_done"], 1)
                        if on(m, M):
                            project(m, par, 3 * u + 2)
                        if u == 1 and on(m + 1, M):
                            transposes(m + 1)

                transposes(0)
                sequence(pe, body)


def experts(nc, A, S, out):
    h, ident, ident_bf = S["h"], S["ident"], S["ident_bf"]
    bn, mv, rstd, neg_half = S["bn"], S["mv"], S["rstd"], S["neg_half"]
    N = TILES
    E = EXPERTS
    SLOT_TILES = 2 * TOKENS // P + E
    FC = FF // P
    WCOLS = DC * 2 * FF
    RING = 4

    h_rows = nc.dram_tensor("h_rows", (TOKENS, DIM), F32, kind="Internal").ap()
    y_rows = nc.dram_tensor("y_rows", (SLOT_TILES * P, DIM), F32, kind="Internal").ap()
    bias_rows = nc.dram_tensor("bias_rows", (3, E * 2 * FF), BF16, kind="Internal").ap()

    with ExitStack() as c:
        def sb(name, shape, dt=F32, cc=c):
            return S["sb"](name, shape, dt, cc)

        w_hi, w_lo = sb("we_hi", [P, E, WCOLS], BF16), sb("we_lo", [P, E, WCOLS], BF16)
        wo_hi, wo_lo = sb("wo2_hi", [P, FC * DIM], BF16), sb("wo2_lo", [P, FC * DIM], BF16)
        bias3 = sb("bias3", [3, E * 2 * FF], BF16)
        ones3 = sb("ones3", [3, P], BF16)
        bo = sb("bo", [P, DIM])
        share = [sb(f"share{n}", [P, N]) for n in range(2)]
        slot = [sb(f"slot{n}", [P, N], U32) for n in range(2)]
        owner = sb("owner", [P, SLOT_TILES], mybir.dt.int32)
        source = sb("source", [P, SLOT_TILES], U32)
        s_gate = {n: S["sem"](n) for n in (
            "e_consts", "e_w_in", "e_w_hi", "e_w_lo", "e_small", "e_bias_dma", "h_out", "g_fetch", "g_trans",
            "g_hT", "g_logit", "g_exp", "g_chain", "g_pool", "g_count", "g_onehot", "g_inv")}

        with ExitStack() as cg:
            def gb(name, shape, dt=F32):
                return S["sb"](name, shape, dt, cg)

            stage = gb("stage_we", [P, RING, WCOLS])
            wo_f = gb("wo_f", [P, FC * DIM])
            wg = gb("wg", [P, DC * E])
            b1f = gb("b1f", [P, 64])
            b1r = gb("b1r", [P, 64])
            b1p = gb("b1p", [P, 3, 64], BF16)
            lower_f = gb("lower_f", [P, P])
            lower = gb("lower", [P, P], BF16)
            ones = gb("ones", [P, P], BF16)
            count = gb("count", [P, P])
            row = gb("row", [P, 1])
            rank = gb("rank", [P, E])
            tnum = gb("tnum", [P, N])
            hs = gb("hs2", [P, 2 * DIM])
            hT = gb("hT2", [P, 2 * DIM])
            big = {n: gb("g_" + n, [P, N, E]) for n in
                   ("p", "d", "pm", "cand", "oh0", "oh1", "cum_a", "cum_b", "cnt", "pos", "sel")}
            assigned = gb("assigned", [P, N, E], BF16)
            col = {n: gb("gc_" + n, [P, N]) for n in ("mx", "se", "cm", "v0", "v1", "slotf0", "slotf1", "hi", "lo")}
            exp8 = {n: gb("ge_" + n, [P, E]) for n in ("t", "end_a", "end_b", "off")}
            belongs = gb("belongs", [P, SLOT_TILES, E])
            ownf = gb("ownf", [P, SLOT_TILES])
            lo1 = gb("lo1", [P, N, P], BF16)
            hi1 = gb("hi1", [P, N, 2 * SLOT_TILES], BF16)
            ps_x = S["ps"]("ps_gx", [P, 512], F32, cg)
            ps_l = S["ps"]("ps_gl", [P, N, E], F32, cg)
            ps_pre = S["ps"]("ps_gpre", [P, N * E], F32, cg)
            ps_cnt = S["ps"]("ps_gcnt", [P, N * E], F32, cg)
            ps_inv = S["ps"]("ps_ginv", [P, 2 * SLOT_TILES], F32, cg)
            s = s_gate
            with nc.Block() as block:

                @block.sync
                def _(sp):
                    sp.dma_start(h_rows.rearrange("(t p) d -> p t d", p=P), h[:, :, :]).then_inc(s["h_out"], 16)
                    for e in range(E):
                        if e >= RING:
                            sp.wait_ge(s["e_w_lo"], e - RING + 1)
                        if e:
                            sp.wait_ge(s["e_w_in"], 16 * e)
                        sp.dma_start(stage[:, e % RING, :], A["we"][:, e, :]).then_inc(s["e_w_in"], 16)
                    sp.wait_ge(s["h_out"], 16)

                @block.scalar
                def _(act):
                    for dst, name in ((wg, "wg"), (b1f, "be"), (lower_f, "lower"), (count, "count"), (row, "row"),
                                      (rank, "rank"), (tnum, "tnum"), (bo, "bo"), (wo_f, "wo2")):
                        act.dma_start(dst[:, :], A[name]).then_inc(s["e_consts"], 16)
                    act.wait_ge(s["e_consts"], 16 * 9)
                    act.wait_ge(s["e_small"], 5)
                    act.dma_start(bias_rows.rearrange("n (p f) -> p n f", p=P), b1p[:, :, :]
                                  ).then_inc(s["e_bias_dma"], 16)
                    act.wait_ge(s["e_bias_dma"], 16)
                    act.dma_start(bias3[:, :], bias_rows).then_inc(s["e_bias_dma"], 16)
                    nc.scalar.copy(lower[:, :], lower_f[:, :])
                    nc.scalar.copy(wo_hi[:, :], wo_f[:, :]).then_inc(s["e_w_hi"], 1)
                    for e in range(2):
                        act.wait_ge(s["e_w_in"], 16 * (e + 1))
                        nc.scalar.copy(w_hi[:, e, :], stage[:, e % RING, :]).then_inc(s["e_w_hi"], 1)
                    act.wait_ge(s["g_chain"], 2)
                    nc.scalar.activation(big["p"][:, :, :], big["d"][:, :, :], ACT.Exp).then_inc(s["g_exp"], 1)
                    for e in range(2, E):
                        act.wait_ge(s["e_w_in"], 16 * (e + 1))
                        nc.scalar.copy(w_hi[:, e, :], stage[:, e % RING, :]).then_inc(s["e_w_hi"], 1)
                    act.wait_ge(s["e_bias_dma"], 32)

                @block.gpsimd
                def _(pool):
                    nc.gpsimd.memset(ones[:, :], 1.0)
                    nc.gpsimd.memset(ones3[:, :], 1.0).then_inc(s["g_pool"], 1)

                    def fetch(n):
                        wait(pool, s["g_trans"], n)
                        nc.gpsimd.tensor_copy(hs[:, :].rearrange("p (t d) -> p t d", t=2),
                                              h[:, bass.ts(n, 2), :]).then_inc(s["g_fetch"], 1)

                    fetch(0)
                    with pool.Fori(1, N // 2) as n:
                        fetch(n)
                    for e in range(E):
                        pool.wait_ge(s["e_w_hi"], e + 2)
                        nc.gpsimd.tensor_tensor(w_lo[:, e, :], stage[:, e % RING, :], w_hi[:, e, :],
                                                ALU.subtract).then_inc(s["e_w_lo"], 1)

                @block.tensor
                def _(pe):
                    pe.wait_ge(s["e_consts"], 16 * 9)
                    pe.wait_ge(s["g_pool"], 1)

                    def logits(n):
                        wait(pe, s["g_fetch"], n + 1)
                        wait(pe, s["g_hT"], n)
                        for k in range(4):
                            ins = nc.tensor.transpose(ps_x[:, k * P:(k + 1) * P], hs[:, k * P:(k + 1) * P],
                                                      ident[:, :])
                        ins.then_inc(s["g_trans"], 1)
                        wait(pe, s["g_hT"], n + 1)
                        for j in range(2):
                            for k in range(DC):
                                ins = nc.tensor.matmul(ps_l[:, bass.ds(2 * n + j, 1), :].rearrange("p a e -> p (a e)"),
                                                       hT[:, (2 * j + k) * P:(2 * j + k + 1) * P],
                                                       wg[:, k * E:(k + 1) * E], start=k == 0, stop=k == DC - 1)
                        ins.then_inc(s["g_logit"], 1)

                    logits(0)
                    with pe.Fori(1, N // 2) as n:
                        logits(n)
                    pe.wait_ge(s["e_w_hi"], 1)
                    pe.wait_ge(s["g_count"], 1)
                    a = assigned[:, :, :].rearrange("p t e -> p (t e)")
                    nc.tensor.matmul(ps_pre[:, :], lower[:, :], a, start=True, stop=True)
                    nc.tensor.matmul(ps_cnt[:, :], ones[:, :], a, start=True, stop=True).then_inc(s["g_count"], 1)
                    for ch in range(2):
                        pe.wait_ge(s["g_onehot"], ch + 1)
                        for t in range(N):
                            ins = nc.tensor.matmul(ps_inv[:, :], lo1[:, t, :], hi1[:, t, :],
                                                   start=ch == 0 and t == 0, stop=ch == 1 and t == N - 1)
                        ins.then_inc(s["g_inv"], 1)

                @block.vector
                def _(dve):
                    chain = [0]

                    def link(ins):
                        chain[0] += 1
                        ins.then_inc(s["g_chain"], 1)
                        dve.wait_ge(s["g_chain"], chain[0])

                    dve.wait_ge(s["e_consts"], 16 * 9)
                    small = 0
                    for part in range(3):
                        src = b1f if part == 0 else b1r
                        nc.vector.tensor_copy(b1p[:, part, :], src[:, :]).then_inc(s["e_small"], 1)
                        small += 1
                        dve.wait_ge(s["e_small"], small)
                        if part < 2:
                            nc.vector.tensor_tensor(b1r[:, :], src[:, :], b1p[:, part, :],
                                                    ALU.subtract).then_inc(s["e_small"], 1)
                            small += 1
                            dve.wait_ge(s["e_small"], small)
                    dve.wait_ge(s["e_w_hi"], 1)
                    nc.vector.tensor_tensor(wo_lo[:, :], wo_f[:, :], wo_hi[:, :], ALU.subtract).then_inc(s["e_small"], 1)

                    def transposed(n):
                        wait(dve, s["g_trans"], n + 1)
                        wait(dve, s["g_logit"], n)
                        nc.vector.tensor_copy(hT[:, :], ps_x[:, :]).then_inc(s["g_hT"], 1)

                    transposed(0)
                    with dve.Fori(1, N // 2) as n:
                        transposed(n)

                    def over_e(x):
                        return x[:, :].unsqueeze(2).to_broadcast([P, N, E])

                    def over_t(x):
                        return x[:, :].unsqueeze(1).to_broadcast([P, N, E])

                    def tt(o, a, b, op):
                        link(nc.vector.tensor_tensor(o, a, b, op))

                    def full(x):
                        return big[x][:, :, :]

                    dve.wait_ge(s["g_logit"], N // 2)
                    link(nc.vector.tensor_reduce(col["mx"][:, :], ps_l[:, :, :], AX.X, ALU.max))
                    tt(full("d"), ps_l[:, :, :], over_e(col["mx"]), ALU.subtract)
                    dve.wait_ge(s["g_exp"], 1)
                    link(nc.vector.tensor_reduce(col["se"][:, :], full("p"), AX.X, ALU.add))
                    link(nc.vector.reciprocal(col["se"][:, :], col["se"][:, :]))
                    tt(full("p"), full("p"), over_e(col["se"]), ALU.mult)
                    for ch in range(2):
                        pm, oh, v = full("p") if ch == 0 else full("pm"), full(f"oh{ch}"), col[f"v{ch}"]
                        link(nc.vector.tensor_reduce(v[:, :], pm, AX.X, ALU.max))
                        tt(full("cand"), pm, over_e(v), ALU.is_equal)
                        tt(full("cand"), full("cand"), over_t(rank), ALU.mult)
                        link(nc.vector.tensor_reduce(col["cm"][:, :], full("cand"), AX.X, ALU.max))
                        tt(oh, full("cand"), over_e(col["cm"]), ALU.is_equal)
                        if ch == 0:
                            link(nc.vector.scalar_tensor_tensor(full("pm"), oh, -4.0, full("p"), ALU.mult, ALU.add))
                    tt(col["se"][:, :], col["v0"][:, :], col["v1"][:, :], ALU.add)
                    link(nc.vector.tensor_scalar(col["se"][:, :], col["se"][:, :], 1e-9, None, ALU.add))
                    link(nc.vector.reciprocal(col["se"][:, :], col["se"][:, :]))
                    for ch in range(2):
                        tt(share[ch][:, :], col[f"v{ch}"][:, :], col["se"][:, :], ALU.mult)
                    nc.vector.tensor_tensor(assigned[:, :, :], full("oh0"), full("oh1"), ALU.add
                                            ).then_inc(s["g_count"], 1)
                    dve.wait_ge(s["g_count"], 2)
                    link(nc.vector.tensor_copy(full("cnt").rearrange("p t e -> p (t e)"), ps_cnt[:, :]))
                    a, b = "cnt", "cum_a"
                    step = 1
                    while step < N:
                        nc.vector.tensor_copy(big[b][:, 0:step, :], big[a][:, 0:step, :])
                        tt(big[b][:, step:N, :], big[a][:, step:N, :], big[a][:, 0:N - step, :], ALU.add)
                        a, b = b, "cum_b" if b == "cum_a" else "cum_a"
                        step *= 2
                    total = big[a][:, N - 1, :]
                    t8 = exp8["t"][:, :]
                    link(nc.vector.tensor_scalar(t8, total, 1.0 / P, 63.5 / P, ALU.mult, ALU.add))
                    link(nc.vector.tensor_scalar(t8, t8, ROUND, None, ALU.add))
                    link(nc.vector.tensor_scalar(t8, t8, ROUND, None, ALU.subtract))
                    x, y = "t", "end_a"
                    step = 1
                    while step < E:
                        nc.vector.tensor_copy(exp8[y][:, 0:step], exp8[x][:, 0:step])
                        tt(exp8[y][:, step:E], exp8[x][:, step:E], exp8[x][:, 0:E - step], ALU.add)
                        x, y = y, "end_b" if y == "end_a" else "end_a"
                        step *= 2
                    end = exp8[x]
                    tt(exp8["off"][:, :], end[:, :], t8, ALU.subtract)
                    link(nc.vector.tensor_scalar(exp8["off"][:, :], exp8["off"][:, :], float(P), None, ALU.mult))
                    tt(full("pos"), big[a][:, :, :], full("cnt"), ALU.subtract)
                    tt(full("pos"), full("pos"), over_t(exp8["off"]), ALU.add)
                    tt(full("pos").rearrange("p t e -> p (t e)"), ps_pre[:, :],
                       full("pos").rearrange("p t e -> p (t e)"), ALU.add)
                    tt(belongs[:, :, :], end[:, :].unsqueeze(1).to_broadcast([P, SLOT_TILES, E]),
                       count[:, 0:SLOT_TILES].unsqueeze(2).to_broadcast([P, SLOT_TILES, E]), ALU.is_le)
                    link(nc.vector.tensor_reduce(ownf[:, :], belongs[:, :, :], AX.X, ALU.add))
                    link(nc.vector.tensor_scalar(owner[:, :], ownf[:, :], float(E - 1), None, ALU.min))
                    for ch in range(2):
                        sf, hi, lo = col[f"slotf{ch}"][:, :], col["hi"], col["lo"]
                        tt(full("sel"), full(f"oh{ch}"), full("pos"), ALU.mult)
                        link(nc.vector.tensor_reduce(sf, full("sel"), AX.X, ALU.add))
                        link(nc.vector.tensor_copy(slot[ch][:, :], sf))
                        link(nc.vector.tensor_scalar(hi[:, :], sf, 1.0 / P, -63.5 / P, ALU.mult, ALU.add))
                        link(nc.vector.tensor_scalar(hi[:, :], hi[:, :], ROUND, None, ALU.add))
                        link(nc.vector.tensor_scalar(hi[:, :], hi[:, :], ROUND, None, ALU.subtract))
                        link(nc.vector.scalar_tensor_tensor(lo[:, :], hi[:, :], -float(P), sf, ALU.mult, ALU.add))
                        if ch:
                            dve.wait_ge(s["g_inv"], ch)
                        K = SLOT_TILES
                        nc.vector.tensor_tensor(lo1[:, :, :], count[:, :].unsqueeze(1).to_broadcast([P, N, P]),
                                                lo[:, :].unsqueeze(2).to_broadcast([P, N, P]), ALU.is_equal)
                        tt(hi1[:, :, K:2 * K], count[:, 0:K].unsqueeze(1).to_broadcast([P, N, K]),
                           hi[:, :].unsqueeze(2).to_broadcast([P, N, K]), ALU.is_equal)
                        tt(hi1[:, :, 0:K], hi1[:, :, K:2 * K], tnum[:, :].unsqueeze(2).to_broadcast([P, N, K]),
                           ALU.mult)
                        nc.vector.tensor_scalar(hi1[:, :, K:2 * K], hi1[:, :, K:2 * K], row[:, 0:1], None,
                                                ALU.mult).then_inc(s["g_onehot"], 1)
                    dve.wait_ge(s["g_inv"], 2)
                    link(nc.vector.tensor_scalar(ownf[:, :], ps_inv[:, 0:SLOT_TILES], float(P), None, ALU.mult))
                    nc.vector.tensor_tensor(source[:, :], ps_inv[:, SLOT_TILES:2 * SLOT_TILES], ownf[:, :],
                                            ALU.add).then_inc(s["e_small"], 1)

        slot_tiles(nc, S, c, dict(
            h_rows=h_rows, y_rows=y_rows, w_hi=w_hi, w_lo=w_lo, wo_hi=wo_hi, wo_lo=wo_lo, bias3=bias3, ones3=ones3,
            bo=bo, owner=owner, source=source, tiles=SLOT_TILES, wcols=WCOLS, fc=FC))
        combine(nc, S, c, out, y_rows, share, slot)


def slot_tiles(nc, S, c0, G):
    ident = S["ident"]
    n_tiles, FC = G["tiles"], G["fc"]
    with ExitStack() as c:
        def sb(name, shape, dt=F32):
            return S["sb"](name, shape, dt, c)

        index = [sb(f"index{u}", [P, 1], U32) for u in range(2)]
        x = [sb(f"x_rows{u}", [P, DIM]) for u in range(2)]
        xT_hi, xT_lo = sb("xT_hi", [P, DIM], BF16), sb("xT_lo", [P, DIM], BF16)
        sig = sb("sig", [P, FF])
        g = sb("g", [P, FF])
        gT_hi, gT_lo = sb("gT_hi", [P, FF], BF16), sb("gT_lo", [P, FF], BF16)
        y = [sb(f"y{u}", [P, DIM]) for u in range(2)]
        ps_x = S["ps"]("ps_ex", [P, DIM], F32, c)
        ps_a = S["ps"]("ps_ea", [P, FF], F32, c)
        ps_b = S["ps"]("ps_eb", [P, FF], F32, c)
        ps_g = S["ps"]("ps_eg", [P, FF], F32, c)
        ps_y = S["ps"]("ps_ey", [P, DIM], F32, c)
        s = {n: S["sem"](n) for n in (
            "m_index", "m_x_in0", "m_x_in1", "m_xT_done", "m_xT_hi", "m_xT_lo", "m_up_b", "m_up", "m_sig", "m_g", "m_gT_done",
            "m_gT_hi", "m_gT_lo", "m_down", "m_y", "m_y_out0", "m_y_out1")}

        with nc.Block() as block:

            @block.gpsimd
            def _(pool):
                def step(i, u, pair):
                    wait(pool, s[f"m_x_in{u}"], 16 * pair)
                    nc.gpsimd.tensor_copy(index[u][:, :], G["source"][:, bass.ds(i, 1)]).then_inc(s["m_index"], 1)
                    wait(pool, s["m_index"], i + 1)
                    wait_apart(pool, s["m_xT_done"], i - 1)
                    nc.gpsimd.indirect_dma_start(x[u][:, :], None, G["h_rows"],
                                                 bass.IndirectOffsetOnAxis(ap=index[u][:, :], axis=0)
                                                 ).then_inc(s[f"m_x_in{u}"], 16)

                in_pairs(pool, step, n_tiles)

            @block.sync
            def _(sp):
                def step(i, u, pair):
                    wait(sp, s["m_y"], i + 1)
                    sp.dma_start(G["y_rows"][bass.ts(i, P), :], y[u][:, :]).then_inc(s[f"m_y_out{u}"], 16)

                in_pairs(sp, step, n_tiles)
                for u in range(2):
                    sp.wait_ge(s[f"m_y_out{u}"], 16 * (n_tiles // 2))

            @block.scalar
            def _(act):
                def high(i):
                    wait(act, s["m_xT_done"], i + 1)
                    wait(act, s["m_up"], i)
                    nc.scalar.copy(xT_hi[:, :], ps_x[:, :]).then_inc(s["m_xT_hi"], 1)

                def step(i, u, pair):
                    wait(act, s["m_up_b"], i + 1)
                    wait(act, s["m_g"], i)
                    nc.scalar.activation(sig[:, :], ps_b[:, :], ACT.Sigmoid).then_inc(s["m_sig"], 1)
                    if on(i + 1, n_tiles):
                        high(i + 1)
                    wait(act, s["m_gT_done"], i + 1)
                    wait(act, s["m_down"], i)
                    nc.scalar.copy(gT_hi[:, :], ps_g[:, :]).then_inc(s["m_gT_hi"], 1)

                high(0)
                in_pairs(act, step, n_tiles)

            @block.vector
            def _(dve):
                def low(i):
                    wait(dve, s["m_xT_hi"], i + 1)
                    nc.vector.tensor_tensor(xT_lo[:, :], ps_x[:, :], xT_hi[:, :],
                                            ALU.subtract).then_inc(s["m_xT_lo"], 1)

                def finish(i, u, pair):
                    wait(dve, s["m_down"], i + 1)
                    wait(dve, s[f"m_y_out{u}"], 16 * pair)
                    nc.vector.tensor_tensor(y[u][:, :], ps_y[:, :], G["bo"][:, :], ALU.add).then_inc(s["m_y"], 1)

                def step(i, u, pair):
                    wait(dve, s["m_sig"], i + 1)
                    wait(dve, s["m_up"], i + 1)
                    wait(dve, s["m_gT_done"], i)
                    nc.vector.tensor_tensor(g[:, :], ps_a[:, :], sig[:, :], ALU.mult).then_inc(s["m_g"], 1)
                    if on(i + 1, n_tiles):
                        low(i + 1)
                    if on(i - 1, n_tiles):
                        finish(i - 1, 1 - u, pair - 1 if u == 0 else pair)
                    wait(dve, s["m_gT_hi"], i + 1)
                    nc.vector.tensor_tensor(gT_lo[:, :], ps_g[:, :], gT_hi[:, :],
                                            ALU.subtract).then_inc(s["m_gT_lo"], 1)

                low(0)
                in_pairs(dve, step, n_tiles)
                finish(n_tiles - 1, 1, n_tiles // 2 - 1)

            @block.tensor
            def _(pe):
                def transposes(i, u, pair):
                    wait(pe, s[f"m_x_in{u}"], 16 * (pair + 1))
                    wait(pe, s["m_xT_lo"], i)
                    for k in range(DC):
                        ins = nc.tensor.transpose(ps_x[:, k * P:(k + 1) * P], x[u][:, k * P:(k + 1) * P], ident[:, :])
                    ins.then_inc(s["m_xT_done"], 1)

                def down(i):
                    wait(pe, s["m_gT_hi"], i + 1)
                    wait(pe, s["m_gT_lo"], i + 1)
                    wait(pe, s["m_y"], i)
                    split_matmul(nc, ps_y[:, :],
                                 [(gT_hi[:, k * P:(k + 1) * P], gT_lo[:, k * P:(k + 1) * P]) for k in range(FC)],
                                 [(G["wo_hi"][:, k * DIM:(k + 1) * DIM], G["wo_lo"][:, k * DIM:(k + 1) * DIM])
                                  for k in range(FC)]).then_inc(s["m_down"], 1)

                def step(i, u, pair):
                    e = pe.value_load(G["owner"][0:1, bass.ds(i, 1)], min_val=0, max_val=EXPERTS - 1)
                    wait(pe, s["m_xT_hi"], i + 1)
                    wait(pe, s["m_xT_lo"], i + 1)
                    wait(pe, s["m_g"], i)
                    xx = [(xT_hi[:, k * P:(k + 1) * P], xT_lo[:, k * P:(k + 1) * P]) for k in range(DC)]
                    for half, dst in ((1, ps_b), (0, ps_a)):
                        ww = []
                        for k in range(DC):
                            off = k * 2 * FF + half * FF
                            ww.append(tuple(w[:, bass.ds(e, 1), off:off + FF].rearrange("p a n -> p (a n)")
                                            for w in (G["w_hi"], G["w_lo"])))
                        split_matmul(nc, dst[:, :], xx, ww, last=False)
                        ins = nc.tensor.matmul(dst[:, :], G["ones3"][:, :],
                                               G["bias3"][:, bass.ds(e * (2 * FF) + half * FF, FF)],
                                               start=False, stop=True)
                        ins.then_inc(s["m_up_b" if half else "m_up"], 1)
                    if on(i + 1, n_tiles):
                        transposes(i + 1, 1 - u, pair if u == 0 else pair + 1)
                    if on(i - 1, n_tiles):
                        down(i - 1)
                    wait(pe, s["m_g"], i + 1)
                    wait(pe, s["m_gT_lo"], i)
                    for k in range(FC):
                        ins = nc.tensor.transpose(ps_g[:, k * P:(k + 1) * P], g[:, k * P:(k + 1) * P], ident[:, :])
                    ins.then_inc(s["m_gT_done"], 1)

                transposes(0, 0, 0)
                in_pairs(pe, step, n_tiles)
                down(n_tiles - 1)


def combine(nc, S, c0, out, y_rows, share, slot):
    h, bn, mv, rstd, neg_half = S["h"], S["bn"], S["mv"], S["rstd"], S["neg_half"]
    N = TILES
    with ExitStack() as c:
        def sb(name, shape, dt=F32):
            return S["sb"](name, shape, dt, c)

        index = [[sb(f"cindex{ch}{u}", [P, 1], U32) for u in range(2)] for ch in range(2)]
        y = [[sb(f"cy{ch}{u}", [P, DIM]) for u in range(2)] for ch in range(2)]
        mixed = [sb(f"mixed{u}", [P, DIM]) for u in range(2)]
        final = [sb(f"final{u}", [P, DIM]) for u in range(2)]
        s = {n: S["sem"](n) for n in (
            "c_index", "c_y_in0", "c_y_in1", "c_half", "c_mixed", "c_bn", "c_var", "c_rstd", "c_final",
            "c_out0", "c_out1")}

        with nc.Block() as block:

            @block.gpsimd
            def _(pool):
                def step(t, u, pair):
                    wait(pool, s[f"c_y_in{u}"], 32 * pair)
                    for ch in range(2):
                        ins = nc.gpsimd.tensor_copy(index[ch][u][:, :], slot[ch][:, bass.ds(t, 1)])
                    ins.then_inc(s["c_index"], 1)
                    wait(pool, s["c_index"], t + 1)
                    wait_apart(pool, s["c_mixed"], t - 1)
                    for ch in range(2):
                        nc.gpsimd.indirect_dma_start(y[ch][u][:, :], None, y_rows,
                                                     bass.IndirectOffsetOnAxis(ap=index[ch][u][:, :], axis=0)
                                                     ).then_inc(s[f"c_y_in{u}"], 16)
                    if on(t - 1, N):
                        root(t - 1)

                def root(t):
                    wait(pool, s["c_var"], t + 1)
                    wait_apart(pool, s["c_final"], t)
                    nc.gpsimd.tensor_scalar(rstd[:, :], mv[:, 1:2], EPS, None, ALU.add).then_inc(s["c_rstd"], 1)
                    wait(pool, s["c_rstd"], 2 * t + 1)
                    nc.gpsimd.tensor_tensor(rstd[:, :], rstd[:, :], neg_half[:, :], ALU.pow).then_inc(s["c_rstd"], 1)

                in_pairs(pool, step, N)
                root(N - 1)

            @block.vector
            def _(dve):
                def step(t, u, pair):
                    wait(dve, s[f"c_y_in{u}"], 32 * (pair + 1))
                    nc.vector.scalar_tensor_tensor(mixed[u][:, :], y[0][u][:, :], share[0][:, bass.ds(t, 1)],
                                                   h[:, t, :], ALU.mult, ALU.add).then_inc(s["c_half"], 1)
                    wait(dve, s["c_half"], t + 1)
                    nc.vector.scalar_tensor_tensor(mixed[u][:, :], y[1][u][:, :], share[1][:, bass.ds(t, 1)],
                                                   mixed[u][:, :], ALU.mult, ALU.add).then_inc(s["c_mixed"], 1)
                    wait(dve, s["c_mixed"], t + 1)
                    if on(t - 1, N):
                        finish(t - 1, 1 - u, pair - 1 if u == 0 else pair)
                    nc.vector.bn_stats(bn[:, :], mixed[u][:, :]).then_inc(s["c_bn"], 1)
                    wait_apart(dve, s["c_bn"], t + 1)
                    nc.vector.bn_aggr(mv[:, :], bn[:, :]).then_inc(s["c_var"], 1)

                def finish(t, u, pair):
                    wait(dve, s["c_rstd"], 2 * t + 2)
                    wait(dve, s[f"c_out{u}"], 16 * pair)
                    nc.vector.tensor_scalar(final[u][:, :], mixed[u][:, :], mv[:, 0:1], rstd[:, 0:1],
                                            ALU.subtract, ALU.mult).then_inc(s["c_final"], 1)

                in_pairs(dve, step, N)
                finish(N - 1, 1, N // 2 - 1)

            @block.sync
            def _(sp):
                def step(t, u, pair):
                    wait(sp, s["c_final"], t + 1)
                    sp.dma_start(out[bass.ts(t, P), :], final[u][:, :]).then_inc(s[f"c_out{u}"], 16)

                in_pairs(sp, step, N)
                for u in range(2):
                    sp.wait_ge(s[f"c_out{u}"], 16 * (N // 2))


def _rows(w, chunks):
    n = w.shape[1]
    return np.ascontiguousarray(w.reshape(chunks, P, n).transpose(1, 0, 2).reshape(P, chunks * n))


def _tables():
    grid = np.stack(np.meshgrid(np.arange(8), np.arange(8), indexing="ij"))
    q = DIM // 4
    factor = np.float32(10000.0) ** (np.arange(q, dtype=np.float32) / np.float32(q))
    a = grid[0].reshape(-1).astype(np.float32)[:, None] / factor
    b = grid[1].reshape(-1).astype(np.float32)[:, None] / factor
    pos = np.concatenate([np.sin(a), np.cos(a), np.sin(b), np.cos(b)], -1).astype(np.float32)
    inv = np.float32(1000.0) ** (np.float32(-2.0) * np.arange(DK0 // 2, dtype=np.float32) / np.float32(DK0))
    ang = (np.arange(TOK, dtype=np.float32)[:, None] * inv[None]).astype(np.float32)
    cos, sin = np.cos(ang), np.sin(ang)
    rc = np.repeat(cos, 2, axis=1)
    rs = np.stack([-sin, sin], -1).reshape(TOK, DK0)
    causal = np.where(np.tril(np.ones((TOK, TOK), bool)), 0.0, MASKED).astype(np.float32)
    order = np.array([(tk * HEADS1 + hd) for hd in range(HEADS1) for tk in range(4)])
    causal1 = causal[np.ix_(order, order)]
    return {
        "ident": np.eye(P, dtype=np.float32),
        "pos": np.tile(pos, (2, 1)),
        "rope_c": np.tile(rc, (2, 2 * HEADS0)).astype(np.float32),
        "rope_s": np.tile(rs, (2, 2 * HEADS0)).astype(np.float32),
        "lower": np.triu(np.ones((P, P)), 1).astype(np.float32),
        "count": np.tile(np.arange(P, dtype=np.float32)[None], (P, 1)),
        "row": np.arange(P, dtype=np.float32)[:, None],
        "rank": np.tile(EXPERTS - np.arange(EXPERTS, dtype=np.float32)[None], (P, 1)),
        "tnum": np.tile(np.arange(TILES, dtype=np.float32)[None], (P, 1)),
        "mask0": np.tile(causal, (2, 4)),
        "mask1": np.tile(causal1, (2, 8)),
    }


def _layout(i):
    x = i["x"].reshape(IMAGES, 3, 8, 16, 8, 16).transpose(0, 2, 4, 3, 5, 1).reshape(TOKENS, PATCH)
    a = {
        "patches": np.ascontiguousarray(
            x.reshape(TILES, P, PC, P).transpose(3, 0, 2, 1).reshape(P, TILES, PC * P)),
        "wp": _rows(i["L0_tok_Wp"].T, PC),
        "tok_b": np.tile(i["L0_tok_b"][None], (P, 1)),
        "wqkv": _rows(np.concatenate([i["L0_attn_wq"].T, i["L0_attn_wk"].T,
                                      i["L0_attn_wv"].T.reshape(DIM, 2, 2, 4, DK0)
                                      .transpose(0, 2, 3, 1, 4).reshape(DIM, DIM)], 1), DC),
        "wo": _rows(i["L0_attn_wo"].T, DC),
        "w1": _rows(i["L0_ffn_w1"].T, DC),
        "b1": np.ascontiguousarray(i["L0_ffn_b1"].reshape(HC, P).T),
        "w2": _rows(i["L0_ffn_w2"].T, HC),
        "wqkv1": _rows(np.concatenate([i["L1_attn_" + n].transpose(1, 0, 2).reshape(DIM, HEADS1 * DK1)
                                       for n in ("Wq", "Wk", "Wv")], 1), DC),
        "wp1": _rows(i["L1_attn_proj_w"].T, HEADS1 * DK1 // P),
        "bp": np.tile(i["L1_attn_proj_b"][None], (P, 1)),
        "we": np.ascontiguousarray(i["L1_ffn_W1"].transpose(0, 2, 1).reshape(EXPERTS, DC, P, 2 * FF)
                                   .transpose(2, 0, 1, 3).reshape(P, EXPERTS, DC * 2 * FF)),
        "be": np.ascontiguousarray(i["L1_ffn_b1"].reshape(P, EXPERTS * 2 * FF // P)),
        "wg": _rows(i["L1_ffn_Wg"].T, DC),
        "wo2": _rows(i["L1_ffn_Wo"].T, FF // P),
        "bo": np.tile(i["L1_ffn_bo"][None], (P, 1)),
        "b2": np.tile(i["L0_ffn_b2"][None], (P, 1)),
    }
    t = _tables()
    a.update(t)
    return a


def kernel(**inputs):
    import concourse.bacc as bacc
    from concourse.bass_utils import run_bass_kernel_spmd

    nc = bacc.Bacc("TRN2", target_bir_lowering=False, num_devices=1)
    arrays = _layout({k: np.asarray(v) for k, v in inputs.items()})
    aps = {n: nc.dram_tensor(n + "_in", a.shape, mybir.dt.from_np(a.dtype), kind="ExternalInput").ap()
           for n, a in arrays.items()}
    out = nc.dram_tensor("tower_out", (TOKENS, DIM), F32, kind="ExternalOutput").ap()
    build(nc, aps, out)
    r = run_bass_kernel_spmd(nc, [{n + "_in": a for n, a in arrays.items()}], core_ids=[0])
    return r.results[0]["tower_out"].reshape(IMAGES, TOK, DIM)
```

```python
from contextlib import ExitStack

import numpy as np
import concourse.bass as bass
from concourse import mybir

F32 = mybir.dt.float32
BF16 = mybir.dt.bfloat16
U32 = mybir.dt.uint32
ALU = mybir.AluOpType
ACT = mybir.ActivationFunctionType
AX = mybir.AxisListType

P = 128
IMAGES, TOK, DIM = 64, 64, 256
TOKENS = IMAGES * TOK
TILES = TOKENS // P
PATCH = 768
PC = PATCH // P
DC = DIM // P
HEADS0, DK0 = 16, 16
SLOT = 32
PAIRS = HEADS0 // 2
VW = DK0 + 1
HID = 1024
HC = HID // P
HEADS1, DK1 = 16, 64
EXPERTS, FF = 8, 512
ROUND = 12582912.0
MASKED = -1.0e30
CONSTANTS = 6
EPS = 1e-5


def on(t, n):
    return not isinstance(t, int) or 0 <= t < n


def wait(eng, sem, value):
    if not isinstance(value, int) or value > 0:
        eng.wait_ge(sem, value)


def wait_apart(eng, sem, value):
    wait(eng, sem, value)
    eng.nop(nofuse=True)


def in_pairs(eng, step, n, apart=4):
    for t in range(apart):
        step(t, t % 2, t // 2)
    with eng.Fori(apart // 2, n // 2 - 1) as pair:
        step(2 * pair, 0, pair)
        step(2 * pair + 1, 1, pair)
    for t in (n - 2, n - 1):
        step(t, t % 2, n // 2 - 1)


def split_matmul(nc, out, stat, mov, first=True, last=True):
    n = len(stat)
    for k in range(n):
        (sh, sl), (mh, ml) = stat[k], mov[k]
        nc.tensor.matmul(out, sh, mh, start=first and k == 0, stop=False)
        nc.tensor.matmul(out, sh, ml, start=False, stop=False)
        ins = nc.tensor.matmul(out, sl, mh, start=False, stop=last and k == n - 1)
    return ins


def build(nc, A, out, upto=9):
    ctx = ExitStack()
    with ctx:
        def sb(name, shape, dt=F32, c=None):
            return (c or ctx).enter_context(nc.sbuf_tensor(name, shape, dt))

        def ps(name, shape, dt=F32, c=None):
            return (c or ctx).enter_context(nc.psum_tensor(name, shape, dt))

        def sem(name):
            return ctx.enter_context(nc.semaphore(name))

        h = sb("h", [P, TILES, DIM])
        ident = sb("ident", [P, P])
        ident_bf = sb("ident_bf", [P, P], BF16)
        bn = sb("bn", [P, 6])
        mv = sb("mv", [P, 2])
        rstd = sb("rstd", [P, 1])
        neg_half = sb("neg_half", [P, 1])
        S = dict(sb=sb, ps=ps, sem=sem, h=h, ident=ident, ident_bf=ident_bf,
                 bn=bn, mv=mv, rstd=rstd, neg_half=neg_half)
        with ExitStack() as mlp:
            S.update(w1q=sb("w1q", [P, DC, HID], BF16, mlp), w2q=sb("w2q", [P, HC, DIM], BF16, mlp),
                     b1=sb("b1", [P, HC], F32, mlp), b2=sb("b2", [P, DIM], F32, mlp),
                     amax=sb("amax", [P, TILES], F32, mlp),
                     wscale=sb("wscale", [P, 2], F32, mlp))
            embed_and_rotary_attention(nc, A, S)
            if upto >= 2:
                quantised_mlp(nc, A, S)
        if upto >= 3:
            S["h_rows"] = nc.dram_tensor("h_rows", (TOKENS, DIM), F32, kind="Internal").ap()
            S.update(wg=sb("wg", [P, DC * EXPERTS]), logit=sb("logit", [P, TILES, EXPERTS]),
                     lower_f=sb("lower_f", [P, P]), b1f=sb("b1f", [P, 64]), count=sb("count", [P, P]),
                     row=sb("row", [P, 1]), rank=sb("rank", [P, EXPERTS]), tnum=sb("tnum", [P, 2, TILES]))
            S["gate_consts"] = [(S["lower_f"], "lower"), (S["b1f"], "be"), (S["count"], "count"),
                                (S["row"], "row"), (S["rank"], "rank"), (S["tnum"], "tnum")]
            cross_head_attention(nc, A, S)
        if upto >= 4:
            experts(nc, A, S, out)
        else:
            store_h(nc, S, out)


def store_h(nc, S, out):
    stored = S["sem"]("stored")
    with nc.Block() as block:
        @block.sync
        def _(sp):
            sp.dma_start(out.rearrange("(t p) d -> p t d", p=P), S["h"][:, :, :]).then_inc(stored, 16)
            sp.wait_ge(stored, 16)


def embed_and_rotary_attention(nc, A, S):
    h, ident, ident_bf = S["h"], S["ident"], S["ident_bf"]
    bn, mv, rstd, neg_half, amax = S["bn"], S["mv"], S["rstd"], S["neg_half"], S["amax"]
    sem = S["sem"]
    N = TILES
    PT = N // 4
    FIRST = 2
    with ExitStack() as c:
        def sb(name, shape, dt=F32):
            return S["sb"](name, shape, dt, c)

        def ps(name, shape, dt=F32):
            return S["ps"](name, shape, dt, c)

        patches = sb("patches", [P, 2 * PT, PC * P])
        whole = {}
        parts = {}
        for name, n in (("wp", PC * DIM), ("wqkv", DC * 3 * DIM), ("wo", DC * DIM)):
            whole[name] = sb(name, [P, n])
            parts[name] = (sb(name + "_hi", [P, n], BF16), sb(name + "_lo", [P, n], BF16))
        w1f = sb("w1f", [P, DC * HID])
        w2f = sb("w2f", [P, HC * DIM])
        posb = sb("posb", [P, DIM])
        tokb = sb("tokb", [P, DIM])
        rope_c = sb("rope_c", [P, 2 * DIM])
        rope_s = sb("rope_s", [P, 2 * DIM])
        mask = sb("mask", [P, DIM], BF16)
        mask_f = sb("mask_f", [P, DIM])
        wmax = sb("wmax", [P, 2])
        wall = sb("wall", [P, 2])
        winv = sb("winv", [P, 2])
        fresh = sb("fresh", [P, DIM])
        x_hi = sb("x_hi", [P, PC * P], BF16)
        x_lo = sb("x_lo", [P, PC * P], BF16)
        hT_hi = sb("hT_hi", [P, DC * P], BF16)
        hT_lo = sb("hT_lo", [P, DC * P], BF16)
        rot_a = sb("rot_a", [P, 2 * DIM])
        rot_b = sb("rot_b", [P, 2 * DIM])
        slots = sb("slots", [P, 3 * DIM])
        qkT = sb("qkT", [P, 6, P])
        vpair = [[sb(f"vpair{par}{b}", [P, PAIRS, 2 * VW]) for b in range(2)] for par in range(2)]
        top = sb("top", [P, HEADS0])
        shifted = sb("shifted", [P, HEADS0 * TOK])
        probs = sb("probs", [P, HEADS0 * TOK])
        probsT = sb("probsT", [P, PAIRS, P])
        rsum = sb("rsum", [P, HEADS0])
        att = sb("att", [P, DIM])
        aT_hi = sb("aT_hi", [P, DC * P], BF16)
        aT_lo = sb("aT_lo", [P, DC * P], BF16)

        ps_tr = ps("ps_tr", [P, 2 * DIM])
        tr, emb = ps_tr[:, 0:DIM], ps_tr[:, DIM:2 * DIM]
        ps_t = ps("ps_t", [P, 1024])
        out0 = ps_t[:, 512:512 + DIM]
        ps_sc = ps("ps_sc", [P, 1024])
        ps_s = ps_sc[:, :].rearrange("p (bank half n) -> p bank half n", bank=2, half=2)
        ps_p = ps("ps_p", [P, 4, DIM])
        ps_qk, ps_v = ps_p[:, 0:2, :], ps_p[:, 2:4, 0:P]
        ps_qkT = ps_p[:, 0:3, :].rearrange("p a b -> p (a b)")
        ps_o = ps("ps_o", [P, HEADS0 * VW])

        consts_in, weights_in = sem("consts_in"), sem("weights_in")
        first_in, mlp_in = sem("first_in"), sem("mlp_in")
        patches_in = [sem(f"patches_in{n}") for n in range(4)]
        w_hi, w_lo, setup_dve, setup_pool = sem("w_hi"), sem("w_lo"), sem("setup_dve"), sem("setup_pool")
        wmax_ready, wall_ready, wq_round = sem("wmax_ready"), sem("wall_ready"), sem("wq_round")
        x_split = sem("x_split")
        emb_done, h0_saved, h0_ready = sem("emb_done"), sem("h0_saved"), sem("h0_ready")
        hT_done, hT_hi_ready, hT_lo_ready = sem("hT_done"), sem("hT_hi_ready"), sem("hT_lo_ready")
        qk_done, v_done = sem("qk_done"), sem("v_done")
        rot_parts, rotated, v_ready = sem("rot_parts"), sem("rotated"), sem("v_ready")
        qkT_done, qkT_ready = sem("qkT_done"), sem("qkT_ready")
        half_scores = sem("half_scores")
        scores_done, shift_ready, probs_ready = sem("scores_done"), sem("shift_ready"), sem("probs_ready")
        pT_done, pT_a_ready, pT_b_ready, pv_done = (
            sem("pT_done"), sem("pT_a_ready"), sem("pT_b_ready"), sem("pv_done"))
        att_ready = sem("att_ready")
        aT_done, aT_hi_ready, aT_lo_ready = sem("aT_done"), sem("aT_hi_ready"), sem("aT_lo_ready")
        wo_done, res_ready, var_ready = sem("wo_done"), sem("res_ready"), sem("var_ready")
        rstd_ready, ln_ready = sem("rstd_ready"), sem("ln_ready")

        def chunks(pair, n, k0=0):
            hi, lo = pair
            return lambda a, b: [(hi[:, k * n + a:k * n + b], lo[:, k * n + a:k * n + b])
                                 for k in range(hi.shape[1] // n)]

        def both(hi, lo, n, a=0, b=P):
            return [(hi[:, k * n + a:k * n + b], lo[:, k * n + a:k * n + b])
                    for k in range(hi.shape[1] // n)]

        wp_k = chunks(parts["wp"], DIM)(0, DIM)
        wqkv = chunks(parts["wqkv"], 3 * DIM)
        wo_k = chunks(parts["wo"], DIM)(0, DIM)

        with nc.Block() as block:

            @block.sync
            def _(sp):
                sp.dma_start(whole["wp"][:, :], A["wp"]).then_inc(weights_in, 16)
                sp.dma_start(patches[:, 0:FIRST, :], A["patches"][:, 0:FIRST, :]).then_inc(first_in, 16)
                for name in ("wqkv", "wo"):
                    sp.dma_start(whole[name][:, :], A[name]).then_inc(weights_in, 16)
                sp.wait_ge(weights_in, 48)
                sp.wait_ge(consts_in, 16 * CONSTANTS)
                for part in range(4):
                    if part >= 2:
                        sp.wait_ge(x_split, 2 * (part - 1) * PT)
                    place = part % 2 * PT
                    skip = FIRST if part == 0 else 0
                    sp.dma_start(patches[:, place + skip:place + PT, :],
                                 A["patches"][:, part * PT + skip:(part + 1) * PT, :]
                                 ).then_inc(patches_in[part], 16)
                    if part == 0:
                        for dst, name in ((w1f, "w1"), (w2f, "w2"), (S["b1"], "b1"), (S["b2"], "b2")):
                            sp.dma_start(dst[:, :], A[name]).then_inc(mlp_in, 16)

            @block.scalar
            def _(act):
                for dst, name in ((ident, "ident"), (posb, "pos"), (tokb, "tok_b"), (rope_c, "rope_c"),
                                  (rope_s, "rope_s"), (mask_f, "mask0")):
                    act.dma_start(dst[:, :], A[name]).then_inc(consts_in, 16)
                act.wait_ge(weights_in, 48)
                for name in ("wp", "wqkv", "wo"):
                    nc.scalar.copy(parts[name][0][:, :], whole[name][:, :]).then_inc(w_hi, 1)
                act.wait_ge(consts_in, 16 * CONSTANTS)
                nc.scalar.copy(mask[:, :], mask_f[:, :])
                nc.scalar.copy(ident_bf[:, :], ident[:, :]).then_inc(w_hi, 1)

                def body(t, par, _):
                    if on(t - 2, N):
                        wait(act, aT_done, t - 1)
                        wait(act, wo_done, t - 2)
                        nc.scalar.copy(aT_hi[:, :], ps_t[:, 0:DIM]).then_inc(aT_hi_ready, 1)
                    if on(t, N):
                        wait(act, hT_done, t + 1)
                        wait(act, v_done, t)
                        nc.scalar.copy(hT_hi[:, :], tr[:, :]).then_inc(hT_hi_ready, 1)
                    if on(t - 1, N):
                        wait(act, shift_ready, 2 * t)
                        wait(act, pT_done, t - 1)
                        nc.scalar.activation(probs[:, :], shifted[:, :], ACT.Exp,
                                             scale=float(DK0) ** -0.5).then_inc(probs_ready, 1)
                    if on(t, N):
                        wait(act, v_done, t + 1)
                        if on(t - 2, N):
                            wait(act, pv_done, t - 1)
                        for b in range(2):
                            for half in range(2):
                                q = slice(64 * half, 64 * half + 64)
                                ins = nc.scalar.copy(vpair[par][b][q, :, half * VW:half * VW + DK0],
                                                     ps_v[q, b, :].rearrange("p (pr d) -> p pr d", d=DK0))
                        ins.then_inc(v_ready, 1)
                    if on(t - 1, N):
                        wait(act, pT_done, t)
                        wait(act, pv_done, t - 1)
                        nc.scalar.copy(probsT[:, 0:4, :].rearrange("p a b -> p (a b)"),
                                       ps_t[:, 0:512]).then_inc(pT_a_ready, 1)
                    if on(t, N):
                        wait(act, qkT_done, t + 1)
                        wait(act, scores_done, t)
                        nc.scalar.copy(qkT[:, :, :].rearrange("p a b -> p (a b)"),
                                       ps_qkT).then_inc(qkT_ready, 1)

                in_pairs(act, body, N)
                body(N, 0, 0)
                body(N + 1, 1, 0)

            @block.gpsimd
            def _(pool):
                nc.gpsimd.memset(neg_half[:, :], -0.5)
                for tile in range(2):
                    for b in range(2):
                        nc.gpsimd.memset(vpair[tile][b][:, :, :], 0.0)
                nc.gpsimd.memset(slots[:, :], 0.0).then_inc(setup_pool, 1)
                pool.wait_ge(setup_pool, 1)
                n = 1
                for tile in range(2):
                    for b in range(2):
                        for half in range(2):
                            col = half * VW + DK0
                            nc.gpsimd.memset(vpair[tile][b][64 * half:64 * half + 64, :, col:col + 1],
                                             1.0).then_inc(setup_pool, 1)
                            n += 1
                            pool.wait_ge(setup_pool, n)

                def split(t, part):
                    src = patches[:, t - (part - part % 2) * PT, :]
                    wait(pool, emb_done, t)
                    nc.gpsimd.tensor_copy(x_hi[:, :], src).then_inc(x_split, 1)
                    wait_apart(pool, x_split, 2 * t + 1)
                    nc.gpsimd.tensor_tensor(x_lo[:, :], src, x_hi[:, :],
                                            ALU.subtract).then_inc(x_split, 1)

                def save(t):
                    wait(pool, h0_ready, t + 1)
                    nc.gpsimd.tensor_copy(h[:, t, :], fresh[:, :]).then_inc(h0_saved, 1)

                def norm(t):
                    wait(pool, var_ready, 2 * t + 2)
                    wait_apart(pool, ln_ready, t)
                    nc.gpsimd.tensor_scalar(rstd[:, :], mv[:, 1:2], EPS, None, ALU.add).then_inc(rstd_ready, 1)
                    wait(pool, rstd_ready, 2 * t + 1)
                    nc.gpsimd.tensor_tensor(rstd[:, :], rstd[:, :], neg_half[:, :],
                                            ALU.pow).then_inc(rstd_ready, 1)

                pool.wait_ge(first_in, 16)
                for t in range(FIRST):
                    split(t, 0)
                    save(t)
                for part in range(4):
                    pool.wait_ge(patches_in[part], 16)
                    if part == 0:
                        for t in range(FIRST, 4):
                            split(t, 0)
                            save(t)
                            if t == 3:
                                pool.wait_ge(wmax_ready, 2)
                                nc.gpsimd.partition_all_reduce(wall[:, :], wmax[:, :], P,
                                                               bass.bass_isa.ReduceOp.max
                                                               ).then_inc(wall_ready, 1)
                                norm(0)
                    with pool.Fori(max(4, part * PT), (part + 1) * PT) as t:
                        split(t, part)
                        save(t)
                        norm(t - 3)
                for t in (N - 3, N - 2, N - 1):
                    norm(t)

            @block.vector
            def _(dve):
                dve.wait_ge(weights_in, 48)
                for n, name in enumerate(("wp", "wqkv", "wo")):
                    dve.wait_ge(w_hi, n + 1)
                    nc.vector.tensor_tensor(parts[name][1][:, :], whole[name][:, :], parts[name][0][:, :],
                                            ALU.subtract).then_inc(w_lo, 1)
                dve.wait_ge(consts_in, 16 * CONSTANTS)
                nc.vector.tensor_tensor(posb[:, :], posb[:, :], tokb[:, :], ALU.add).then_inc(setup_dve, 1)

                def largest(n):
                    nc.vector.tensor_reduce(wmax[:, n:n + 1], (w1f, w2f)[n][:, :], AX.X, ALU.max,
                                            apply_absolute_value=True).then_inc(wmax_ready, 1)

                def scales():
                    dve.wait_ge(wall_ready, 1)
                    nc.vector.tensor_scalar(S["wscale"][:, :], wall[:, :], 1e-6, 1.0 / 127.0,
                                            ALU.max, ALU.mult).then_inc(setup_dve, 1)
                    dve.wait_ge(setup_dve, 2)
                    nc.vector.reciprocal(winv[:, :], S["wscale"][:, :]).then_inc(setup_dve, 1)
                    dve.wait_ge(setup_dve, 3)

                def quantise(n):
                    w, q = ((w1f, S["w1q"]), (w2f, S["w2q"]))[n]
                    nc.vector.tensor_scalar(w[:, :], w[:, :], winv[:, n:n + 1], ROUND,
                                            ALU.mult, ALU.add).then_inc(wq_round, 1)
                    dve.wait_ge(wq_round, n + 1)
                    nc.vector.tensor_scalar(q[:, :, :].rearrange("p a b -> p (a b)"), w[:, :], ROUND, None,
                                            ALU.subtract).then_inc(setup_dve, 1)

                def embedded(t):
                    wait(dve, emb_done, t + 1)
                    wait(dve, h0_saved, t)
                    wait(dve, hT_done, t)
                    nc.vector.tensor_tensor(fresh[:, :], emb, posb[:, :], ALU.add).then_inc(h0_ready, 1)

                def normalise(t):
                    wait(dve, rstd_ready, 2 * t + 2)
                    nc.vector.tensor_scalar(h[:, t, :], h[:, t, :], mv[:, 0:1], rstd[:, 0:1],
                                            ALU.subtract, ALU.mult).then_inc(ln_ready, 1)
                    wait(dve, ln_ready, t + 1)
                    nc.vector.tensor_reduce(amax[:, bass.ds(t, 1)] if not isinstance(t, int) else amax[:, t:t + 1],
                                            h[:, t, :], AX.X, ALU.max,
                                            apply_absolute_value=True)

                def body(t, par, _):
                    if on(t - 2, N):
                        wait(dve, aT_hi_ready, t - 1)
                        wait(dve, wo_done, t - 2)
                        nc.vector.tensor_tensor(aT_lo[:, :], ps_t[:, 0:DIM], aT_hi[:, :],
                                                ALU.subtract).then_inc(aT_lo_ready, 1)
                    if on(t, N):
                        wait(dve, hT_hi_ready, t + 1)
                        wait(dve, v_done, t)
                        nc.vector.tensor_tensor(hT_lo[:, :], tr[:, :], hT_hi[:, :],
                                                ALU.subtract).then_inc(hT_lo_ready, 1)
                    if on(t - 1, N):
                        s4 = ps_s.rearrange("p bank half (a b) -> p (bank half) a b", b=TOK)
                        t3 = top[:, :].rearrange("p (j a) -> p j a", j=4)
                        wait(dve, scores_done, t)
                        nc.vector.tensor_reduce(t3, s4, AX.X, ALU.max).then_inc(shift_ready, 1)
                        wait(dve, shift_ready, 2 * t - 1)
                        wait(dve, probs_ready, t - 1)
                        nc.vector.tensor_tensor(shifted[:, :].rearrange("p (j a b) -> p j a b", j=4, b=TOK), s4,
                                                t3.unsqueeze(3).to_broadcast([P, 4, 4, TOK]),
                                                ALU.subtract).then_inc(shift_ready, 1)
                    if on(t - 2, N):
                        wait(dve, wo_done, t - 1)
                        wait(dve, h0_saved, t - 1)
                        nc.vector.tensor_tensor(h[:, t - 2, :], out0, h[:, t - 2, :],
                                                ALU.add).then_inc(res_ready, 1)
                    if on(t, N):
                        wait(dve, qk_done, t + 1)
                        nc.vector.tensor_tensor(rot_a[:, :].rearrange("p (s n) -> p s n", s=2), ps_qk,
                                                rope_c[:, :].rearrange("p (s n) -> p s n", s=2), ALU.mult)
                        pair = ps_qk.rearrange("p s (n two) -> p s n two", two=2)
                        sgn = rope_s[:, :].rearrange("p (s n two) -> p s n two", s=2, two=2)
                        dst = rot_b[:, :].rearrange("p (s n two) -> p s n two", s=2, two=2)
                        nc.vector.tensor_tensor(dst[:, :, :, 0], pair[:, :, :, 1], sgn[:, :, :, 0], ALU.mult)
                        nc.vector.tensor_tensor(dst[:, :, :, 1], pair[:, :, :, 0], sgn[:, :, :, 1],
                                                ALU.mult).then_inc(rot_parts, 1)
                        wait(dve, rot_parts, t + 1)
                        wait(dve, qkT_done, t)
                        nc.vector.tensor_tensor(slots[:, 0:DIM], rot_a[:, 0:DIM], rot_b[:, 0:DIM], ALU.add)
                        spread = slots[:, DIM:].rearrange("p (v pair w d) -> p v pair w d", v=2, w=2, d=DK0)
                        ka, kb = (r[:, DIM:].rearrange("p (pair v d) -> p v pair d", v=2, d=DK0) for r in (rot_a, rot_b))
                        for v in range(2):
                            ins = nc.vector.tensor_tensor(spread[:, v, :, v, :], ka[:, v, :, :], kb[:, v, :, :], ALU.add)
                        ins.then_inc(rotated, 1)
                    if on(t - 2, N):
                        wait_apart(dve, res_ready, t - 1)
                        nc.vector.bn_stats(bn[:, :], h[:, t - 2, :]).then_inc(var_ready, 1)
                        wait_apart(dve, var_ready, 2 * t - 3)
                        nc.vector.bn_aggr(mv[:, :], bn[:, :]).then_inc(var_ready, 1)
                    if on(t + 1, N):
                        embedded(t + 1)
                    if on(t - 1, N):
                        wait(dve, pT_done, t)
                        wait(dve, pv_done, t - 1)
                        nc.vector.tensor_copy(probsT[:, 4:8, :].rearrange("p a b -> p (a b)"),
                                              ps_t[:, 512:1024]).then_inc(pT_b_ready, 1)
                        o3 = ps_o[:, :].rearrange("p (n d) -> p n d", d=VW)
                        wait(dve, pv_done, t)
                        nc.vector.reciprocal(rsum[:, :], o3[:, :, DK0]).then_inc(att_ready, 1)
                        wait(dve, att_ready, 2 * t - 1)
                        wait(dve, aT_done, t - 1)
                        for cc in range(2):
                            ins = nc.vector.tensor_tensor(
                                att[:, cc * P:(cc + 1) * P].rearrange("p (j v d) -> p j v d", j=4, v=2),
                                o3[:, :, 0:DK0].rearrange("p (j c v) d -> p c j v d", j=4, c=2)[:, cc],
                                rsum[:, :].rearrange("p (j c v) -> p c j v", j=4, c=2)[:, cc].unsqueeze(3)
                                .to_broadcast([P, 4, 2, DK0]), ALU.mult)
                        ins.then_inc(att_ready, 1)
                    if on(t - 2, N):
                        normalise(t - 2)
                    if isinstance(t, int) and t in (0, 1, 2):
                        if t == 0:
                            dve.wait_ge(mlp_in, 64)
                        if t < 2:
                            largest(t)
                        else:
                            scales()
                            quantise(0)
                    elif isinstance(t, int) and t == 3:
                        quantise(1)

                dve.wait_ge(setup_dve, 1)
                dve.wait_ge(setup_pool, 1)
                embedded(0)
                in_pairs(dve, body, N)
                body(N, 0, 0)
                body(N + 1, 1, 0)

            @block.tensor
            def _(pe):
                def embed(t):
                    wait(pe, x_split, 2 * t + 2)
                    wait(pe, h0_ready, t)
                    split_matmul(nc, emb, both(x_hi, x_lo, P), wp_k).then_inc(emb_done, 1)

                def transposes(dst, src, n):
                    for k in range(n):
                        ins = nc.tensor.transpose(dst[:, k * P:(k + 1) * P], src[:, k * P:(k + 1) * P], ident[:, :])
                    return ins

                def scores(half):
                    for bank in range(2):
                        nc.tensor.matmul(ps_s[:, bank, half, :], ident_bf[:, :], mask[:, :], start=True, stop=False,
                                         skip_group_check=True)
                    for cc in range(2):
                        for bank in range(2):
                            j = 2 * bank + half
                            q = slice(SLOT * j, SLOT * j + SLOT)
                            for b in range(2):
                                tk = slice(64 * b, 64 * b + 64)
                                ins = nc.tensor.matmul(
                                    ps_s[tk, bank, half, cc * P:(cc + 1) * P].rearrange("p (v k) -> p v k", v=2),
                                    qkT[q, cc, tk], qkT[q, 2 + cc:6:2, tk], start=False, stop=cc == 1,
                                    skip_group_check=True)
                    return ins

                def body(t, par, _):
                    if on(t - 1, N):
                        wait(pe, qkT_ready, t)
                        wait(pe, shift_ready, 2 * t - 2)
                        scores(0).then_inc(half_scores, 1)
                    if on(t - 2, N):
                        wait(pe, att_ready, 2 * t - 2)
                        transposes(ps_t, att, DC).then_inc(aT_done, 1)
                    if on(t, N):
                        wait(pe, h0_ready, t + 1)
                        transposes(tr, fresh, DC).then_inc(hT_done, 1)
                    if on(t - 1, N):
                        wait(pe, half_scores, t)
                        scores(1).then_inc(scores_done, 1)
                    if on(t - 2, N):
                        wait(pe, aT_hi_ready, t - 1)
                        wait(pe, aT_lo_ready, t - 1)
                        split_matmul(nc, out0, both(aT_hi, aT_lo, P), wo_k).then_inc(wo_done, 1)
                    if on(t, N):
                        wait(pe, hT_hi_ready, t + 1)
                        wait(pe, hT_lo_ready, t + 1)
                        wait(pe, qkT_ready, t)
                        for n in range(2):
                            ins = split_matmul(nc, ps_qk[:, n, :], both(hT_hi, hT_lo, P), wqkv(n * DIM, (n + 1) * DIM))
                        ins.then_inc(qk_done, 1)
                    if on(t + 1, N):
                        embed(t + 1)
                    if on(t, N):
                        for b in range(2):
                            for half in range(2):
                                col = 2 * DIM + half * P
                                ins = split_matmul(nc, ps_v[64 * half:64 * half + 64, b, :],
                                                   both(hT_hi, hT_lo, P, 64 * b, 64 * b + 64),
                                                   wqkv(col, col + P))
                        ins.then_inc(v_done, 1)
                    if on(t - 1, N):
                        wait(pe, probs_ready, t)
                        wait(pe, res_ready, t - 1)
                        transposes(ps_t, probs, PAIRS).then_inc(pT_done, 1)
                    if on(t, N):
                        wait(pe, rotated, t + 1)
                        wait(pe, v_ready, t + 1)
                        transposes(ps_qkT, slots, 6).then_inc(qkT_done, 1)
                    if on(t - 1, N):
                        wait(pe, pT_a_ready, t)
                        wait(pe, pT_b_ready, t)
                        wait(pe, v_ready, t)
                        wait(pe, att_ready, 2 * t - 2)
                        for b in range(2):
                            tk = slice(64 * b, 64 * b + 64)
                            for pr in range(PAIRS):
                                ins = nc.tensor.matmul(ps_o[tk, pr * 2 * VW:(pr + 1) * 2 * VW], probsT[:, pr, tk],
                                                       vpair[1 - par][b][:, pr, :], start=True, stop=True)
                        ins.then_inc(pv_done, 1)

                pe.wait_ge(w_lo, 1)
                embed(0)
                pe.wait_ge(consts_in, 16 * CONSTANTS)
                pe.wait_ge(w_hi, 4)
                pe.wait_ge(w_lo, 3)
                pe.wait_ge(setup_pool, 9)
                in_pairs(pe, body, N)
                body(N, 0, 0)
                body(N + 1, 1, 0)


def quantised_mlp(nc, A, S):
    h, w1q, w2q, b1, b2 = S["h"], S["w1q"], S["w2q"], S["b1"], S["b2"]
    bn, mv, rstd, neg_half, amax, wscale = (S["bn"], S["mv"], S["rstd"], S["neg_half"], S["amax"], S["wscale"])
    N = TILES
    CH = 4
    CHUNKS = N // CH
    W = CH * P
    with ExitStack() as c:
        def sb(name, shape, dt=F32):
            return S["sb"](name, shape, dt, c)

        def ps(name, shape, dt=F32):
            return S["ps"](name, shape, dt, c)

        hidden = sb("hidden", [P, HC, TOKENS])
        rounding = sb("rounding", [P, CH * DIM])
        xq = sb("xq", [P, CH * DIM], BF16)
        xqT = [sb(f"xqT{u}", [P, DC, W], BF16) for u in range(2)]
        hq = [sb(f"hq{u}", [P, HC, P], BF16) for u in range(2)]
        hmax = sb("hmax", [P, CHUNKS * 4])
        b2s = sb("b2s", [P, DIM])
        b1s = sb("b1s", [P, HC])
        scale_x, scale_h = sb("scale_x", [P, 5]), sb("scale_h", [P, 5])
        ps_x = ps("ps_x", [P, DC, W], BF16)
        ps_f = ps("ps_f", [P, 4, 512])
        ps_y = ps("ps_y", [P, 2, 512])
        s = {n: S["sem"](n) for n in (
            "x_max", "x_all", "x_scale", "xq_up", "xq_ready", "xT_done", "xqT_ready", "up_done", "gelu_ready",
            "hmax_ready", "h_max", "h_all", "h_scale", "hq_up", "hq_ready", "down_done", "mlp_hb",
            "mlp_res", "mlp_var", "mlp_rstd", "mlp_norm")}

        def quantise(eng, unit, n):
            src = h[:, n * CH:(n + 1) * CH, :].rearrange("p t d -> p (t d)")
            wait_apart(eng, s["xq_ready"], n)
            unit.tensor_scalar(rounding[:, :], src, scale_x[:, 3:4], ROUND, ALU.mult, ALU.add).then_inc(s["xq_up"], 1)
            wait(eng, s["xq_up"], n + 1)
            wait_apart(eng, s["xT_done"], n)
            unit.tensor_scalar(xq[:, :], rounding[:, :], ROUND, None, ALU.subtract).then_inc(s["xq_ready"], 1)

        with nc.Block() as block:

            @block.gpsimd
            def _(pool):
                for col, (ready, done) in ((scale_x, ("x_max", "x_all")), (scale_h, ("h_max", "h_all"))):
                    pool.wait_ge(s[ready], 1)
                    nc.gpsimd.partition_all_reduce(col[:, 1:2], col[:, 0:1], P,
                                                   bass.bass_isa.ReduceOp.max).then_inc(s[done], 1)
                    if col is scale_x:
                        pool.wait_ge(s["x_scale"], 4)
                        for n in range(1, CHUNKS):
                            quantise(pool, nc.gpsimd, n)

                def add_bias(t):
                    nc.gpsimd.tensor_tensor(h[:, t, :], h[:, t, :], b2s[:, :], ALU.add).then_inc(s["mlp_hb"], 1)

                def root(t):
                    wait(pool, s["mlp_var"], 2 * t + 2)
                    wait_apart(pool, s["mlp_norm"], t)
                    nc.gpsimd.tensor_scalar(rstd[:, :], mv[:, 1:2], EPS, None, ALU.add).then_inc(s["mlp_rstd"], 1)
                    wait(pool, s["mlp_rstd"], 2 * t + 1)
                    nc.gpsimd.tensor_tensor(rstd[:, :], rstd[:, :], neg_half[:, :],
                                            ALU.pow).then_inc(s["mlp_rstd"], 1)

                pool.wait_ge(s["h_scale"], 4)
                add_bias(0)
                add_bias(1)
                root(0)
                with pool.Fori(1, N - 1) as t:
                    add_bias(t + 1)
                    root(t)
                root(N - 1)

            @block.vector
            def _(dve):
                def scales(col, data, w, mx, all_, done):
                    nc.vector.tensor_reduce(col[:, 0:1], data, AX.X, ALU.max).then_inc(s[mx], 1)
                    dve.wait_ge(s[all_], 1)
                    nc.vector.tensor_scalar(col[:, 2:3], col[:, 1:2], 1e-6, 1.0 / 127.0,
                                            ALU.max, ALU.mult).then_inc(s[done], 1)
                    dve.wait_ge(s[done], 1)
                    nc.vector.reciprocal(col[:, 3:4], col[:, 2:3]).then_inc(s[done], 1)
                    nc.vector.tensor_tensor(col[:, 4:5], col[:, 2:3], wscale[:, w:w + 1],
                                            ALU.mult).then_inc(s[done], 1)
                    dve.wait_ge(s[done], 3)

                scales(scale_x, amax[:, :], 0, "x_max", "x_all", "x_scale")
                nc.vector.tensor_scalar(b1s[:, :], b1[:, :], scale_x[:, 4:5], None,
                                        ALU.mult).then_inc(s["x_scale"], 1)

                def gather(n, u):
                    wait(dve, s["xT_done"], n + 1)
                    wait(dve, s["up_done"], HC * (n - 1))
                    nc.vector.tensor_copy(xqT[u][:, :, :], ps_x[:, :, :]).then_inc(s["xqT_ready"], 1)

                def largest(n):
                    for f in range(0, HC, 2):
                        wait(dve, s["gelu_ready"], HC * n + f + 2)
                        col = n * 4 + f // 2
                        nc.vector.tensor_reduce(hmax[:, bass.ds(col, 1)], hidden[:, f:f + 2, bass.ts(n, W)],
                                                AX.XY, ALU.max, apply_absolute_value=True).then_inc(s["hmax_ready"], 1)

                quantise(dve, nc.vector, 0)
                gather(0, 0)

                def chunk(n, u, _):
                    if on(n + 1, CHUNKS):
                        gather(n + 1, 1 - u)
                    largest(n)

                in_pairs(dve, chunk, CHUNKS, 2)
                dve.wait_ge(s["hmax_ready"], 4 * CHUNKS)
                scales(scale_h, hmax[:, :], 1, "h_max", "h_all", "h_scale")
                nc.vector.tensor_scalar(b2s[:, :], b2[:, :], scale_h[:, 4:5], None,
                                        ALU.mult).then_inc(s["h_scale"], 1)

                def quantise_hidden(t):
                    v = hidden[:, :, bass.ts(t, P)]
                    nc.vector.tensor_scalar(v, v, scale_h[:, 3:4], ROUND, ALU.mult, ALU.add).then_inc(s["hq_up"], 1)

                def finish(t, u):
                    wait(dve, s["down_done"], t + 1)
                    wait_apart(dve, s["mlp_hb"], t + 1)
                    nc.vector.scalar_tensor_tensor(h[:, t, :], ps_y[:, u, 0:DIM], scale_h[:, 4:5], h[:, t, :],
                                                   ALU.mult, ALU.add).then_inc(s["mlp_res"], 1)
                    if on(t + 3, N):
                        quantise_hidden(t + 3)
                    if on(t - 1, N):
                        normalise(t - 1)
                    wait_apart(dve, s["mlp_res"], t + 1)
                    nc.vector.bn_stats(bn[:, :], h[:, t, :]).then_inc(s["mlp_var"], 1)
                    wait_apart(dve, s["mlp_var"], 2 * t + 1)
                    nc.vector.bn_aggr(mv[:, :], bn[:, :]).then_inc(s["mlp_var"], 1)

                def normalise(t):
                    wait(dve, s["mlp_rstd"], 2 * t + 2)
                    nc.vector.tensor_scalar(h[:, t, :], h[:, t, :], mv[:, 0:1], rstd[:, 0:1],
                                            ALU.subtract, ALU.mult).then_inc(s["mlp_norm"], 1)

                for t in range(3):
                    quantise_hidden(t)
                finish(0, 0)
                finish(1, 1)
                with dve.Fori(1, N // 2 - 2) as pair:
                    finish(2 * pair, 0)
                    finish(2 * pair + 1, 1)
                for t in range(N - 4, N):
                    finish(t, t % 2)
                normalise(N - 1)

            @block.scalar
            def _(act):
                act.wait_ge(s["x_scale"], 4)

                def gelus(n):
                    for f in range(HC):
                        act.wait_ge(s["up_done"], n * HC + f + 1)
                        nc.scalar.activation(hidden[:, f, bass.ts(n, W)], ps_f[:, f % 4, :], ACT.Gelu,
                                             bias=b1s[:, f:f + 1], scale=scale_x[:, 4:5]).then_inc(s["gelu_ready"], 1)

                gelus(0)
                with act.Fori(1, CHUNKS) as n:
                    gelus(n)

                def lower(t, u):
                    wait(act, s["hq_up"], t + 1)
                    wait(act, s["down_done"], t - 1)
                    nc.scalar.activation(hq[u][:, :, :], hidden[:, :, bass.ts(t, P)], ACT.Copy,
                                         bias=-ROUND).then_inc(s["hq_ready"], 1)

                lower(0, 0)
                lower(1, 1)
                with act.Fori(1, N // 2) as pair:
                    lower(2 * pair, 0)
                    lower(2 * pair + 1, 1)

            @block.tensor
            def _(pe):
                def transposes(n):
                    wait(pe, s["xq_ready"], n + 1)
                    wait(pe, s["xqT_ready"], n)
                    for j in range(CH):
                        for k in range(DC):
                            ins = nc.tensor.transpose(ps_x[:, k, j * P:(j + 1) * P],
                                                      xq[:, j * DIM + k * P:j * DIM + (k + 1) * P],
                                                      S["ident_bf"][:, :])
                    ins.then_inc(s["xT_done"], 1)

                def up(n, u, _):
                    wait(pe, s["xqT_ready"], n + 1)
                    for f in range(HC):
                        wait(pe, s["gelu_ready"], n * HC + f - 3)
                        for k in range(DC):
                            ins = nc.tensor.matmul(ps_f[:, f % 4, :], w1q[:, k, f * P:(f + 1) * P],
                                                   xqT[u][:, k, :], start=k == 0, stop=k == DC - 1)
                        ins.then_inc(s["up_done"], 1)
                        if f == 3 and on(n + 1, CHUNKS):
                            transposes(n + 1)

                def down(t, u):
                    wait(pe, s["hq_ready"], t + 1)
                    wait(pe, s["mlp_res"], t - 1)
                    for f in range(HC):
                        ins = nc.tensor.matmul(ps_y[:, u, 0:DIM], hq[u][:, f, :], w2q[:, f, :],
                                               start=f == 0, stop=f == HC - 1)
                    ins.then_inc(s["down_done"], 1)

                transposes(0)
                in_pairs(pe, up, CHUNKS, 2)
                down(0, 0)
                down(1, 1)
                with pe.Fori(1, N // 2) as pair:
                    down(2 * pair, 0)
                    down(2 * pair + 1, 1)


def cross_head_attention(nc, A, S):
    h, ident, ident_bf = S["h"], S["ident"], S["ident_bf"]
    bn, mv, rstd, neg_half = S["bn"], S["mv"], S["rstd"], S["neg_half"]
    MACRO = 2 * P
    M = TOKENS // MACRO
    GROUPS = MACRO // 4
    UNITS = M * 4
    UG = 16
    R = 3 * HEADS1 * DK1 // MACRO
    QKV = 3 * HEADS1 * DK1
    OC = HEADS1 * DK1 // P
    with ExitStack() as c:
        def sb(name, shape, dt=F32):
            return S["sb"](name, shape, dt, c)

        def ps(name, shape, dt=F32):
            return S["ps"](name, shape, dt, c)

        qkv = [sb(f"qkv{par}", [P, 3, GROUPS, HEADS1, 4]) for par in range(2)]
        w_hi, w_lo = sb("wqkv1_hi", [P, DC * QKV], BF16), sb("wqkv1_lo", [P, DC * QKV], BF16)
        wp_hi, wp_lo = sb("wp1_hi", [P, OC * DIM], BF16), sb("wp1_lo", [P, OC * DIM], BF16)
        stage = qkv[1][:, :, :, :, :].rearrange("p x g i t -> p (x g i t)")
        stage_w = stage[:, 0:DC * QKV].rearrange("p (kk n) -> p kk n", kk=DC)
        stage_p = stage[:, DC * QKV:DC * QKV + OC * DIM]

        def weights(n, w, p, count=1):
            if n >= 6:
                return p[:, (n - 6) * OC * DIM // 2:(n - 6 + count) * OC * DIM // 2]
            w = w.rearrange("p (kk n) -> p kk n", kk=DC) if len(w.shape) == 2 else w
            return w[:, :, n * QKV // 6:(n + count) * QKV // 6]

        LOADS = ((0, 1), (1, 1), (2, 2), (4, 2), (6, 2))

        def arrived(n):
            return w_in[max(i for i, (first, _) in enumerate(LOADS) if first <= n)]

        mask = sb("mask1", [P, 512], BF16)
        mask_f = sb("mask1_f", [P, 512])
        bp = sb("bp", [P, DIM])
        hs = sb("hs", [P, 2, DIM])
        hT_hi = [sb(f"h1T_hi{u}", [P, DC, MACRO], BF16) for u in range(2)]
        hT_lo = [sb(f"h1T_lo{u}", [P, DC, MACRO], BF16) for u in range(2)]
        top = sb("top1", [P, 8])
        sums = sb("sums1", [P, 8])
        inv = sb("inv1", [P, 8])
        shifted = sb("shifted1", [P, 512])
        probs = sb("probs1", [P, 512])
        normed = sb("normed1", [P, 512])
        probsT = sb("probsT1", [P, 512])
        vdiag = sb("vdiag", [P, 8, P])
        oT_hi, oT_lo = sb("oT_hi", [P, OC, P], BF16), sb("oT_lo", [P, OC, P], BF16)
        g_rows, g_rowsT = sb("g_rows", [P, DIM]), sb("g_rowsT", [P, DIM])

        ps_tr = ps("ps_tr1", [P, DC, MACRO])
        ps_p = [ps(f"ps_p{u}", [P, 2, MACRO]) for u in range(2)]
        ps_s = ps("ps_s1", [P, 512])
        ps_t = ps("ps_t1", [P, 512])
        ps_v = ps("ps_v1", [P, 512])
        ps_o = ps("ps_o1", [P, 512])
        ps_y = ps("ps_y1", [P, 512])

        w_in = [S["sem"](f"a1_w_in{n}") for n in range(5)]
        s = {n: S["sem"](n) for n in (
            "a1_consts", "mask_ready", "h_out", "gate_in", "a1_w_hi", "a1_w_lo", "a1_zero", "hs_ready", "hb_ready", "a1_tr_done",
            "a1_hT_hi", "a1_hT_lo", "proj_done", "proj_act", "proj_dve", "a1_scores", "a1_shift",
            "a1_probs", "a1_inv", "a1_normed", "a1_pT_done", "a1_pT", "a1_vT_done", "vdiag_act",
            "vdiag_dve", "a1_pv", "oT_hi_ready", "oT_lo_ready", "a1_out", "a1_res", "a1_var",
            "a1_rstd", "a1_norm", "g_rows", "g_trans", "g_hT", "g_logit")}

        def rows(m):
            return h[:, 2 * m:2 * m + 2, :] if isinstance(m, int) else h[:, bass.ts(m, 2), :]

        def sequence(eng, body):
            body(0, 0)
            body(1, 1)
            with eng.Fori(1, M // 2 - 1) as pair:
                body(2 * pair, 0)
                body(2 * pair + 1, 1)
            for m in range(M - 2, M + 2):
                body(m, m % 2)

        with nc.Block() as block:

            @block.sync
            def _(sp):
                for i, (n, count) in enumerate(LOADS):
                    sp.dma_start(weights(n, stage_w, stage_p, count),
                                 weights(n, A["wqkv1"], A["wp1"], count)).then_inc(w_in[i], 16)
                    if i == 1:
                        for dst, name in ((bp, "bp"), (mask_f, "mask1"), (S["wg"], "wg")):
                            sp.dma_start(dst[:, :], A[name]).then_inc(s["a1_consts"], 16)
                for dst, name in S["gate_consts"]:
                    sp.dma_start(dst[:], A[name].rearrange("p (c n) -> p c n", c=2) if name == "tnum" else A[name]
                                 ).then_inc(s["gate_in"], 16)
                with sp.Fori(0, TILES) as j:
                    sp.wait_ge(s["a1_norm"], j + 1)
                    sp.dma_start(S["h_rows"][bass.ts(j, P), :], h[:, j, :]).then_inc(s["h_out"], 16)
                sp.wait_ge(s["h_out"], 16 * TILES)
                sp.wait_ge(s["gate_in"], 16 * len(S["gate_consts"]))

            def slot_index(m, u):
                return 4 * (m - 1) + u

            def tile_index(m, u):
                return 2 * m - 3 + (u - 1) // 2

            def gate_index(m, u):
                return 2 * m - 4 + u // 2

            @block.scalar
            def _(act):
                def high(n):
                    act.wait_ge(arrived(n), 16)
                    nc.scalar.copy(weights(n, w_hi[:, :], wp_hi[:, :]),
                                   weights(n, stage_w, stage_p)).then_inc(s["a1_w_hi"], 1)

                def transposed(m, par):
                    wait(act, s["a1_tr_done"], m + 1)
                    wait(act, s["proj_done"], R * (m - 1))
                    nc.scalar.copy(hT_hi[par][:, :, :], ps_tr[:, :, :]).then_inc(s["a1_hT_hi"], 1)

                def evacuate(m, par, r):
                    wait(act, s["proj_done"], R * m + r + 1)
                    if r == 0:
                        wait(act, s["a1_vT_done"], 4 * (m - 1))
                        if isinstance(m, int) and m == 1:
                            act.wait_ge(s["a1_w_lo"], 8)
                    i = 4 * (r % 4)
                    nc.scalar.copy(qkv[par][0:64, r // 4, :, i:i + 3:2, :].rearrange("p g a t -> p a g t"),
                                   ps_p[r % 2][0:64, :, :].rearrange("p a (g t) -> p a g t", t=4)
                                   ).then_inc(s["proj_act"], 1)
                    if isinstance(m, int) and m == 0 and r % 2:
                        high((r + 3) // 2)

                def exponentials(k):
                    wait(act, s["a1_shift"], 2 * k + 2)
                    wait(act, s["a1_normed"], k)
                    nc.scalar.activation(probs[:, :], shifted[:, :], ACT.Exp,
                                         scale=float(DK1) ** -0.5).then_inc(s["a1_probs"], 1)

                def turned(k):
                    wait(act, s["a1_pT_done"], k + 1)
                    wait(act, s["a1_pv"], k)
                    nc.scalar.copy(probsT[:, :], ps_t[:, :]).then_inc(s["a1_pT"], 1)

                def body(m, par):
                    for u in range(4):
                        k = slot_index(m, u)
                        if u % 2 and on(gate_index(m, u - 1), TILES):
                            wait(act, s["g_trans"], gate_index(m, u - 1) + 1)
                            nc.scalar.copy(g_rowsT[:, :], ps_y[:, DIM:2 * DIM]).then_inc(s["g_hT"], 1)
                        if on(m, M):
                            evacuate(m, par, 3 * u)
                        if u % 2 and on(k, UNITS):
                            exponentials(k)
                        if on(k - 1, UNITS):
                            turned(k - 1)
                        if u % 2 == 0 and on(k, UNITS):
                            exponentials(k)
                        if on(m, M):
                            evacuate(m, par, 3 * u + 1)
                        if on(k - 1, UNITS):
                            wait(act, s["a1_pv"], k)
                            if (u - 1) % 2 == 0:
                                wait(act, s["a1_out"], 2 * m - 3 + (u + 1) // 2)
                            src = ps_o[:, :].rearrange("p (ca m two t) -> p two m ca t", ca=8, two=2, t=4)
                            half = slice(64 * ((u - 1) % 2), 64 * ((u - 1) % 2) + 64)
                            dst = oT_hi[:, :, half].rearrange("p m (ca pp t) -> p pp m ca t", pp=2, t=4)
                            for pp in range(2):
                                for ip in range(2):
                                    ins = nc.scalar.copy(dst[64 * ip:64 * ip + 64, pp], src[64 * pp:64 * pp + 64, ip])
                            ins.then_inc(s["oT_hi_ready"], 1)
                        if on(k, UNITS):
                            wait(act, s["a1_vT_done"], k + 1)
                            wait(act, s["a1_pv"], k)
                            nc.scalar.copy(vdiag[0:64, :, 0:64],
                                           ps_v[0:64, :].rearrange("p (a d) -> p a d", d=64)
                                           ).then_inc(s["vdiag_act"], 1)
                        if on(m, M):
                            evacuate(m, par, 3 * u + 2)
                        if u == 1 and on(m + 1, M):
                            transposed(m + 1, 1 - par)

                high(0)
                transposed(0, 0)
                high(1)
                act.wait_ge(s["a1_consts"], 48)
                nc.scalar.copy(mask[:, :], mask_f[:, :]).then_inc(s["mask_ready"], 1)
                sequence(act, body)

            @block.gpsimd
            def _(pool):
                def fetch(m):
                    wait(pool, s["a1_tr_done"], m)
                    nc.gpsimd.tensor_copy(hs[:, :, :], rows(m)).then_inc(s["hs_ready"], 1)
                    if isinstance(m, int) and m == 0:
                        pool.wait_ge(s["a1_consts"], 48)
                    nc.gpsimd.tensor_tensor(rows(m), rows(m), bp[:, :].unsqueeze(1).to_broadcast([P, 2, DIM]),
                                            ALU.add).then_inc(s["hb_ready"], 1)

                def body(m, par):
                    for u in range(4):
                        k = slot_index(m, u)
                        if u == 1 and on(m + 1, M):
                            fetch(m + 1)
                        if on(k, UNITS):
                            wait(pool, s["a1_inv"], 2 * k + 2)
                            wait(pool, s["a1_pT_done"], k)
                            nc.gpsimd.tensor_tensor(normed[:, :].rearrange("p (a b) -> p a b", b=64),
                                                    probs[:, :].rearrange("p (a b) -> p a b", b=64),
                                                    inv[:, :].unsqueeze(2).to_broadcast([P, 8, 64]),
                                                    ALU.mult).then_inc(s["a1_normed"], 1)
                        if u % 2 == 0 and on(gate_index(m, u), TILES):
                            wait(pool, s["a1_norm"], gate_index(m, u) + 1)
                            nc.gpsimd.tensor_copy(g_rows[:, :], h[:, gate_index(m, u), :]).then_inc(s["g_rows"], 1)
                        if u % 2 and on(tile_index(m, u), TILES):
                            j = tile_index(m, u)
                            wait(pool, s["a1_var"], 2 * j + 2)
                            wait_apart(pool, s["a1_norm"], j)
                            nc.gpsimd.tensor_scalar(rstd[:, :], mv[:, 1:2], EPS, None,
                                                    ALU.add).then_inc(s["a1_rstd"], 1)
                            wait(pool, s["a1_rstd"], 2 * j + 1)
                            nc.gpsimd.tensor_tensor(rstd[:, :], rstd[:, :], neg_half[:, :],
                                                    ALU.pow).then_inc(s["a1_rstd"], 1)

                fetch(0)
                nc.gpsimd.memset(vdiag[:, :, :], 0.0).then_inc(s["a1_zero"], 1)
                sequence(pool, body)

            @block.vector
            def _(dve):
                def low(n):
                    dve.wait_ge(s["a1_w_hi"], n + 1)
                    nc.vector.tensor_tensor(weights(n, w_lo[:, :], wp_lo[:, :]),
                                            weights(n, stage_w, stage_p),
                                            weights(n, w_hi[:, :], wp_hi[:, :]),
                                            ALU.subtract).then_inc(s["a1_w_lo"], 1)

                def transposed(m, par):
                    wait(dve, s["a1_hT_hi"], m + 1)
                    wait(dve, s["proj_done"], R * (m - 1))
                    nc.vector.tensor_tensor(hT_lo[par][:, :, :], ps_tr[:, :, :], hT_hi[par][:, :, :],
                                            ALU.subtract).then_inc(s["a1_hT_lo"], 1)

                def evacuate(m, par, r):
                    wait(dve, s["proj_done"], R * m + r + 1)
                    if r == 0:
                        wait(dve, s["a1_vT_done"], 4 * (m - 1))
                    i = 4 * (r % 4) + 1
                    nc.vector.tensor_copy(qkv[par][0:64, r // 4, :, i:i + 3:2, :].rearrange("p g a t -> p a g t"),
                                          ps_p[r % 2][64:128, :, :].rearrange("p a (g t) -> p a g t", t=4)
                                          ).then_inc(s["proj_dve"], 1)
                    if isinstance(m, int) and m == 0 and r % 2:
                        low((r + 3) // 2)

                def gate(j):
                    wait(dve, s["g_logit"], j + 1)
                    nc.vector.tensor_copy(S["logit"][:, bass.ds(j, 1), :].rearrange("p a e -> p (a e)"),
                                          ps_y[:, DIM:DIM + EXPERTS])

                def body(m, par):
                    for u in range(4):
                        k = slot_index(m, u)
                        s3 = ps_s[:, :].rearrange("p (a b) -> p a b", b=64)
                        if on(k, UNITS):
                            wait(dve, s["a1_scores"], k + 1)
                            nc.vector.tensor_reduce(top[:, :], s3, AX.X, ALU.max).then_inc(s["a1_shift"], 1)
                            wait(dve, s["a1_shift"], 2 * k + 1)
                            wait(dve, s["a1_probs"], k)
                            nc.vector.tensor_tensor(shifted[:, :].rearrange("p (a b) -> p a b", b=64), s3,
                                                    top[:, :].unsqueeze(2).to_broadcast([P, 8, 64]),
                                                    ALU.subtract).then_inc(s["a1_shift"], 1)
                        if on(m, M):
                            evacuate(m, par, 3 * u)
                        if u % 2 and on(tile_index(m, u), TILES):
                            j = tile_index(m, u)
                            wait(dve, s["a1_out"], j + 1)
                            nc.vector.tensor_tensor(h[:, j, :], ps_y[:, 0:DIM], h[:, j, :],
                                                    ALU.add).then_inc(s["a1_res"], 1)
                            if on(j - 1, TILES):
                                gate(j - 1)
                            wait_apart(dve, s["a1_res"], j + 1)
                            nc.vector.bn_stats(bn[:, :], h[:, j, :]).then_inc(s["a1_var"], 1)
                            wait_apart(dve, s["a1_var"], 2 * j + 1)
                            nc.vector.bn_aggr(mv[:, :], bn[:, :]).then_inc(s["a1_var"], 1)
                        elif u % 2 and on(gate_index(m, u - 1), TILES):
                            gate(gate_index(m, u - 1))
                        if on(k, UNITS):
                            wait(dve, s["a1_probs"], k + 1)
                            nc.vector.tensor_reduce(sums[:, :], probs[:, :].rearrange("p (a b) -> p a b", b=64),
                                                    AX.X, ALU.add).then_inc(s["a1_inv"], 1)
                            wait(dve, s["a1_inv"], 2 * k + 1)
                            wait(dve, s["a1_normed"], k)
                            nc.vector.reciprocal(inv[:, :], sums[:, :]).then_inc(s["a1_inv"], 1)
                        if on(m, M):
                            evacuate(m, par, 3 * u + 1)
                        if on(k - 1, UNITS):
                            wait(dve, s["oT_hi_ready"], k)
                            if (u - 1) % 2 == 0:
                                wait(dve, s["a1_out"], 2 * m - 3 + (u + 1) // 2)
                            src = ps_o[:, :].rearrange("p (ca m two t) -> p two m ca t", ca=8, two=2, t=4)
                            half = slice(64 * ((u - 1) % 2), 64 * ((u - 1) % 2) + 64)
                            hi = oT_hi[:, :, half].rearrange("p m (ca pp t) -> p pp m ca t", pp=2, t=4)
                            lo = oT_lo[:, :, half].rearrange("p m (ca pp t) -> p pp m ca t", pp=2, t=4)
                            for pp in range(2):
                                for ip in range(2):
                                    q = slice(64 * ip, 64 * ip + 64)
                                    ins = nc.vector.tensor_tensor(lo[q, pp], src[64 * pp:64 * pp + 64, ip],
                                                                  hi[q, pp], ALU.subtract)
                            ins.then_inc(s["oT_lo_ready"], 1)
                        if on(k, UNITS):
                            wait(dve, s["a1_vT_done"], k + 1)
                            wait(dve, s["a1_pv"], k)
                            nc.vector.tensor_copy(vdiag[64:128, :, 64:128],
                                                  ps_v[64:128, :].rearrange("p (a d) -> p a d", d=64)
                                                  ).then_inc(s["vdiag_dve"], 1)
                        if on(m, M):
                            evacuate(m, par, 3 * u + 2)
                        if u == 1 and on(m + 1, M):
                            transposed(m + 1, 1 - par)
                        if u % 2 and on(tile_index(m, u), TILES):
                            j = tile_index(m, u)
                            wait(dve, s["a1_rstd"], 2 * j + 2)
                            nc.vector.tensor_scalar(h[:, j, :], h[:, j, :], mv[:, 0:1], rstd[:, 0:1],
                                                    ALU.subtract, ALU.mult).then_inc(s["a1_norm"], 1)

                low(0)
                transposed(0, 0)
                low(1)
                dve.wait_ge(s["a1_zero"], 1)
                sequence(dve, body)

            @block.tensor
            def _(pe):
                def transposes(m):
                    wait(pe, s["hs_ready"], m + 1)
                    wait(pe, s["a1_hT_lo"], m)
                    for j in range(2):
                        for kk in range(DC):
                            ins = nc.tensor.transpose(ps_tr[:, kk, j * P:(j + 1) * P],
                                                      hs[:, j, kk * P:(kk + 1) * P], ident[:, :])
                    ins.then_inc(s["a1_tr_done"], 1)

                def project(m, par, r):
                    if r == 0:
                        wait(pe, s["a1_hT_hi"], m + 1)
                        wait(pe, s["a1_hT_lo"], m + 1)
                    if isinstance(m, int) and m == 0 and r % 2 == 0:
                        pe.wait_ge(s["a1_w_lo"], r // 2 + 1)
                    wait(pe, s["proj_act"], R * m + r - 1)
                    wait(pe, s["proj_dve"], R * m + r - 1)
                    x = [(hT_hi[par][:, kk, :], hT_lo[par][:, kk, :]) for kk in range(DC)]
                    for a in range(2):
                        col = (2 * r + a) * P
                        w = [(w_hi[:, kk * QKV + col:kk * QKV + col + P], w_lo[:, kk * QKV + col:kk * QKV + col + P])
                             for kk in range(DC)]
                        ins = split_matmul(nc, ps_p[r % 2][:, a, :], w, x)
                    ins.then_inc(s["proj_done"], 1)

                def body(m, par):
                    prev = qkv[1 - par]
                    for u in range(4):
                        k = slot_index(m, u)
                        if on(k, UNITS):
                            if isinstance(m, int) and m == 1 and u == 0:
                                pe.wait_ge(s["mask_ready"], 1)
                                pe.wait_ge(s["a1_w_lo"], 8)
                            if u == 0:
                                wait(pe, s["proj_act"], R * (m - 1) + 8)
                                wait(pe, s["proj_dve"], R * (m - 1) + 8)
                            wait(pe, s["a1_shift"], 2 * k)
                            nc.tensor.matmul(ps_s[:, :], ident_bf[:, :], mask[:, :], start=True, stop=False,
                                             skip_group_check=True)
                            for g in range(UG):
                                cc, ab, pp = g // 4, g // 2 % 2, g % 2
                                q, kx = (prev[0:64, x, UG * u + g, :, :].rearrange("p i t -> p (i t)") for x in (0, 1))
                                ins = nc.tensor.matmul(ps_s[64 * ab:64 * ab + 64, (2 * cc + pp) * 64:(2 * cc + pp + 1) * 64],
                                                       q, kx, start=False, stop=g >= UG - 4, skip_group_check=True)
                            ins.then_inc(s["a1_scores"], 1)
                        if on(m, M):
                            project(m, par, 3 * u)
                        if u % 2 and on(gate_index(m, u - 1), TILES):
                            wait(pe, s["g_hT"], gate_index(m, u - 1) + 1)
                            for kk in range(DC):
                                ins = nc.tensor.matmul(ps_y[:, DIM:DIM + EXPERTS], g_rowsT[:, kk * P:(kk + 1) * P],
                                                       S["wg"][:, kk * EXPERTS:(kk + 1) * EXPERTS],
                                                       start=kk == 0, stop=kk == DC - 1)
                            ins.then_inc(s["g_logit"], 1)
                        if u % 2 and on(tile_index(m, u), TILES):
                            j = tile_index(m, u)
                            wait(pe, s["oT_hi_ready"], 2 * j + 2)
                            wait(pe, s["oT_lo_ready"], 2 * j + 2)
                            wait(pe, s["a1_res"], j)
                            split_matmul(nc, ps_y[:, 0:DIM],
                                         [(oT_hi[:, n, :], oT_lo[:, n, :]) for n in range(OC)],
                                         [(wp_hi[:, n * DIM:(n + 1) * DIM], wp_lo[:, n * DIM:(n + 1) * DIM])
                                          for n in range(OC)]).then_inc(s["a1_out"], 1)
                        if on(k - 1, UNITS):
                            wait(pe, s["a1_normed"], k)
                            wait(pe, s["a1_pT"], k - 1)
                            for cc in range(4):
                                ins = nc.tensor.transpose(ps_t[:, cc * P:(cc + 1) * P], normed[:, cc * P:(cc + 1) * P],
                                                          ident[:, :])
                            ins.then_inc(s["a1_pT_done"], 1)
                        if on(m, M):
                            project(m, par, 3 * u + 1)
                        if on(k - 1, UNITS):
                            wait(pe, s["a1_pT"], k)
                            wait(pe, s["vdiag_act"], k)
                            wait(pe, s["vdiag_dve"], k)
                            wait(pe, s["oT_lo_ready"], k - 1)
                            for ca in range(8):
                                ins = nc.tensor.matmul(ps_o[:, ca * 64:(ca + 1) * 64], vdiag[:, ca, :],
                                                       probsT[:, (ca // 2) * P + (ca % 2) * 64:
                                                              (ca // 2) * P + (ca % 2) * 64 + 64],
                                                       start=True, stop=True)
                            ins.then_inc(s["a1_pv"], 1)
                        if on(k, UNITS):
                            wait(pe, s["vdiag_act"], k)
                            if u == 0:
                                wait(pe, s["proj_act"], R * m)
                                wait(pe, s["proj_dve"], R * m)
                            wait_apart(pe, s["vdiag_dve"], k)
                            for ca in range(8):
                                g = UG * u + 2 * ca
                                ins = nc.tensor.transpose(ps_v[:, ca * 64:(ca + 1) * 64],
                                                          prev[0:64, 2, g:g + 2, :, :].rearrange("p g i t -> p (g i t)"),
                                                          ident[0:64, 0:64])
                            ins.then_inc(s["a1_vT_done"], 1)
                        if on(m, M):
                            project(m, par, 3 * u + 2)
                        if u == 1 and on(m + 1, M):
                            transposes(m + 1)
                        if u % 2 == 0 and on(gate_index(m, u), TILES):
                            wait(pe, s["g_rows"], gate_index(m, u) + 1)
                            for kk in range(DC):
                                ins = nc.tensor.transpose(ps_y[:, DIM + kk * P:DIM + (kk + 1) * P],
                                                          g_rows[:, kk * P:(kk + 1) * P], ident[:, :])
                            ins.then_inc(s["g_trans"], 1)

                transposes(0)
                sequence(pe, body)


def experts(nc, A, S, out):
    h, ident, ident_bf = S["h"], S["ident"], S["ident_bf"]
    bn, mv, rstd, neg_half = S["bn"], S["mv"], S["rstd"], S["neg_half"]
    N = TILES
    E = EXPERTS
    SLOT_TILES = 2 * TOKENS // P + E
    FC = FF // P
    WCOLS = DC * 2 * FF
    RING = 4
    BY_POOL, BY_DVE, BY_POOL_LATE = range(0, E - 3), range(E - 3, E - 1), range(E - 1, E)

    h_rows = S["h_rows"]
    PAIR_ROWS = 1 + 2 * TOKENS
    y_rows = nc.dram_tensor("y_rows", (PAIR_ROWS + SLOT_TILES * P, DIM), F32, kind="Internal").ap()
    bias_rows = nc.dram_tensor("bias_rows", (3, E * 2 * FF), BF16, kind="Internal").ap()

    with ExitStack() as c:
        def sb(name, shape, dt=F32, cc=c):
            return S["sb"](name, shape, dt, cc)

        w_hi, w_lo = sb("we_hi", [P, E, WCOLS], BF16), sb("we_lo", [P, E, WCOLS], BF16)
        wo_hi, wo_lo = sb("wo2_hi", [P, FC * DIM], BF16), sb("wo2_lo", [P, FC * DIM], BF16)
        bias3 = sb("bias3", [3, E * 2 * FF], BF16)
        ones3 = sb("ones3", [3, P], BF16)
        bo = sb("bo", [P, DIM])
        share = [sb(f"share{n}", [P, N]) for n in range(2)]
        owner = sb("owner", [P, SLOT_TILES], mybir.dt.int32)
        source = sb("source", [P, SLOT_TILES], U32)
        dest = sb("dest", [P, SLOT_TILES], U32)
        s_gate = {n: S["sem"](n) for n in (
            "e_consts", "e_w_in0", "e_w_in1", "e_w_hi", "e_w_lo", "e_small", "e_bias_dma", "g_exp", "g_chain", "g_pool", "g_count", "g_lo", "g_lo1", "g_hi", "g_hi_high",
            "g_hi_rest", "e_wo_hi", "g_inv")}

        with ExitStack() as cg:
            def gb(name, shape, dt=F32):
                return S["sb"](name, shape, dt, cg)

            stage = gb("stage_we", [P, RING, WCOLS])
            wo_f = gb("wo_f", [P, FC * DIM])
            b1r = gb("b1r", [P, 64])
            b1p = gb("b1p", [P, 3, 64], BF16)
            lower = gb("lower", [P, P], BF16)
            ones = gb("ones", [P, P], BF16)
            count = S["count"]
            row = S["row"]
            rank = S["rank"]
            tnum = S["tnum"]
            b1f, lower_f = S["b1f"], S["lower_f"]
            big = {n: gb("g_" + n, [P, N, E]) for n in
                   ("p", "d", "pm", "oh0", "oh1", "cum_a", "cum_b", "cnt", "pos", "sel")}
            assigned = gb("assigned", [P, N, E], BF16)
            col = {n: gb("gc_" + n, [P, N]) for n in ("mx", "se", "cm", "v0", "v1", "slotf0", "slotf1", "hi0", "hi1",
                                                 "lo0", "lo1")}
            exp8 = {n: gb("ge_" + n, [P, E]) for n in ("t", "end_a", "end_b", "off")}
            belongs = gb("belongs", [P, SLOT_TILES, E])
            ownf = gb("ownf", [P, SLOT_TILES])
            spare = gb("spare", [P, SLOT_TILES])
            lo1 = [gb(f"lo1{n}", [P, N, P], BF16) for n in range(2)]
            hi1 = [gb(f"hi1{n}", [P, N, 2 * SLOT_TILES], BF16) for n in range(2)]
            ps_pre = S["ps"]("ps_gpre", [P, N * E], F32, cg)
            ps_cnt = S["ps"]("ps_gcnt", [P, N * E], F32, cg)
            ps_inv = S["ps"]("ps_ginv", [P, 2 * SLOT_TILES], F32, cg)
            s = s_gate
            with nc.Block() as block:

                @block.sync
                def _(sp):
                    for e in range(E):
                        if e >= RING:
                            sp.wait_ge(s["e_w_lo"], e - RING + 1)
                        if e >= 2:
                            sp.wait_ge(s[f"e_w_in{e % 2}"], 16 * (e // 2))
                        sp.dma_start(stage[:, e % RING, :], A["we"][:, e, :]).then_inc(s[f"e_w_in{e % 2}"], 16)
                    sp.wait_ge(s["e_small"], 5)
                    sp.dma_start(bias_rows.rearrange("n (p f) -> p n f", p=P), b1p[:, :, :]
                                 ).then_inc(s["e_bias_dma"], 16)
                    sp.wait_ge(s["e_bias_dma"], 16)
                    sp.dma_start(bias3[:, :], bias_rows).then_inc(s["e_bias_dma"], 16)
                    sp.wait_ge(s["e_bias_dma"], 32)

                @block.scalar
                def _(act):
                    act.dma_start(wo_f[:, :], A["wo2"]).then_inc(s["e_consts"], 16)
                    act.dma_start(bo[:, :], A["bo"]).then_inc(s["e_consts"], 16)

                    def high(e):
                        act.wait_ge(s[f"e_w_in{e % 2}"], 16 * (e // 2 + 1))
                        nc.scalar.copy(w_hi[:, e, :], stage[:, e % RING, :]).then_inc(s["e_w_hi"], 1)

                    act.wait_ge(s["g_chain"], 2)
                    nc.scalar.activation(big["p"][:, :, :], big["d"][:, :, :], ACT.Exp).then_inc(s["g_exp"], 1)
                    high(0)
                    act.wait_ge(s["e_consts"], 32)
                    nc.scalar.copy(lower[:, :], lower_f[:, :])
                    nc.scalar.copy(wo_hi[:, :], wo_f[:, :]).then_inc(s["e_wo_hi"], 1)
                    for e in range(1, E):
                        high(e)
                    K = SLOT_TILES
                    for ch in range(2):
                        act.wait_ge(s["g_hi"], ch + 1)
                        act.wait_ge(s["g_hi_high"], ch + 1)
                        nc.scalar.activation(hi1[ch][:, :, K:2 * K], hi1[ch][:, :, K:2 * K], ACT.Copy,
                                             scale=row[:, 0:1]).then_inc(s["g_hi_rest"], 1)

                @block.gpsimd
                def _(pool):
                    nc.gpsimd.memset(ones[:, :], 1.0)
                    nc.gpsimd.memset(ones3[:, :], 1.0).then_inc(s["g_pool"], 1)
                    def low(e):
                        pool.wait_ge(s["e_w_hi"], e + 1)
                        nc.gpsimd.tensor_tensor(w_lo[:, e, :], stage[:, e % RING, :], w_hi[:, e, :],
                                                ALU.subtract).then_inc(s["e_w_lo"], 1)

                    for e in BY_POOL:
                        low(e)
                    K = SLOT_TILES
                    for ch in range(2):
                        pool.wait_ge(s["g_hi"], ch + 1)
                        nc.gpsimd.tensor_tensor(hi1[ch][:, :, 0:K], hi1[ch][:, :, K:2 * K],
                                                tnum[:, ch, :].unsqueeze(2).to_broadcast([P, N, K]),
                                                ALU.mult).then_inc(s["g_hi_high"], 1)
                    for e in BY_POOL_LATE:
                        low(e)
                    pool.wait_ge(s["e_wo_hi"], 1)
                    nc.gpsimd.tensor_tensor(wo_lo[:, :], wo_f[:, :], wo_hi[:, :], ALU.subtract)

                @block.tensor
                def _(pe):

                    pe.wait_ge(s["g_pool"], 1)
                    pe.wait_ge(s["e_wo_hi"], 1)
                    pe.wait_ge(s["g_count"], 1)
                    a = assigned[:, :, :].rearrange("p t e -> p (t e)")
                    nc.tensor.matmul(ps_pre[:, :], lower[:, :], a, start=True, stop=True)
                    nc.tensor.matmul(ps_cnt[:, :], ones[:, :], a, start=True, stop=True).then_inc(s["g_count"], 1)
                    for ch in range(2):
                        pe.wait_ge(s["g_lo1"], ch + 1)
                        pe.wait_ge(s["g_hi_rest"], ch + 1)
                        for t in range(N):
                            ins = nc.tensor.matmul(ps_inv[:, :], lo1[ch][:, t, :], hi1[ch][:, t, :],
                                                   start=ch == 0 and t == 0, stop=ch == 1 and t == N - 1)
                        ins.then_inc(s["g_inv"], 1)

                @block.vector
                def _(dve):
                    chain = [0]

                    def link(ins):
                        chain[0] += 1
                        ins.then_inc(s["g_chain"], 1)
                        dve.wait_ge(s["g_chain"], chain[0])

                    def over_e(x):
                        return x[:, :].unsqueeze(2).to_broadcast([P, N, E])

                    def over_t(x):
                        return x[:, :].unsqueeze(1).to_broadcast([P, N, E])

                    def tt(o, a, b, op):
                        link(nc.vector.tensor_tensor(o, a, b, op))

                    def full(x):
                        return big[x][:, :, :]

                    link(nc.vector.tensor_reduce(col["mx"][:, :], S["logit"][:, :, :], AX.X, ALU.max))
                    tt(full("d"), S["logit"][:, :, :], over_e(col["mx"]), ALU.subtract)
                    dve.wait_ge(s["g_exp"], 1)
                    link(nc.vector.tensor_reduce(col["se"][:, :], full("p"), AX.X, ALU.add))
                    link(nc.vector.reciprocal(col["se"][:, :], col["se"][:, :]))
                    tt(full("p"), full("p"), over_e(col["se"]), ALU.mult)
                    for ch in range(2):
                        pm, oh, v = full("p") if ch == 0 else full("pm"), full(f"oh{ch}"), col[f"v{ch}"]
                        link(nc.vector.tensor_reduce(v[:, :], pm, AX.X, ALU.max))
                        tt(full("sel"), pm, over_e(v), ALU.is_equal)
                        tt(full("sel"), full("sel"), over_t(rank), ALU.mult)
                        link(nc.vector.tensor_reduce(col["cm"][:, :], full("sel"), AX.X, ALU.max))
                        tt(oh, full("sel"), over_e(col["cm"]), ALU.is_equal)
                        if ch == 0:
                            link(nc.vector.scalar_tensor_tensor(full("pm"), oh, -4.0, full("p"), ALU.mult, ALU.add))
                    tt(col["se"][:, :], col["v0"][:, :], col["v1"][:, :], ALU.add)
                    link(nc.vector.tensor_scalar(col["se"][:, :], col["se"][:, :], 1e-9, None, ALU.add))
                    link(nc.vector.reciprocal(col["se"][:, :], col["se"][:, :]))
                    for ch in range(2):
                        tt(share[ch][:, :], col[f"v{ch}"][:, :], col["se"][:, :], ALU.mult)
                    nc.vector.tensor_tensor(assigned[:, :, :], full("oh0"), full("oh1"), ALU.add
                                            ).then_inc(s["g_count"], 1)
                    small = 0
                    for part in range(3):
                        src = b1f if part == 0 else b1r
                        nc.vector.tensor_copy(b1p[:, part, :], src[:, :]).then_inc(s["e_small"], 1)
                        small += 1
                        dve.wait_ge(s["e_small"], small)
                        if part < 2:
                            nc.vector.tensor_tensor(b1r[:, :], src[:, :], b1p[:, part, :],
                                                    ALU.subtract).then_inc(s["e_small"], 1)
                            small += 1
                            dve.wait_ge(s["e_small"], small)
                    dve.wait_ge(s["g_count"], 2)
                    link(nc.vector.tensor_copy(full("cnt").rearrange("p t e -> p (t e)"), ps_cnt[:, :]))
                    a, b = "cnt", "cum_a"
                    step = 1
                    while step < N:
                        nc.vector.tensor_copy(big[b][:, 0:step, :], big[a][:, 0:step, :])
                        tt(big[b][:, step:N, :], big[a][:, step:N, :], big[a][:, 0:N - step, :], ALU.add)
                        a, b = b, "cum_b" if b == "cum_a" else "cum_a"
                        step *= 2
                    total = big[a][:, N - 1, :]
                    t8 = exp8["t"][:, :]
                    link(nc.vector.tensor_scalar(t8, total, 1.0 / P, 63.5 / P, ALU.mult, ALU.add))
                    link(nc.vector.tensor_scalar(t8, t8, ROUND, None, ALU.add))
                    link(nc.vector.tensor_scalar(t8, t8, ROUND, None, ALU.subtract))
                    x, y = "t", "end_a"
                    step = 1
                    while step < E:
                        nc.vector.tensor_copy(exp8[y][:, 0:step], exp8[x][:, 0:step])
                        tt(exp8[y][:, step:E], exp8[x][:, step:E], exp8[x][:, 0:E - step], ALU.add)
                        x, y = y, "end_b" if y == "end_a" else "end_a"
                        step *= 2
                    end = exp8[x]
                    tt(exp8["off"][:, :], end[:, :], t8, ALU.subtract)
                    link(nc.vector.tensor_scalar(exp8["off"][:, :], exp8["off"][:, :], float(P), None, ALU.mult))
                    tt(full("pos"), big[a][:, :, :], full("cnt"), ALU.subtract)
                    tt(full("pos"), full("pos"), over_t(exp8["off"]), ALU.add)
                    tt(full("pos").rearrange("p t e -> p (t e)"), ps_pre[:, :],
                       full("pos").rearrange("p t e -> p (t e)"), ALU.add)
                    tt(belongs[:, :, :], end[:, :].unsqueeze(1).to_broadcast([P, SLOT_TILES, E]),
                       count[:, 0:SLOT_TILES].unsqueeze(2).to_broadcast([P, SLOT_TILES, E]), ALU.is_le)
                    link(nc.vector.tensor_reduce(ownf[:, :], belongs[:, :, :], AX.X, ALU.add))
                    link(nc.vector.tensor_scalar(owner[:, :], ownf[:, :], float(E - 1), None, ALU.min))
                    for ch in range(2):
                        sf, hi, lo = col[f"slotf{ch}"][:, :], col[f"hi{ch}"], col[f"lo{ch}"]
                        tt(full("sel"), full(f"oh{ch}"), full("pos"), ALU.mult)
                        link(nc.vector.tensor_reduce(sf, full("sel"), AX.X, ALU.add))
                        link(nc.vector.tensor_scalar(hi[:, :], sf, 1.0 / P, -63.5 / P, ALU.mult, ALU.add))
                        link(nc.vector.tensor_scalar(hi[:, :], hi[:, :], ROUND, None, ALU.add))
                        link(nc.vector.tensor_scalar(hi[:, :], hi[:, :], ROUND, None, ALU.subtract))
                        nc.vector.scalar_tensor_tensor(lo[:, :], hi[:, :], -float(P), sf, ALU.mult,
                                                       ALU.add).then_inc(s["g_lo"], 1)
                        dve.wait_ge(s["g_lo"], ch + 1)
                    K = SLOT_TILES
                    for ch in range(2):
                        nc.vector.tensor_tensor(hi1[ch][:, :, K:2 * K],
                                                count[:, 0:K].unsqueeze(1).to_broadcast([P, N, K]),
                                                col[f"hi{ch}"][:, :].unsqueeze(2).to_broadcast([P, N, K]),
                                                ALU.is_equal).then_inc(s["g_hi"], 1)
                        nc.vector.tensor_tensor(lo1[ch][:, :, :],
                                                count[:, :].unsqueeze(1).to_broadcast([P, N, P]),
                                                col[f"lo{ch}"][:, :].unsqueeze(2).to_broadcast([P, N, P]),
                                                ALU.is_equal).then_inc(s["g_lo1"], 1)
                    for e in BY_DVE:
                        dve.wait_ge(s["e_w_hi"], e + 1)
                        nc.vector.tensor_tensor(w_lo[:, e, :], stage[:, e % RING, :], w_hi[:, e, :], ALU.subtract)
                    link(nc.vector.tensor_scalar(spare[:, :], count[:, 0:K], float(P), row[:, 0:1],
                                                 ALU.mult, ALU.add))
                    link(nc.vector.tensor_scalar(spare[:, :], spare[:, :], float(2 * TOKENS), None, ALU.add))
                    number, empty, high = ownf, belongs[:, :, 0], belongs[:, :, 1]
                    dve.wait_ge(s["g_inv"], 2)
                    link(nc.vector.tensor_scalar(number[:, :], ps_inv[:, 0:K], float(P), None, ALU.mult))
                    tt(number[:, :], ps_inv[:, K:2 * K], number[:, :], ALU.add)
                    nc.vector.tensor_scalar(high, number[:, :], float(TOKENS) + 0.5, -float(TOKENS),
                                            ALU.is_gt, ALU.mult)
                    link(nc.vector.tensor_scalar(empty, number[:, :], 0.5, None, ALU.is_lt))
                    tt(spare[:, :], spare[:, :], empty, ALU.mult)
                    nc.vector.tensor_tensor(dest[:, :], number[:, :], spare[:, :], ALU.add)
                    tt(number[:, :], number[:, :], high, ALU.add)
                    nc.vector.tensor_scalar(source[:, :], number[:, :], 1.0, 0.0, ALU.subtract,
                                            ALU.max).then_inc(s["e_small"], 1)

        slot_tiles(nc, S, c, dict(
            h_rows=h_rows, y_rows=y_rows, w_hi=w_hi, w_lo=w_lo, wo_hi=wo_hi, wo_lo=wo_lo, bias3=bias3, ones3=ones3,
            bo=bo, owner=owner, source=source, dest=dest, tiles=SLOT_TILES, wcols=WCOLS, fc=FC))
        combine(nc, S, c, out, y_rows, share)


def slot_tiles(nc, S, c0, G):
    ident = S["ident"]
    n_tiles, FC = G["tiles"], G["fc"]
    with ExitStack() as c:
        def sb(name, shape, dt=F32):
            return S["sb"](name, shape, dt, c)

        index = [sb(f"index{u}", [P, 1], U32) for u in range(2)]
        y_index = [sb(f"y_index{u}", [P, 1], U32) for u in range(2)]
        x = [sb(f"x_rows{u}", [P, DIM]) for u in range(2)]
        xT_hi, xT_lo = sb("xT_hi", [P, DIM], BF16), sb("xT_lo", [P, DIM], BF16)
        sig = sb("sig", [P, FF])
        g = sb("g", [P, FF])
        gT_hi, gT_lo = sb("gT_hi", [P, FF], BF16), sb("gT_lo", [P, FF], BF16)
        y = [sb(f"y{u}", [P, DIM]) for u in range(2)]
        ps_x = S["ps"]("ps_ex", [P, DIM], F32, c)
        ps_a = S["ps"]("ps_ea", [P, FF], F32, c)
        ps_b = S["ps"]("ps_eb", [P, FF], F32, c)
        ps_g = S["ps"]("ps_eg", [P, FF], F32, c)
        ps_y = S["ps"]("ps_ey", [P, DIM], F32, c)
        s = {n: S["sem"](n) for n in (
            "m_index", "m_y_index", "m_x_in0", "m_x_in1", "m_xT_done", "m_xT_hi", "m_xT_lo", "m_up_b", "m_up", "m_sig", "m_g", "m_gT_done",
            "m_gT_hi", "m_gT_lo", "m_down", "m_y", "m_y_out0", "m_y_out1")}

        with nc.Block() as block:

            @block.gpsimd
            def _(pool):
                def step(i, u, pair):
                    wait(pool, s[f"m_x_in{u}"], 16 * pair)
                    nc.gpsimd.tensor_copy(index[u][:, :], G["source"][:, bass.ds(i, 1)]).then_inc(s["m_index"], 1)
                    wait(pool, s["m_index"], i + 1)
                    wait_apart(pool, s["m_xT_done"], i - 1)
                    nc.gpsimd.indirect_dma_start(x[u][:, :], None, G["h_rows"],
                                                 bass.IndirectOffsetOnAxis(ap=index[u][:, :], axis=0)
                                                 ).then_inc(s[f"m_x_in{u}"], 16)
                    if on(i - 3, n_tiles):
                        scatter(i - 3, 1 - u, pair - 2 + u)

                def scatter(i, u, pair):
                    wait(pool, s[f"m_y_out{u}"], 16 * pair)
                    nc.gpsimd.tensor_copy(y_index[u][:, :], G["dest"][:, bass.ds(i, 1)]).then_inc(s["m_y_index"], 1)
                    wait(pool, s["m_y_index"], i + 1)
                    wait_apart(pool, s["m_y"], i + 1)
                    nc.gpsimd.indirect_dma_start(G["y_rows"], bass.IndirectOffsetOnAxis(ap=y_index[u][:, :], axis=0),
                                                 y[u][:, :], None).then_inc(s[f"m_y_out{u}"], 16)

                in_pairs(pool, step, n_tiles, 6)
                for i in range(n_tiles - 3, n_tiles):
                    scatter(i, i % 2, i // 2)
                for u in range(2):
                    pool.wait_ge(s[f"m_y_out{u}"], 16 * (n_tiles // 2))

            @block.scalar
            def _(act):
                def high(i):
                    wait(act, s["m_xT_done"], i + 1)
                    wait(act, s["m_up"], i)
                    nc.scalar.copy(xT_hi[:, :], ps_x[:, :]).then_inc(s["m_xT_hi"], 1)

                def step(i, u, pair):
                    wait(act, s["m_up_b"], i + 1)
                    wait(act, s["m_g"], i)
                    nc.scalar.activation(sig[:, :], ps_b[:, :], ACT.Sigmoid).then_inc(s["m_sig"], 1)
                    if on(i + 1, n_tiles):
                        high(i + 1)
                    wait(act, s["m_gT_done"], i + 1)
                    wait(act, s["m_down"], i)
                    nc.scalar.copy(gT_hi[:, :], ps_g[:, :]).then_inc(s["m_gT_hi"], 1)

                high(0)
                in_pairs(act, step, n_tiles)

            @block.vector
            def _(dve):
                def low(i):
                    wait(dve, s["m_xT_hi"], i + 1)
                    nc.vector.tensor_tensor(xT_lo[:, :], ps_x[:, :], xT_hi[:, :],
                                            ALU.subtract).then_inc(s["m_xT_lo"], 1)

                def finish(i, u, pair):
                    wait(dve, s["m_down"], i + 1)
                    wait(dve, s[f"m_y_out{u}"], 16 * pair)
                    nc.vector.tensor_tensor(y[u][:, :], ps_y[:, :], G["bo"][:, :], ALU.add).then_inc(s["m_y"], 1)

                def step(i, u, pair):
                    wait(dve, s["m_sig"], i + 1)
                    wait(dve, s["m_up"], i + 1)
                    wait(dve, s["m_gT_done"], i)
                    nc.vector.tensor_tensor(g[:, :], ps_a[:, :], sig[:, :], ALU.mult).then_inc(s["m_g"], 1)
                    if on(i + 1, n_tiles):
                        low(i + 1)
                    if on(i - 1, n_tiles):
                        finish(i - 1, 1 - u, pair - 1 if u == 0 else pair)
                    wait(dve, s["m_gT_hi"], i + 1)
                    nc.vector.tensor_tensor(gT_lo[:, :], ps_g[:, :], gT_hi[:, :],
                                            ALU.subtract).then_inc(s["m_gT_lo"], 1)

                low(0)
                in_pairs(dve, step, n_tiles)
                finish(n_tiles - 1, 1, n_tiles // 2 - 1)

            @block.tensor
            def _(pe):
                def transposes(i, u, pair):
                    wait(pe, s[f"m_x_in{u}"], 16 * (pair + 1))
                    wait(pe, s["m_xT_lo"], i)
                    for k in range(DC):
                        ins = nc.tensor.transpose(ps_x[:, k * P:(k + 1) * P], x[u][:, k * P:(k + 1) * P], ident[:, :])
                    ins.then_inc(s["m_xT_done"], 1)

                def down(i):
                    wait(pe, s["m_gT_hi"], i + 1)
                    wait(pe, s["m_gT_lo"], i + 1)
                    wait(pe, s["m_y"], i)
                    split_matmul(nc, ps_y[:, :],
                                 [(gT_hi[:, k * P:(k + 1) * P], gT_lo[:, k * P:(k + 1) * P]) for k in range(FC)],
                                 [(G["wo_hi"][:, k * DIM:(k + 1) * DIM], G["wo_lo"][:, k * DIM:(k + 1) * DIM])
                                  for k in range(FC)]).then_inc(s["m_down"], 1)

                def step(i, u, pair):
                    e = pe.value_load(G["owner"][0:1, bass.ds(i, 1)], min_val=0, max_val=EXPERTS - 1)
                    wait(pe, s["m_xT_hi"], i + 1)
                    wait(pe, s["m_xT_lo"], i + 1)
                    wait(pe, s["m_g"], i)
                    xx = [(xT_hi[:, k * P:(k + 1) * P], xT_lo[:, k * P:(k + 1) * P]) for k in range(DC)]
                    for half, dst in ((1, ps_b), (0, ps_a)):
                        ww = []
                        for k in range(DC):
                            off = k * 2 * FF + half * FF
                            ww.append(tuple(w[:, bass.ds(e, 1), off:off + FF].rearrange("p a n -> p (a n)")
                                            for w in (G["w_hi"], G["w_lo"])))
                        split_matmul(nc, dst[:, :], xx, ww, last=False)
                        ins = nc.tensor.matmul(dst[:, :], G["ones3"][:, :],
                                               G["bias3"][:, bass.ds(e * (2 * FF) + half * FF, FF)],
                                               start=False, stop=True)
                        ins.then_inc(s["m_up_b" if half else "m_up"], 1)
                    if on(i + 1, n_tiles):
                        transposes(i + 1, 1 - u, pair if u == 0 else pair + 1)
                    if on(i - 1, n_tiles):
                        down(i - 1)
                    wait(pe, s["m_g"], i + 1)
                    wait(pe, s["m_gT_lo"], i)
                    for k in range(FC):
                        ins = nc.tensor.transpose(ps_g[:, k * P:(k + 1) * P], g[:, k * P:(k + 1) * P], ident[:, :])
                    ins.then_inc(s["m_gT_done"], 1)

                transposes(0, 0, 0)
                in_pairs(pe, step, n_tiles)
                down(n_tiles - 1)


def combine(nc, S, c0, out, y_rows, share):
    h = S["h"]
    N = TILES // 2
    with ExitStack() as c:
        def sb(name, shape, dt=F32):
            return S["sb"](name, shape, dt, c)

        y = [sb(f"cy{place}", [P, 2, 2, DIM]) for place in range(4)]
        mixed = [sb(f"mixed{u}", [P, 2, DIM]) for u in range(2)]
        final = [sb(f"final{u}", [P, 2, DIM]) for u in range(2)]
        stats = sb("cstats", [P, 2, 6])
        mv = [sb(f"cmv{u}", [P, 2, 2]) for u in range(2)]
        rstd = [sb(f"crstd{u}", [P, 2]) for u in range(2)]
        neg_half = sb("cneg_half", [P, 2])
        s = {n: S["sem"](n) for n in (
            "c_y_in0", "c_y_in1", "c_y_in2", "c_y_in3", "c_mixed", "c_var", "c_rstd", "c_final", "c_out0", "c_out1")}
        rows = y_rows[1:1 + 2 * TOKENS, :].rearrange("(ch n t p) d -> p n t ch d", ch=2, t=2, p=P)
        out_rows = out.rearrange("(n t p) d -> p n t d", t=2, p=P)

        def in_fours(eng, step):
            for n in range(8):
                step(n, n % 4, n // 4)
            with eng.Fori(2, N // 4 - 1) as four:
                for place in range(4):
                    step(4 * four + place, place, four)
            for n in range(N - 4, N):
                step(n, n % 4, n // 4)

        with nc.Block() as block:

            @block.scalar
            def _(act):
                def step(n, place, four):
                    wait(act, s["c_mixed"], 2 * n - 6)
                    for t in range(2):
                        act.dma_start(y[place][:, t, :, :], rows[:, bass.ds(n, 1), t, :, :].rearrange(
                            "p a ch d -> p (a ch) d")).then_inc(s[f"c_y_in{place}"], 16)

                in_fours(act, step)

            @block.gpsimd
            def _(pool):
                nc.gpsimd.memset(neg_half[:, :], -0.5)

                def step(n, u, pair):
                    wait(pool, s["c_var"], 2 * n + 2)
                    wait_apart(pool, s["c_final"], n - 1)
                    nc.gpsimd.tensor_scalar(rstd[u][:, :], mv[u][:, :, 1], EPS, None,
                                            ALU.add).then_inc(s["c_rstd"], 1)
                    wait(pool, s["c_rstd"], 2 * n + 1)
                    nc.gpsimd.tensor_tensor(rstd[u][:, :], rstd[u][:, :], neg_half[:, :],
                                            ALU.pow).then_inc(s["c_rstd"], 1)

                in_pairs(pool, step, N)

            @block.vector
            def _(dve):
                def step(n, place, four):
                    u = place % 2
                    wait(dve, s[f"c_y_in{place}"], 32 * (four + 1))
                    for t in range(2):
                        ins = nc.vector.scalar_tensor_tensor(
                            mixed[u][:, t, :], y[place][:, t, 0, :], share[0][:, bass.ds(2 * n + t, 1)],
                            h[:, 2 * n + t, :], ALU.mult, ALU.add)
                    ins.then_inc(s["c_mixed"], 1)
                    wait(dve, s["c_mixed"], 2 * n + 1)
                    for t in range(2):
                        ins = nc.vector.scalar_tensor_tensor(
                            mixed[u][:, t, :], y[place][:, t, 1, :], share[1][:, bass.ds(2 * n + t, 1)],
                            mixed[u][:, t, :], ALU.mult, ALU.add)
                    ins.then_inc(s["c_mixed"], 1)
                    if on(n - 1, N):
                        finish(n - 1, 1 - u, 2 * four + (place + 1) // 2 - 1)
                    wait_apart(dve, s["c_mixed"], 2 * n + 2)
                    for t in range(2):
                        ins = nc.vector.bn_stats(stats[:, t, :], mixed[u][:, t, :])
                    ins.then_inc(s["c_var"], 1)
                    wait_apart(dve, s["c_var"], 2 * n + 1)
                    for t in range(2):
                        ins = nc.vector.bn_aggr(mv[u][:, t, :], stats[:, t, :])
                    ins.then_inc(s["c_var"], 1)

                def finish(n, u, pair):
                    wait(dve, s["c_rstd"], 2 * n + 2)
                    wait(dve, s[f"c_out{u}"], 16 * pair)
                    for t in range(2):
                        ins = nc.vector.tensor_scalar(final[u][:, t, :], mixed[u][:, t, :], mv[u][:, t, 0:1],
                                                      rstd[u][:, t:t + 1], ALU.subtract, ALU.mult)
                    ins.then_inc(s["c_final"], 1)

                in_fours(dve, step)
                finish(N - 1, 1, N // 2 - 1)

            @block.sync
            def _(sp):
                def step(n, u, pair):
                    wait(sp, s["c_final"], n + 1)
                    sp.dma_start(out_rows[:, bass.ds(n, 1), :, :].rearrange("p a t d -> p (a t) d"),
                                 final[u][:, :, :]).then_inc(s[f"c_out{u}"], 16)

                in_pairs(sp, step, N)
                for u in range(2):
                    sp.wait_ge(s[f"c_out{u}"], 16 * (N // 2))


def _rows(w, chunks):
    n = w.shape[1]
    return np.ascontiguousarray(w.reshape(chunks, P, n).transpose(1, 0, 2).reshape(P, chunks * n))


def _tables():
    grid = np.stack(np.meshgrid(np.arange(8), np.arange(8), indexing="ij"))
    q = DIM // 4
    factor = np.float32(10000.0) ** (np.arange(q, dtype=np.float32) / np.float32(q))
    a = grid[0].reshape(-1).astype(np.float32)[:, None] / factor
    b = grid[1].reshape(-1).astype(np.float32)[:, None] / factor
    pos = np.concatenate([np.sin(a), np.cos(a), np.sin(b), np.cos(b)], -1).astype(np.float32)
    inv = np.float32(1000.0) ** (np.float32(-2.0) * np.arange(DK0 // 2, dtype=np.float32) / np.float32(DK0))
    ang = (np.arange(TOK, dtype=np.float32)[:, None] * inv[None]).astype(np.float32)
    cos, sin = np.cos(ang), np.sin(ang)
    rc = np.repeat(cos, 2, axis=1)
    rs = np.stack([-sin, sin], -1).reshape(TOK, DK0)
    causal = np.where(np.tril(np.ones((TOK, TOK), bool)), 0.0, MASKED).astype(np.float32)
    order = np.array([(tk * HEADS1 + hd) for hd in range(HEADS1) for tk in range(4)])
    causal1 = causal[np.ix_(order, order)]
    return {
        "ident": np.eye(P, dtype=np.float32),
        "pos": np.tile(pos, (2, 1)),
        "rope_c": np.tile(rc, (2, 2 * HEADS0)).astype(np.float32),
        "rope_s": np.tile(rs, (2, 2 * HEADS0)).astype(np.float32),
        "lower": np.triu(np.ones((P, P)), 1).astype(np.float32),
        "count": np.tile(np.arange(P, dtype=np.float32)[None], (P, 1)),
        "row": np.arange(1, P + 1, dtype=np.float32)[:, None],
        "rank": np.tile(EXPERTS - np.arange(EXPERTS, dtype=np.float32)[None], (P, 1)),
        "tnum": np.tile(np.arange(2 * TILES, dtype=np.float32)[None], (P, 1)),
        "mask0": np.tile(causal, (2, 4)),
        "mask1": np.tile(causal1, (2, 8)),
    }


def _layout(i):
    x = i["x"].reshape(IMAGES, 3, 8, 16, 8, 16).transpose(0, 2, 4, 3, 5, 1).reshape(TOKENS, PATCH)
    a = {
        "patches": np.ascontiguousarray(
            x.reshape(TILES, P, PC, P).transpose(3, 0, 2, 1).reshape(P, TILES, PC * P)),
        "wp": _rows(i["L0_tok_Wp"].T, PC),
        "tok_b": np.tile(i["L0_tok_b"][None], (P, 1)),
        "wqkv": _rows(np.concatenate([i["L0_attn_wq"].T, i["L0_attn_wk"].T,
                                      i["L0_attn_wv"].T.reshape(DIM, 2, 4, 2, DK0)
                                      .transpose(0, 3, 2, 1, 4).reshape(DIM, DIM)], 1), DC),
        "wo": _rows(i["L0_attn_wo"].T, DC),
        "w1": _rows(i["L0_ffn_w1"].T, DC),
        "b1": np.ascontiguousarray(i["L0_ffn_b1"].reshape(HC, P).T),
        "w2": _rows(i["L0_ffn_w2"].T, HC),
        "wqkv1": _rows(np.concatenate([i["L1_attn_" + n].transpose(1, 0, 2).reshape(DIM, HEADS1 * DK1)
                                       for n in ("Wq", "Wk", "Wv")], 1), DC),
        "wp1": _rows(i["L1_attn_proj_w"].T, HEADS1 * DK1 // P),
        "bp": np.tile(i["L1_attn_proj_b"][None], (P, 1)),
        "we": np.ascontiguousarray(i["L1_ffn_W1"].transpose(0, 2, 1).reshape(EXPERTS, DC, P, 2 * FF)
                                   .transpose(2, 0, 1, 3).reshape(P, EXPERTS, DC * 2 * FF)),
        "be": np.ascontiguousarray(i["L1_ffn_b1"].reshape(P, EXPERTS * 2 * FF // P)),
        "wg": _rows(i["L1_ffn_Wg"].T, DC),
        "wo2": _rows(i["L1_ffn_Wo"].T, FF // P),
        "bo": np.tile(i["L1_ffn_bo"][None], (P, 1)),
        "b2": np.tile(i["L0_ffn_b2"][None], (P, 1)),
    }
    t = _tables()
    a.update(t)
    return a


def kernel(**inputs):
    import concourse.bacc as bacc
    from concourse.bass_utils import run_bass_kernel_spmd

    nc = bacc.Bacc("TRN2", target_bir_lowering=False, num_devices=1)
    arrays = _layout({k: np.asarray(v) for k, v in inputs.items()})
    aps = {n: nc.dram_tensor(n + "_in", a.shape, mybir.dt.from_np(a.dtype), kind="ExternalInput").ap()
           for n, a in arrays.items()}
    out = nc.dram_tensor("tower_out", (TOKENS, DIM), F32, kind="ExternalOutput").ap()
    build(nc, aps, out)
    r = run_bass_kernel_spmd(nc, [{n + "_in": a for n, a in arrays.items()}], core_ids=[0])
    return r.results[0]["tower_out"].reshape(IMAGES, TOK, DIM)
```
